# Optimizing a Trainium2 kernel written in Bass

```python
import numpy as np
import jax
import jax.numpy as jnp

def _softmax(x, axis=-1):
    return jax.nn.softmax(x, axis=axis)

def _gelu(x):
    return jax.nn.gelu(x, approximate=True)

def _silu(x):
    return jax.nn.silu(x)

def _sigmoid(x):
    return jax.nn.sigmoid(x)

def _layernorm(x, axis=-1, eps=1e-05):
    m = jnp.mean(x, axis=axis, keepdims=True)
    v = jnp.var(x, axis=axis, keepdims=True)
    return (x - m) / jnp.sqrt(v + eps)

def _scatter_add(tgt, idx, src, axis=0):
    return tgt.at[idx].add(src)

def _segment_sum(src, seg, n):
    return jax.ops.segment_sum(src, seg, n)
kernel_name = 'mk_adaln_attn_ffn_d1_seqx_r4_9bdb05'

def setup_inputs(seed: int=0):
    np.random.seed(seed)
    _w = jnp.asarray

    def _rec_inputs():
        import jax
        import jax.numpy as jnp
        _rk = jax.random.key(seed)
        x = -1.394e-06 + 0.9999 * jax.random.normal(jax.random.fold_in(_rk, 1), (4, 512, 512), jnp.float32)
        _lenS = 512 - jax.random.randint(jax.random.fold_in(_rk, 7), (4,), 0, max(1, 512 // 4) + 1, jnp.int32)
        _lenS2 = 512 - jax.random.randint(jax.random.fold_in(_rk, 8), (4,), 0, max(1, 512 // 4) + 1, jnp.int32)
        cond_2048 = -0.00499425 + 1.0058 * jax.random.normal(jax.random.fold_in(_rk, 11), (4, 512), jnp.float32)
        return (x, cond_2048)
    x, cond_2048 = _rec_inputs()

    def _L0_cond_setup():
        import jax, jax.numpy as jnp
        import numpy as np
        B, T, D = (16, 128, 512)
        key = jax.random.key(seed)
        k0, k1, k2, k3 = jax.random.split(key, 4)
        scale = 1.0 / np.sqrt(D)
        return {'initial_state': jax.random.normal(k0, (B, D), jnp.float32), 'inputs': jax.random.normal(k1, (B, T, D), jnp.float32), 'W_ih': jax.random.normal(k2, (D, 3 * D), jnp.float32) * scale, 'W_hh': jax.random.normal(k3, (D, 3 * D), jnp.float32) * scale, 'b_ih': jnp.zeros((3 * D,), jnp.float32), 'b_hh': jnp.zeros((3 * D,), jnp.float32)}
    _L0_cond_all = _L0_cond_setup()
    _L0_cond_in = {k: v for k, v in _L0_cond_all.items() if k in ('W_ih', 'W_hh', 'b_ih', 'b_hh')}
    del _L0_cond_all

    def _L0_attn_setup():
        import math
        import jax, jax.numpy as jnp
        import numpy as np
        B, S, E, H = (1, 512, 512, 16)
        QL, KL = (384, 128)
        DN, DR, DV = (128, 64, 128)
        DQ = DN + DR
        ROPE_BASE = 10000.0
        EPS = 1e-06

        def _rope_cache(seq_len):
            inv_freq = 1.0 / ROPE_BASE ** (np.arange(0, DR, 2, dtype=np.float32) / DR)
            t = np.arange(seq_len, dtype=np.float32)
            freqs = np.outer(t, inv_freq)
            emb = np.concatenate([freqs, freqs], axis=-1)
            return (jnp.asarray(np.cos(emb)), jnp.asarray(np.sin(emb)))

        def _rmsnorm(x, w):
            return x * jax.lax.rsqrt(jnp.mean(x * x, axis=-1, keepdims=True) + EPS) * w

        def _apply_rope(x, cos, sin):
            b, s, h, d = x.shape
            xr = x.reshape(b, s, h, d // 2, 2)
            x = jnp.concatenate([xr[..., 0], xr[..., 1]], axis=-1)
            rot = jnp.concatenate([-x[..., d // 2:], x[..., :d // 2]], axis=-1)
            return x * cos[None, :, None, :] + rot * sin[None, :, None, :]
        key = jax.random.key(seed)
        ks = jax.random.split(key, 8)
        w = lambda k, shape, fan_in: jax.random.normal(k, shape, jnp.float32) / math.sqrt(fan_in)
        return {'x': jax.random.normal(ks[0], (B, S, E), jnp.float32), 'w_q_a': w(ks[1], (E, QL), E), 'q_a_ln': jnp.ones((QL,), jnp.float32), 'w_q_b': w(ks[2], (QL, H * DQ), QL), 'w_kv_a': w(ks[3], (E, KL + DR), E), 'kv_a_ln': jnp.ones((KL,), jnp.float32), 'w_kv_b': w(ks[4], (KL, H * (DN + DV)), KL), 'w_out': w(ks[5], (H * DV, E), H * DV)}
    _L0_attn_all = _L0_attn_setup()
    _L0_attn_in = {k: v for k, v in _L0_attn_all.items() if k in ('w_q_a', 'q_a_ln', 'w_q_b', 'w_kv_a', 'kv_a_ln', 'w_kv_b', 'w_out')}
    del _L0_attn_all

    def _L0_cond2_setup():
        import jax, jax.numpy as jnp
        import numpy as np
        NUM_BLOCKS = 8
        NUM_LAYERS = 4
        EPS = 1e-06
        key = jax.random.key(seed)
        ks = jax.random.split(key, 6)
        B, S, H = (4, 1024, 512)
        inputs = jax.random.normal(ks[0], (B, S, H), dtype=jnp.float32)
        query_vectors = jax.random.normal(ks[1], (NUM_LAYERS, H), dtype=jnp.float32) * 0.01
        lim = float(np.sqrt(6.0 / (H + H)))
        Wk = jax.random.uniform(ks[2], (H, H), minval=-lim, maxval=lim, dtype=jnp.float32)
        Wo = jax.random.uniform(ks[3], (H, H), minval=-lim, maxval=lim, dtype=jnp.float32)
        rms_weight = jnp.ones((H,), dtype=jnp.float32)
        ln_gamma = jnp.ones((H,), dtype=jnp.float32)
        ln_beta = jnp.zeros((H,), dtype=jnp.float32)
        return {'inputs': inputs, 'layer_idx': 1, 'rms_weight': rms_weight, 'query_vectors': query_vectors, 'Wk': Wk, 'Wo': Wo, 'ln_gamma': ln_gamma, 'ln_beta': ln_beta}
    _L0_cond2_all = _L0_cond2_setup()
    _L0_cond2_in = {k: v for k, v in _L0_cond2_all.items() if k in ('rms_weight', 'Wk', 'Wo', 'ln_gamma', 'ln_beta')}
    del _L0_cond2_all

    def _L0_ffn_setup():
        import jax, jax.numpy as jnp
        import numpy as np
        D_MODEL = 512
        D_EXPERT = 2048
        EPS = 1e-08

        def ternary_quant(w):
            scale = jnp.mean(jnp.abs(w)) + EPS
            q = jnp.clip(jnp.round(w / scale), -1.0, 1.0) * scale
            return w + jax.lax.stop_gradient(q - w)
        key = jax.random.key(seed)
        k_x, k_up, k_gate, k_down = jax.random.split(key, 4)
        std_in = 1.0 / np.sqrt(D_MODEL)
        std_exp = 1.0 / np.sqrt(D_EXPERT)
        return {'x': jax.random.normal(k_x, (4, 512, D_MODEL), dtype=jnp.float32), 'W_up': jax.random.normal(k_up, (D_EXPERT, D_MODEL), dtype=jnp.float32) * std_in, 'W_gate': jax.random.normal(k_gate, (D_EXPERT, D_MODEL), dtype=jnp.float32) * std_in, 'W_down': jax.random.normal(k_down, (D_MODEL, D_EXPERT), dtype=jnp.float32) * std_exp}
    _L0_ffn_all = _L0_ffn_setup()
    _L0_ffn_in = {k: v for k, v in _L0_ffn_all.items() if k in ('W_up', 'W_gate', 'W_down')}
    del _L0_ffn_all
    return {'x': x, 'cond_2048': cond_2048, 'L0_cond_W_ih': _L0_cond_in['W_ih'], 'L0_cond_W_hh': _L0_cond_in['W_hh'], 'L0_cond_b_ih': _L0_cond_in['b_ih'], 'L0_cond_b_hh': _L0_cond_in['b_hh'], 'L0_attn_w_q_a': _L0_attn_in['w_q_a'], 'L0_attn_q_a_ln': _L0_attn_in['q_a_ln'], 'L0_attn_w_q_b': _L0_attn_in['w_q_b'], 'L0_attn_w_kv_a': _L0_attn_in['w_kv_a'], 'L0_attn_kv_a_ln': _L0_attn_in['kv_a_ln'], 'L0_attn_w_kv_b': _L0_attn_in['w_kv_b'], 'L0_attn_w_out': _L0_attn_in['w_out'], 'L0_cond2_rms_weight': _L0_cond2_in['rms_weight'], 'L0_cond2_Wk': _L0_cond2_in['Wk'], 'L0_cond2_Wo': _L0_cond2_in['Wo'], 'L0_cond2_ln_gamma': _L0_cond2_in['ln_gamma'], 'L0_cond2_ln_beta': _L0_cond2_in['ln_beta'], 'L0_ffn_W_up': _L0_ffn_in['W_up'], 'L0_ffn_W_gate': _L0_ffn_in['W_gate'], 'L0_ffn_W_down': _L0_ffn_in['W_down']}

def reference(x, cond_2048, L0_cond_W_ih, L0_cond_W_hh, L0_cond_b_ih, L0_cond_b_hh, L0_attn_w_q_a, L0_attn_q_a_ln, L0_attn_w_q_b, L0_attn_w_kv_a, L0_attn_kv_a_ln, L0_attn_w_kv_b, L0_attn_w_out, L0_cond2_rms_weight, L0_cond2_Wk, L0_cond2_Wo, L0_cond2_ln_gamma, L0_cond2_ln_beta, L0_ffn_W_up, L0_ffn_W_gate, L0_ffn_W_down):
    import jax
    import jax.numpy as jnp

    def _L0_cond_ref(initial_state, inputs, W_ih, W_hh, b_ih, b_hh):
        import jax, jax.numpy as jnp
        import numpy as np
        B, T, D = (16, 128, 512)
        "ScanOverTime(GRU cell): sequential per-timestep module call with\n            dict-state passing; merge_dict_trees stacks the per-step\n            'state_predicted' tensors along axis=1 -> [B, T, D]."

        def cell(h, x):
            gi = x @ W_ih + b_ih
            gh = h @ W_hh + b_hh
            i_r, i_z, i_n = jnp.split(gi, 3, axis=-1)
            h_r, h_z, h_n = jnp.split(gh, 3, axis=-1)
            r = jax.nn.sigmoid(i_r + h_r)
            z = jax.nn.sigmoid(i_z + h_z)
            n = jnp.tanh(i_n + r * h_n)
            h_new = (1.0 - z) * n + z * h
            return (h_new, h_new)
        xs = jnp.swapaxes(inputs, 0, 1)
        _, hs = jax.lax.scan(cell, initial_state, xs)
        return jnp.swapaxes(hs, 0, 1)

    def _L0_attn_ref(x, w_q_a, q_a_ln, w_q_b, w_kv_a, kv_a_ln, w_kv_b, w_out):
        import math
        import jax, jax.numpy as jnp
        import numpy as np
        B, S, E, H = (1, 512, 512, 16)
        QL, KL = (384, 128)
        DN, DR, DV = (128, 64, 128)
        DQ = DN + DR
        ROPE_BASE = 10000.0
        EPS = 1e-06

        def _rope_cache(seq_len):
            inv_freq = 1.0 / ROPE_BASE ** (np.arange(0, DR, 2, dtype=np.float32) / DR)
            t = np.arange(seq_len, dtype=np.float32)
            freqs = np.outer(t, inv_freq)
            emb = np.concatenate([freqs, freqs], axis=-1)
            return (jnp.asarray(np.cos(emb)), jnp.asarray(np.sin(emb)))

        def _rmsnorm(x, w):
            return x * jax.lax.rsqrt(jnp.mean(x * x, axis=-1, keepdims=True) + EPS) * w

        def _apply_rope(x, cos, sin):
            b, s, h, d = x.shape
            xr = x.reshape(b, s, h, d // 2, 2)
            x = jnp.concatenate([xr[..., 0], xr[..., 1]], axis=-1)
            rot = jnp.concatenate([-x[..., d // 2:], x[..., :d // 2]], axis=-1)
            return x * cos[None, :, None, :] + rot * sin[None, :, None, :]
        b, s, _ = x.shape
        q = (_rmsnorm(x @ w_q_a, q_a_ln) @ w_q_b).reshape(b, s, H, DQ)
        q_nope, q_pe = (q[..., :DN], q[..., DN:])
        ckv = x @ w_kv_a
        c_kv, k_pe = (ckv[..., :KL], ckv[..., KL:])
        kv = (_rmsnorm(c_kv, kv_a_ln) @ w_kv_b).reshape(b, s, H, DN + DV)
        k_nope, v = (kv[..., :DN], kv[..., DN:])
        cos, sin = _rope_cache(s)
        q_pe = _apply_rope(q_pe, cos, sin)
        k_pe = _apply_rope(k_pe.reshape(b, s, 1, DR), cos, sin)
        qf = jnp.concatenate([q_nope, q_pe], axis=-1)
        kf = jnp.concatenate([k_nope, jnp.broadcast_to(k_pe, (b, s, H, DR))], axis=-1)
        scale = 1.0 / math.sqrt(DQ)
        scores = jnp.einsum('bqhd,bkhd->bhqk', qf, kf) * scale
        mask = jnp.tril(jnp.ones((s, s), dtype=bool))
        scores = jnp.where(mask[None, None], scores, jnp.finfo(scores.dtype).min)
        p = jax.nn.softmax(scores, axis=-1)
        o = jnp.einsum('bhqk,bkhd->bqhd', p, v).reshape(b, s, H * DV)
        return o @ w_out

    def _L0_cond2_ref(inputs, layer_idx, rms_weight, query_vectors, Wk, Wo, ln_gamma, ln_beta):
        import jax, jax.numpy as jnp
        import numpy as np
        NUM_BLOCKS = 8
        NUM_LAYERS = 4
        EPS = 1e-06
        B, S, H = inputs.shape
        block_size = max(1, S // NUM_BLOCKS)
        n_blocks = S // block_size
        block_repr = inputs.reshape(B, n_blocks, block_size, H).sum(axis=2)
        keys = jnp.einsum('bnh,kh->bnk', block_repr, Wk)
        rms = jnp.sqrt(jnp.mean(keys * keys, axis=-1, keepdims=True) + EPS)
        keys = keys / rms * rms_weight
        q = query_vectors[layer_idx]
        scores = jnp.einsum('bnh,h->bn', keys, q)
        attn = jax.nn.softmax(scores, axis=-1)
        attended = jnp.einsum('bn,bnh->bh', attn, block_repr)
        attended = jnp.broadcast_to(attended[:, None, :], (B, S, H))
        proj = jnp.einsum('bsh,kh->bsk', attended, Wo)
        x = inputs + proj
        mu = jnp.mean(x, axis=-1, keepdims=True)
        var = jnp.mean((x - mu) ** 2, axis=-1, keepdims=True)
        out = (x - mu) / jnp.sqrt(var + EPS) * ln_gamma + ln_beta
        return out

    def _L0_ffn_ref(x, W_up, W_gate, W_down):
        import jax, jax.numpy as jnp
        import numpy as np
        D_MODEL = 512
        D_EXPERT = 2048
        EPS = 1e-08

        def ternary_quant(w):
            scale = jnp.mean(jnp.abs(w)) + EPS
            q = jnp.clip(jnp.round(w / scale), -1.0, 1.0) * scale
            return w + jax.lax.stop_gradient(q - w)
        wu = ternary_quant(W_up)
        wg = ternary_quant(W_gate)
        wd = ternary_quant(W_down)
        up = jnp.einsum('bsd,ed->bse', x, wu)
        gate = jnp.einsum('bsd,ed->bse', x, wg)
        hidden = jax.nn.silu(up) * gate
        return jnp.einsum('bse,de->bsd', hidden, wd)
    x = x + _L0_attn_ref(_L0_cond_ref(cond_2048, x, L0_cond_W_ih, L0_cond_W_hh, L0_cond_b_ih, L0_cond_b_hh), L0_attn_w_q_a, L0_attn_q_a_ln, L0_attn_w_q_b, L0_attn_w_kv_a, L0_attn_kv_a_ln, L0_attn_w_kv_b, L0_attn_w_out)
    x = x + _L0_ffn_ref(_L0_cond2_ref(x, 1, L0_cond2_rms_weight, cond_2048, L0_cond2_Wk, L0_cond2_Wo, L0_cond2_ln_gamma, L0_cond2_ln_beta), L0_ffn_W_up, L0_ffn_W_gate, L0_ffn_W_down)
    return x

_drawn_inputs = setup_inputs


def setup_inputs(seed=0):
    import zlib

    import numpy as np

    out = dict(_drawn_inputs(seed))
    spreads = {'L0_cond_b_ih': (0.0, 0.1),
     'L0_cond_b_hh': (0.0, 0.1),
     'L0_attn_q_a_ln': (1.0, 0.2),
     'L0_attn_kv_a_ln': (1.0, 0.2),
     'L0_cond2_rms_weight': (1.0, 0.2),
     'L0_cond2_ln_gamma': (1.0, 0.2),
     'L0_cond2_ln_beta': (0.0, 0.36)}
    factors = {}
    for name, (base, spread) in spreads.items():
        noise = np.random.default_rng([zlib.crc32(name.encode()), seed]).standard_normal(out[name].shape)
        drawn = base * np.exp(spread * noise) if base else spread * noise
        out[name] = jnp.asarray(drawn.astype(out[name].dtype))
    for name, factor in factors.items():
        out[name] = (out[name] * factor).astype(out[name].dtype)
    return out
```

```python
from contextlib import ExitStack

import concourse.bass as bass
import numpy as np
from concourse import mybir

F32 = mybir.dt.float32
F32R = mybir.dt.float32r
BF16 = mybir.dt.bfloat16
ACT = mybir.ActivationFunctionType
ALU = mybir.AluOpType
AX_X = mybir.AxisListType.X

P = 128
B, T, D = 4, 512, 512
C = D // P
G3 = 3
NH = 16
QL, KL = 384, 128
DN, DR, DV = 128, 64, 128
QC = QL // P
NT = T // P
F = 2048
FT = F // P
CH = 16
U = 8
NBLK, BLK = 8, T // 8
QSCALE = float(1.0 / np.sqrt(DN + DR))
RMS_EPS = 1e-6
TERN_EPS = 1e-8
KEY0 = [0, 128, 384, 768]
PT0 = [0, 512, 896, 1152]


def build(nc, a):
    x_t, x_rows = a["x_t"], a["x_rows"]
    gi_scratch = nc.dram_tensor("gi_scratch", [B, T, NT * G3 * P], F32, kind="Internal").ap()
    wqk_scratch = nc.dram_tensor("wqk_scratch", [NH, P, QC * P], F32, kind="Internal").ap()

    with ExitStack() as ctx:
        def sem(name):
            return ctx.enter_context(nc.semaphore(name))

        def sb(stack, name, shape, dt=F32):
            return stack.enter_context(nc.sbuf_tensor(name, shape, dt))

        bank = [ctx.enter_context(nc.psum_tensor(f"bank{i}", [P, 512], F32)) for i in range(8)]

        ident = sb(ctx, "ident", [P, P])
        ones = sb(ctx, "ones", [P, P])
        minus_half = sb(ctx, "minus_half", [P, 1])
        hist = sb(ctx, "hist", [P, B, C, T])
        x1 = hist

        with ExitStack() as st:
            w_ih = sb(st, "w_ih", [P, C, 1536])
            gbias = sb(st, "gbias", [P, 1536])
            gbias2 = sb(st, "gbias2", [P, 1536])
            xt_in = sb(st, "xt_in", [P, 2, C, P])
            gi_out = sb(st, "gi_out", [P, 2, 1536])
            ld_const = sem("ld_const")
            ld_wih = sem("ld_wih")
            ld_bias = sem("ld_bias")
            ld_x = [sem("ld_xt0"), sem("ld_xt1")]
            bias_ready = sem("bias_ready")
            gi_mm = sem("gi_mm")
            gi_added = sem("gi_added")
            gi_stored = [sem("gi_stored0"), sem("gi_stored1")]
            NROW = B * NT
            with nc.Block() as block:
                @block.sync
                def _(sp):
                    sp.dma_start(ident[:], a["ident"]).then_inc(ld_const, 16)
                    sp.dma_start(w_ih[:], a["w_ih"]).then_inc(ld_wih, 16)
                    sp.dma_start(gbias[:], a["b_ih"].to_broadcast([P, 1536])).then_inc(ld_bias, 16)
                    sp.dma_start(gbias2[:], a["b_hh"].to_broadcast([P, 1536])).then_inc(ld_bias, 16)
                    for u in range(2):
                        sp.dma_start(xt_in[:, u], x_t[u]).then_inc(ld_x[u], 16)
                    with sp.Fori(0, NROW // 2 - 1) as i:
                        for u in range(2):
                            sp.wait_ge(gi_mm, i * 2 + u + 1)
                            sp.dma_start(xt_in[:, u], x_t[i * 2 + u + 2]).then_inc(ld_x[u], 16)

                @block.gpsimd
                def _(pool):
                    pool.memset(ones[:], 1.0)
                    pool.memset(minus_half[:], -0.5)

                @block.tensor
                def _(pe):
                    pe.wait_ge(ld_wih, 16)
                    with pe.Fori(0, NROW // 2) as i:
                        for u in range(2):
                            pe.wait_ge(ld_x[u], i * 16 + 16)
                            if u == 0:
                                pe.wait_ge(bias_ready, i * 2 + 1)
                            else:
                                pe.wait_ge(bias_ready, i * 2 + 2)
                            for c in range(C):
                                for n in range(3):
                                    mm = pe.matmul(bank[3 * u + n][:], xt_in[:, u, c], w_ih[:, c, n * 512:n * 512 + 512],
                                                   start=(c == 0), stop=(c == C - 1))
                            mm.then_inc(gi_mm, 1)

                @block.vector
                def _(dve):
                    dve.wait_ge(ld_bias, 32)
                    gb = gbias[:].rearrange("p (j g n) -> p j g n", j=4, g=3)
                    gb2 = gbias2[:].rearrange("p (j g n) -> p j g n", j=4, g=3)
                    dve.tensor_tensor(gb[:, :, 0], gb[:, :, 0], gb2[:, :, 0], ALU.add).then_inc(bias_ready, 1)
                    dve.tensor_tensor(gb[:, :, 1], gb[:, :, 1], gb2[:, :, 1], ALU.add).then_inc(bias_ready, 1)
                    dve.wait_ge(bias_ready, 2)
                    with dve.Fori(0, NROW // 2) as i:
                        for u in range(2):
                            dve.wait_ge(gi_mm, i * 2 + u + 1)
                            dve.wait_ge(gi_stored[u], i * 16 + 16)
                            for n in range(3):
                                add = dve.tensor_tensor(gi_out[:, u, n * 512:n * 512 + 512], bank[3 * u + n][:],
                                                        gbias[:, n * 512:n * 512 + 512], ALU.add)
                            add.then_inc(bias_ready, 1)

                @block.scalar
                def _(act):
                    gi_rows = gi_scratch.rearrange("b (q p) n -> (b q) p n", p=P)
                    act.dma_start(gi_out[:, 0, 0:1], a["zero_col"]).then_inc(gi_stored[0], 16)
                    act.dma_start(gi_out[:, 1, 0:1], a["zero_col"]).then_inc(gi_stored[1], 16)
                    with act.Fori(0, NROW // 2) as i:
                        for u in range(2):
                            act.wait_ge(bias_ready, i * 2 + u + 3)
                            act.dma_start(gi_rows[i * 2 + u], gi_out[:, u]).then_inc(gi_stored[u], 16)
                    for u in range(2):
                        act.wait_ge(gi_stored[u], 16 * (NROW // 2 + 1))

        att_weights = ExitStack()
        wvo = sb(att_weights, "wvo", [P, NH, D])
        with ExitStack() as st:
            fold_in = sb(st, "fold_in", [P, 2, QL + KL + DV + D])
            wqk_out = sb(st, "wqk_out", [P, 2, QC * P])
            ld_fold = [sem("ld_fold0"), sem("ld_fold1")]
            qk_mm = sem("qk_mm")
            vo_mm = sem("vo_mm")
            qk_out = sem("qk_out")
            vo_out = sem("vo_out")
            qk_stored = [sem("qk_stored0"), sem("qk_stored1")]
            with nc.Block() as block:
                @block.sync
                def _(sp):
                    for u in range(2):
                        sp.dma_start(fold_in[:, u], a["fold"][u]).then_inc(ld_fold[u], 16)
                    with sp.Fori(0, NH // 2 - 1) as i:
                        for u in range(2):
                            sp.wait_ge(vo_mm, i * 2 + u + 1)
                            sp.dma_start(fold_in[:, u], a["fold"][i * 2 + u + 2]).then_inc(ld_fold[u], 16)

                @block.tensor
                def _(pe):
                    with pe.Fori(0, NH // 2) as i:
                        for u in range(2):
                            pe.wait_ge(ld_fold[u], i * 16 + 16)
                            pe.wait_ge(qk_out, i * 2 + u + 1)
                            pe.wait_ge(vo_out, i * 2 + u + 1)
                            for m in range(QC):
                                mm = pe.matmul(bank[u][:, m * P:m * P + P], fold_in[:, u, m * P:m * P + P],
                                               fold_in[:, u, QL:QL + KL], start=True, stop=True)
                            mm.then_inc(qk_mm, 1)
                            pe.matmul(bank[2 + u][:], fold_in[:, u, QL + KL:QL + KL + DV],
                                      fold_in[:, u, QL + KL + DV:], start=True, stop=True).then_inc(vo_mm, 1)

                @block.scalar
                def _(act):
                    act.dma_start(wqk_out[:, 0, 0:1], a["zero_col"]).then_inc(qk_stored[0], 16)
                    act.dma_start(wqk_out[:, 1, 0:1], a["zero_col"]).then_inc(qk_stored[1], 16)
                    act.wait_ge(qk_stored[0], 16)
                    act.wait_ge(qk_stored[1], 16)
                    act.activation(wqk_out[:, 0, 1:2], ones[:, 0:1], ACT.Copy).then_inc(qk_out, 1)
                    act.activation(wqk_out[:, 1, 1:2], ones[:, 0:1], ACT.Copy).then_inc(qk_out, 1)
                    act.wait_ge(qk_out, 2)
                    with act.Fori(0, NH // 2) as i:
                        for u in range(2):
                            act.wait_ge(qk_mm, i * 2 + u + 1)
                            act.wait_ge(qk_stored[u], i * 16 + 16)
                            act.activation(wqk_out[:, u], bank[u][:, 0:QL], ACT.Copy).then_inc(qk_out, 1)
                            act.wait_ge(qk_out, i * 2 + u + 3)
                            act.dma_start(wqk_scratch[i * 2 + u], wqk_out[:, u]).then_inc(qk_stored[u], 16)
                    for u in range(2):
                        act.wait_ge(qk_stored[u], 16 * (NH // 2 + 1))

                @block.vector
                def _(dve):
                    dve.memset(wvo[:, 0, 0:1], 0.0).then_inc(vo_out, 2)
                    dve.wait_ge(vo_out, 2)
                    with dve.Fori(0, NH // 2) as i:
                        for u in range(2):
                            dve.wait_ge(vo_mm, i * 2 + u + 1)
                            dve.tensor_copy(wvo[:, i * 2 + u], bank[2 + u][:]).then_inc(vo_out, 1)

        with ExitStack() as st:
            w_hh = sb(st, "w_hh", [P, C, 4, G3 * P])
            gates_in = sb(st, "gates_in", [P, 2, CH, G3 * P])
            b_hn = sb(st, "b_hn", [P, P])
            n_gate = sb(st, "n_gate", [P, 2, P])
            h = sb(st, "h", [P, P])
            h_t = sb(st, "h_t", [P, P])
            r = sb(st, "r", [P, P])
            z = sb(st, "z", [P, P])
            n = sb(st, "n", [P, P])
            rh = sb(st, "rh", [P, P])
            n_in = sb(st, "n_in", [P, P])
            zh = sb(st, "zh", [P, P])
            zn = sb(st, "zn", [P, P])
            bank_rn, bank_z = bank[0], bank[1]
            HALVES = (slice(0, P // 2), slice(P // 2, P))
            ld_gru = sem("ld_gru")
            gates_zero = sem("gates_zero")
            ld_gates = sem("ld_gates")
            rn_mm, z_mm = sem("rn_mm"), sem("z_mm")
            r_sig, z_sig = sem("r_sig"), sem("z_sig")
            n_tanh = sem("n_tanh")
            n_staged = sem("n_staged")
            rh_done, nin_done = sem("rh_done"), sem("nin_done")
            zh_done = sem("zh_done")
            zn_done = [sem("zn_done0"), sem("zn_done1")]
            h_done = [sem("h_done0"), sem("h_done1")]
            ht_done = [sem("ht_done0"), sem("ht_done1")]
            hist_done = sem("hist_done")
            NC = T // CH
            with nc.Block() as block:
                @block.sync
                def _(sp):
                    sp.dma_start(w_hh[:], a["w_hh"]).then_inc(ld_gru, 16)
                    sp.dma_start(b_hn[:], a["b_hn"]).then_inc(ld_gru, 16)
                    sp.dma_start(h[:], a["h0"]).then_inc(ld_gru, 16)

                    def load_chunk(k):
                        for j in range(4):
                            sp.dma_start(gates_in[32 * j:32 * j + B, k % 2],
                                         gi_scratch[:, bass.ds(k * CH, CH), j * G3 * P:(j + 1) * G3 * P]
                                         ).then_inc(ld_gates, 16)

                    sp.wait_ge(gates_zero, 1)
                    load_chunk(0)
                    sp.wait_ge(ld_gates, 64)
                    load_chunk(1)
                    with sp.Fori(0, NC - 2) as k:
                        sp.wait_ge(ld_gates, k * 64 + 128)
                        sp.wait_ge(nin_done, k * CH + CH + 1)
                        load_chunk(k + 2)

                @block.gpsimd
                def _(pool):
                    ring = gates_in[:].rearrange("p k t n -> p (k t) n")
                    pool.memset(gates_in[:], 0.0).then_inc(gates_zero, 1)
                    pool.wait_ge(ld_gates, 64)
                    for v in range(2):
                        pool.tensor_copy(n_gate[:, v, :], ring[:, v, 2 * P:]).then_inc(n_staged, 1)
                    with pool.Fori(0, T // 2 - 1) as i:
                        for v in range(2):
                            pool.wait_ge(ld_gates, ((i * 2 + v + 2) // CH) * 64 + 64)
                            pool.wait_ge(nin_done, i * 2 + v + 2)
                            pool.tensor_copy(n_gate[:, v, :], ring[:, (i * 2 + v + 2) % (2 * CH), 2 * P:]
                                             ).then_inc(n_staged, 1)

                @block.tensor
                def _(pe):
                    pe.wait_ge(ld_gru, 48)
                    with pe.Fori(0, NC) as k:
                        with pe.Fori(0, CH // U) as s:
                            pe.wait_ge(ld_gates, k * 64 + 64)
                            for v in range(U):
                                now = k * CH + s * U + v + 1
                                at = s * U + v
                                pe.wait_ge(rh_done, now)
                                pe.matmul(bank_rn[:, 0:P], ident[:], gates_in[:, k % 2, at, 0:P],
                                          start=True, stop=False, skip_group_check=True)
                                pe.matmul(bank_rn[:, P:2 * P], ident[:], b_hn[:], start=False, stop=False,
                                          skip_group_check=True)
                                pe.wait_ge(z_sig, now)
                                pe.matmul(bank_z[:, 0:P], ident[:], gates_in[:, k % 2, at, P:2 * P],
                                          start=True, stop=False, skip_group_check=True)
                                for c in range(C):
                                    if c % 2 == 0:
                                        pe.wait_ge(ht_done[c // 2], now)
                                    for j in range(4):
                                        mm = pe.matmul(bank_rn[32 * j:32 * j + B, 0:2 * P], h_t[:, 32 * c:32 * c + B],
                                                       w_hh[:, c, j, 0:2 * P], start=False, stop=(c == C - 1),
                                                       skip_group_check=True)
                                mm.then_inc(rn_mm, 1)
                                for c in range(C):
                                    for j in range(4):
                                        mm = pe.matmul(bank_z[32 * j:32 * j + B, 0:P], h_t[:, 32 * c:32 * c + B],
                                                       w_hh[:, c, j, 2 * P:], start=False, stop=(c == C - 1),
                                                       skip_group_check=True)
                                mm.then_inc(z_mm, 1)

                @block.scalar
                def _(act):
                    act.wait_ge(ld_gru, 48)
                    act.activation(r[:], b_hn[:], ACT.Sigmoid).then_inc(r_sig, 1)
                    act.activation(z[:], b_hn[:], ACT.Sigmoid).then_inc(z_sig, 1)
                    act.activation(n[:], b_hn[:], ACT.Tanh).then_inc(hist_done, 1)
                    act.wait_ge(r_sig, 1)
                    act.wait_ge(z_sig, 1)
                    act.wait_ge(hist_done, 1)
                    with act.Fori(0, T // U) as i:
                        for v in range(U):
                            t = i * U + v
                            act.wait_ge(rn_mm, t + 1)
                            act.activation(r[:], bank_rn[:, 0:P], ACT.Sigmoid).then_inc(r_sig, 1)
                            act.wait_ge(z_mm, t + 1)
                            act.activation(z[:], bank_z[:, 0:P], ACT.Sigmoid).then_inc(z_sig, 1)
                            act.wait_ge(nin_done, t + 2)
                            act.activation(n[:], n_in[:], ACT.Tanh).then_inc(n_tanh, 1)
                            act.wait_ge(ht_done[1], t + 2)
                            act.activation(hist[:, :, :, t].rearrange("p b c -> p c b"),
                                           h_t[:].rearrange("p (c q) -> p c q", c=C)[:, :, 0:B],
                                           ACT.Copy).then_inc(hist_done, 1)

                @block.vector
                def _(dve):
                    dve.wait_ge(ld_gru, 48)
                    dve.memset(n_in[:], 0.0).then_inc(nin_done, 1)
                    dve.memset(rh[:], 0.0).then_inc(rh_done, 1)
                    for q, half in enumerate(HALVES):
                        dve.transpose(h_t[:, half], h[:, half]).then_inc(ht_done[q], 1)
                    dve.wait_ge(nin_done, 1)
                    dve.wait_ge(rh_done, 1)
                    with dve.Fori(0, T // U) as i:
                        for v in range(U):
                            t = i * U + v
                            dve.wait_ge(r_sig, t + 2)
                            dve.tensor_tensor(rh[:], r[:], bank_rn[:, P:2 * P], ALU.mult).then_inc(rh_done, 1)
                            dve.wait_ge(n_staged, t + 1)
                            dve.wait_ge(rh_done, t + 2)
                            dve.tensor_tensor(n_in[:], rh[:], n_gate[:, v % 2, :], ALU.add).then_inc(nin_done, 1)
                            dve.wait_ge(z_sig, t + 2)
                            dve.tensor_tensor(zh[:], z[:], h[:], ALU.mult).then_inc(zh_done, 1)
                            dve.wait_ge(n_tanh, t + 1)
                            for q, half in enumerate(HALVES):
                                dve.scalar_tensor_tensor(zn[:, half], z[:, half], 1.0, n[:, half], ALU.subtract,
                                                         ALU.mult).then_inc(zn_done[q], 1)
                                if q == 0:
                                    dve.wait_ge(zh_done, t + 1)
                                dve.wait_ge(zn_done[q], t + 1)
                                dve.tensor_tensor(h[:, half], zh[:, half], zn[:, half], ALU.subtract
                                                  ).then_inc(h_done[q], 1)
                                if q == 0:
                                    dve.wait_ge(hist_done, t + 1)
                                dve.wait_ge(h_done[q], t + 1)
                                dve.transpose(h_t[:, half], h[:, half]).then_inc(ht_done[q], 1)

        with ExitStack() as st:
            w_qa = sb(st, "w_qa", [P, C, QL])
            w_kva = sb(st, "w_kva", [P, C, 2 * P])
            rope = sb(st, "rope", [P, T])
            dup = sb(st, "dup", [P, P])
            ident_bf = sb(st, "ident_bf", [P, P], BF16)
            causal = sb(st, "causal", [P, P], BF16)
            ln_q = sb(st, "ln_q", [P, QC])
            ln_kv = sb(st, "ln_kv", [P, 1])
            head_w = sb(st, "head_w", [P, 2 * QL])
            q_raw = sb(st, "q_raw", [P, QC, T])
            q_lat = sb(st, "q_lat", [P, QC, T])
            kv_raw = sb(st, "kv_raw", [P, T])
            kv_t = sb(st, "kv_t", [P, T])
            kv_rows = sb(st, "kv_rows", [P, NT, KL])
            k_rot = sb(st, "k_rot", [P, T])
            sq = sb(st, "sq", [P, QC + 1, T])
            rms = sb(st, "rms", [P, 2, NT])
            rms_diag = sb(st, "rms_diag", [P, 2, T])
            q_t = sb(st, "q_t", [P, T])
            q_rot = sb(st, "q_rot", [P, T])
            prob = sb(st, "prob", [P, 10 * P])
            prob_t = sb(st, "prob_t", [P, 10 * P])
            negmax = sb(st, "negmax", [P, NT])
            psum_row = sb(st, "psum_row", [P, NT])
            pinv = sb(st, "pinv", [P, NT])
            o_t = sb(st, "o_t", [P, NH, T])
            ld_att = sem("ld_att")
            ld_head = sem("ld_head")
            ld_x1 = sem("ld_x1")
            lat_mm = sem("lat_mm")
            raw_done = sem("raw_done")
            rotk = sem("rotk")
            sq_done = sem("sq_done")
            ss_mm = sem("ss_mm")
            diag_done = sem("diag_done")
            spread_mm = sem("spread_mm")
            rms_a = sem("rms_a")
            lnq_scaled = sem("lnq_scaled")
            rms_b = sem("rms_b")
            lat_done = sem("lat_done")
            kdup_mm = sem("kdup_mm")
            krot_done = sem("krot_done")
            kvr_mm = sem("kvr_mm")
            kvr_done = sem("kvr_done")
            proj_mm = sem("proj_mm")
            qt_done = sem("qt_done")
            qrot_done = sem("qrot_done")
            s_mm = sem("s_mm")
            max_done = sem("max_done")
            exp_done = sem("exp_done")
            inv_done = sem("inv_done")
            norm_done = sem("norm_done")
            tr_mm = sem("tr_mm")
            ptA = sem("ptA")
            ptB = sem("ptB")
            pv_mm = sem("pv_mm")
            o_done = sem("o_done")
            y_mm = sem("y_mm")
            y_done = sem("y_done")
            with nc.Block() as block:
                @block.sync
                def _(sp):
                    for dst, src in ((w_qa, "w_qa"), (w_kva, "w_kva"), (rope, "rope"), (dup, "dup"),
                                     (ident_bf, "ident_bf"), (causal, "causal"), (ln_q, "ln_q"), (ln_kv, "ln_kv")):
                        sp.dma_start(dst[:], a[src]).then_inc(ld_att, 16)

                    def load_head(g, head):
                        sp.dma_start(head_w[:, 0:QL], wqk_scratch[head]).then_inc(ld_head, 16)
                        sp.dma_start(head_w[:, QL:], a["w_rope"][head]).then_inc(ld_head, 16)

                    load_head(0, 0)
                    with sp.Fori(0, B) as b:
                        sp.wait_ge(lat_mm, b * 5 + 5)
                        sp.dma_start(x1[:, b], x_rows[b]).then_inc(ld_x1, 16)
                        with sp.Fori(0, NH) as hd:
                            sp.wait_ge(proj_mm, (b * NH + hd) * 2 + 2)
                            load_head(b * NH + hd + 1, (hd + 1) % NH)
                    sp.wait_ge(ld_head, 32 * (B * NH + 1))

                @block.tensor
                def _(pe):
                    def project(g):
                        pe.wait_ge(ld_head, g * 32 + 32)
                        for m in range(QC):
                            mm = pe.matmul(bank[4][:], head_w[:, m * P:m * P + P], q_lat[:, m, :],
                                           start=(m == 0), stop=(m == QC - 1))
                        mm.then_inc(proj_mm, 1)

                    def project_rot(g):
                        for m in range(QC):
                            mm = pe.matmul(bank[5][:], head_w[:, QL + m * P:QL + m * P + P], q_lat[:, m, :],
                                           start=(m == 0), stop=(m == QC - 1))
                        mm.then_inc(proj_mm, 1)

                    def scores(g):
                        pe.wait_ge(qt_done, g + 1)
                        pe.wait_ge(qrot_done, g + 1)
                        for q in range(NT):
                            nk = (q + 1) * P
                            pe.matmul(bank[q][:, 0:nk], q_t[:, q * P:q * P + P], kv_t[:, 0:nk],
                                      start=True, stop=False, skip_group_check=True)
                            pe.matmul(bank[q][:, q * P:nk], ident_bf[:], causal[:], start=False, stop=False,
                                      skip_group_check=True)
                            pe.matmul(bank[q][:, 0:nk], q_rot[:, q * P:q * P + P], k_rot[:, 0:nk],
                                      start=False, stop=True, skip_group_check=True).then_inc(s_mm, 1)

                    def turn(g):
                        for q in range(NT):
                            pe.wait_ge(norm_done, g * NT + q + 1)
                            for k in range(q + 1):
                                tr = pe.transpose(bank[k][:, (q - k) * P:(q - k + 1) * P],
                                                  prob[:, KEY0[q] + k * P:KEY0[q] + k * P + P], ident[:])
                        tr.then_inc(tr_mm, 1)

                    def values(g):
                        for k in range(NT):
                            if k % 2 == 0:
                                pe.wait_ge(ptA, g * 2 + k // 2 + 1)
                            else:
                                pe.wait_ge(ptB, g * 2 + k // 2 + 1)
                            mm = pe.matmul(bank[6][:, k * P:], kv_rows[:, k, :], prob_t[:, PT0[k]:PT0[k] + (NT - k) * P],
                                           start=(k == 0), stop=(k == NT - 1), skip_group_check=True)
                        mm.then_inc(pv_mm, 1)

                    pe.wait_ge(ld_att, 16 * 8)
                    with pe.Fori(0, B) as b:
                        for m in range(QC):
                            for c in range(C):
                                mm = pe.matmul(bank[m][:], w_qa[:, c, m * P:m * P + P], hist[:, b, c, :],
                                               start=(c == 0), stop=(c == C - 1))
                            mm.then_inc(lat_mm, 1)
                        for m in range(2):
                            for c in range(C):
                                mm = pe.matmul(bank[3 + m][:], w_kva[:, c, m * P:m * P + P], hist[:, b, c, :],
                                               start=(c == 0), stop=(c == C - 1))
                            mm.then_inc(lat_mm, 1)
                        pe.wait_ge(sq_done, b * 4 + 4)
                        for i, ms in enumerate((range(QC), range(QC, QC + 1))):
                            for q in range(NT):
                                for m in ms:
                                    mm = pe.matmul(bank[5 + i][:, q:q + 1], sq[:, m, q * P:q * P + P], ones[:, 0:1],
                                                   start=(m == ms[0]), stop=(m == ms[-1]))
                            mm.then_inc(ss_mm, 1)
                        pe.wait_ge(rotk, b + 1)
                        pe.matmul(bank[4][:], dup[:], k_rot[:], start=True, stop=True).then_inc(kdup_mm, 1)
                        for i in range(2):
                            pe.wait_ge(diag_done, b * 2 + i + 1)
                            pe.matmul(bank[6 + i][:], ones[:], rms_diag[:, i, :], start=True, stop=True
                                      ).then_inc(spread_mm, 1)
                        pe.wait_ge(lat_done, b * 4 + 4)
                        for k in range(NT):
                            tr = pe.transpose(bank[3][:, k * P:k * P + P], kv_t[:, k * P:k * P + P], ident[:])
                        tr.then_inc(kvr_mm, 1)
                        pe.wait_ge(krot_done, b + 1)
                        project(b * NH)
                        project_rot(b * NH)
                        with pe.Fori(0, NH - 1) as hd:
                            g = b * NH + hd
                            pe.wait_ge(krot_done, b + 1)
                            pe.wait_ge(kvr_done, b + 1)
                            scores(g)
                            project(g + 1)
                            turn(g)
                            project_rot(g + 1)
                            values(g)
                        g = b * NH + NH - 1
                        scores(g)
                        turn(g)
                        values(g)
                        pe.wait_ge(o_done, b * NH + NH)
                        for q in range(NT):
                            for hd in range(NH):
                                mm = pe.matmul(bank[q][:], o_t[:, hd, q * P:q * P + P], wvo[:, hd, :],
                                               start=(hd == 0), stop=(hd == NH - 1))
                            mm.then_inc(y_mm, 1)
                        pe.wait_ge(y_done, b * NT + NT)

                @block.gpsimd
                def _(pool):
                    with pool.Fori(0, B) as b:
                        pool.wait_ge(rms_a, b * 2 + 2)
                        flat = rms[:].rearrange("p i q -> p (i q)")
                        pool.tensor_tensor(flat, flat, minus_half[:, 0:1].to_broadcast([P, 2 * NT]), ALU.pow
                                           ).then_inc(rms_b, 1)

                @block.scalar
                def _(act):
                    def head(g):
                        for q in range(NT):
                            nk = (q + 1) * P
                            act.wait_ge(max_done, g * NT + q + 1)
                            act.activation(prob[:, KEY0[q]:KEY0[q] + nk], bank[q][:, 0:nk], ACT.Exp,
                                           bias=negmax[:, q:q + 1], scale=1.0,
                                           accum_out=psum_row[:, q:q + 1]).then_inc(exp_done, 1)

                    def copy_q(g):
                        act.wait_ge(proj_mm, g * 2 + 1)
                        act.activation(q_t[:], bank[4][:], ACT.Copy).then_inc(qt_done, 1)

                    def turned(g):
                        act.wait_ge(tr_mm, g + 1)
                        for k in (0, 2):
                            act.activation(prob_t[:, PT0[k]:PT0[k] + (NT - k) * P], bank[k][:, 0:(NT - k) * P],
                                           ACT.Copy).then_inc(ptA, 1)

                    def keep_o(g, hd):
                        act.wait_ge(pv_mm, g + 1)
                        act.activation(o_t[:, hd, :], bank[6][:], ACT.Copy).then_inc(o_done, 1)

                    with act.Fori(0, B) as b:
                        for m in range(QC):
                            act.wait_ge(raw_done, b * 4 + m + 1)
                            act.activation(sq[:, m, :], q_raw[:, m, :], ACT.Square).then_inc(sq_done, 1)
                        act.wait_ge(raw_done, b * 4 + 4)
                        act.activation(sq[:, QC, :], kv_raw[:], ACT.Square).then_inc(sq_done, 1)
                        act.wait_ge(kdup_mm, b + 1)
                        act.activation(k_rot[:], bank[4][:], ACT.Copy).then_inc(krot_done, 1)
                        act.wait_ge(kvr_mm, b + 1)
                        act.activation(kv_rows[:].rearrange("p k n -> p (k n)"), bank[3][:], ACT.Copy
                                       ).then_inc(kvr_done, 1)
                        copy_q(b * NH)
                        with act.Fori(0, NH - 1) as hd:
                            g = b * NH + hd
                            head(g)
                            copy_q(g + 1)
                            turned(g)
                            keep_o(g, hd)
                        g = b * NH + NH - 1
                        head(g)
                        turned(g)
                        keep_o(g, NH - 1)

                @block.vector
                def _(dve):
                    def head(g):
                        def normalise(q):
                            nk = (q + 1) * P
                            dve.wait_ge(exp_done, g * NT + q + 1)
                            dve.reciprocal(pinv[:, q:q + 1], psum_row[:, q:q + 1]).then_inc(inv_done, 1)
                            dve.wait_ge(inv_done, g * NT + q + 1)
                            dve.tensor_scalar(prob[:, KEY0[q]:KEY0[q] + nk], prob[:, KEY0[q]:KEY0[q] + nk],
                                              pinv[:, q:q + 1], None, ALU.mult).then_inc(norm_done, 1)

                        for q in range(NT):
                            nk = (q + 1) * P
                            dve.wait_ge(s_mm, g * NT + q + 1)
                            dve.tensor_reduce(negmax[:, q:q + 1], bank[q][:, 0:nk], AX_X, ALU.max,
                                              negate=True).then_inc(max_done, 1)
                            if q > 0:
                                normalise(q - 1)
                        normalise(NT - 1)

                    def turned(g):
                        dve.wait_ge(tr_mm, g + 1)
                        for k in (1, 3):
                            dve.tensor_copy(prob_t[:, PT0[k]:PT0[k] + (NT - k) * P], bank[k][:, 0:(NT - k) * P]
                                            ).then_inc(ptB, 1)

                    def rotate_q(g):
                        dve.wait_ge(proj_mm, g * 2 + 2)
                        dve.tensor_tensor(q_rot[:], bank[5][:], rope[:], ALU.mult).then_inc(qrot_done, 1)

                    dve.wait_ge(ld_att, 16 * 8)
                    dve.tensor_scalar(ln_q[:], ln_q[:], QSCALE, None, ALU.mult).then_inc(lnq_scaled, 1)
                    dve.wait_ge(lnq_scaled, 1)
                    with dve.Fori(0, B) as b:
                        for m in range(QC):
                            dve.wait_ge(lat_mm, b * 5 + m + 1)
                            dve.tensor_copy(q_raw[:, m, :], bank[m][:]).then_inc(raw_done, 1)
                        dve.wait_ge(lat_mm, b * 5 + 4)
                        dve.tensor_copy(kv_raw[:], bank[3][:]).then_inc(raw_done, 1)
                        dve.wait_ge(lat_mm, b * 5 + 5)
                        dve.tensor_tensor(k_rot[:], bank[4][:], rope[:], ALU.mult).then_inc(rotk, 1)
                        for i, width in enumerate((QL, KL)):
                            dve.wait_ge(ss_mm, b * 2 + i + 1)
                            dve.tensor_scalar(rms[:, i], bank[5 + i][:, 0:NT], 1.0 / width, RMS_EPS, ALU.mult, ALU.add
                                              ).then_inc(rms_a, 1)
                        dve.wait_ge(rms_b, b + 1)
                        for i in range(2):
                            for q in range(NT):
                                diag = dve.tensor_scalar(rms_diag[:, i, q * P:q * P + P], ident[:], rms[:, i, q:q + 1],
                                                         None, ALU.mult)
                            diag.then_inc(diag_done, 1)
                        dve.wait_ge(spread_mm, b * 2 + 2)
                        dve.scalar_tensor_tensor(kv_t[:], kv_raw[:], ln_kv[:, 0:1], bank[7][:], ALU.mult, ALU.mult
                                                 ).then_inc(lat_done, 1)
                        for m in range(QC):
                            dve.scalar_tensor_tensor(q_lat[:, m, :], q_raw[:, m, :], ln_q[:, m:m + 1], bank[6][:],
                                                     ALU.mult, ALU.mult).then_inc(lat_done, 1)
                        rotate_q(b * NH)
                        with dve.Fori(0, NH - 1) as hd:
                            g = b * NH + hd
                            head(g)
                            turned(g)
                            rotate_q(g + 1)
                        head(b * NH + NH - 1)
                        turned(b * NH + NH - 1)
                        dve.wait_ge(ld_x1, b * 16 + 16)
                        for q in range(NT):
                            dve.wait_ge(y_mm, b * NT + q + 1)
                            dve.tensor_tensor(x1[:, b, q, :], bank[q][:], x1[:, b, q, :], ALU.add).then_inc(y_done, 1)

        att_weights.close()

        tern = [sb(ctx, f"tern_{w}", [P, 4 * F], F32R) for w in ("up", "gate", "down")]
        shift = sb(ctx, "shift", [P, B, D])
        w_scale = sb(ctx, "w_scale", [P, 3])
        gamma_t = sb(ctx, "gamma_t", [P, C])
        beta_t = sb(ctx, "beta_t", [P, C])
        NB = B * NBLK
        with ExitStack() as st:
            raw = sb(st, "raw", [P, 4 * F])
            below = sb(st, "below", [P, F], BF16)
            abs_sum = sb(st, "abs_sum", [P, 4])
            mean_abs = sb(st, "mean_abs", [P, 1])
            limits = sb(st, "limits", [P, 6])
            wk_t = sb(st, "wk_t", [P, C, D])
            wo_t = sb(st, "wo_t", [P, C, D])
            block_sel = sb(st, "block_sel", [P, 2])
            batch_mask = sb(st, "batch_mask", [NB, B])
            batch_row = sb(st, "batch_row", [B, B * P])
            key_w = sb(st, "key_w", [NB, D])
            query = sb(st, "query", [NB, D])
            blocks_t = sb(st, "blocks_t", [P, C, NB])
            blocks = sb(st, "blocks", [NB, D])
            keys = sb(st, "keys", [NB, D])
            junk = sb(st, "junk", [NB, D])
            stat = sb(st, "stat", [NB, 8])
            row = sb(st, "row", [1, 3, NB])
            rowb = sb(st, "rowb", [1, 3, B])
            pick = sb(st, "pick", [NB, B])
            mix_t = sb(st, "mix_t", [P, C * B])
            proj = sb(st, "proj", [B, D])
            ld_c2 = sem("ld_c2")
            ld_raw = sem("ld_raw")
            raw_free = sem("raw_free")
            abs_done = sem("abs_done")
            abs_mm = sem("abs_mm")
            tern_step = sem("tern_step")
            pe_step = sem("pe_step")
            dve_step = sem("dve_step")
            act_step = sem("act_step")
            pool_step = sem("pool_step")
            with nc.Block() as block:
                @block.sync
                def _(sp):
                    for dst, src in ((wk_t[:], a["wk_t"]), (wo_t[:], a["wo_t"]), (block_sel[:], a["block_sel"]),
                                     (batch_mask[:], a["batch_mask"]), (batch_row[:], a["batch_row"]),
                                     (key_w[:], a["key_w"].to_broadcast([NB, D])),
                                     (query[:], a["query"].to_broadcast([NB, D])),
                                     (gamma_t[:], a["gamma_t"]), (beta_t[:], a["beta_t"])):
                        sp.dma_start(dst, src).then_inc(ld_c2, 16)
                    for w in range(3):
                        if w > 0:
                            sp.wait_ge(raw_free, w)
                        sp.dma_start(raw[:], a["ffn"][w]).then_inc(ld_raw, 16)

                @block.tensor
                def _(pe):
                    pe.wait_ge(ld_c2, 16 * 9)
                    for b in range(B):
                        for q in range(NT):
                            for c in range(C):
                                at = c * NB + b * NBLK + 2 * q
                                mm = pe.matmul(bank[0][:, at:at + 2], x1[:, b, q, c * P:c * P + P], block_sel[:],
                                               start=True, stop=True)
                    mm.then_inc(pe_step, 1)
                    pe.wait_ge(dve_step, 1)
                    for c in range(C):
                        pe.matmul(bank[1][0:NB, :], blocks_t[:, c, :], wk_t[:, c, :], start=(c == 0), stop=(c == C - 1))
                    for c in range(C):
                        mm = pe.transpose(bank[2][0:NB, c * P:c * P + P], blocks_t[:, c, :], ident[:])
                    mm.then_inc(pe_step, 1)
                    pe.wait_ge(dve_step, 7)
                    pe.transpose(bank[3][0:1, 0:NB], stat[:, 3:4], ident[0:NB, 0:NB]).then_inc(pe_step, 1)
                    pe.wait_ge(dve_step, 12)
                    pe.matmul(bank[4][0:NB, 0:1], row[0:1, 2, :], ones[0:1, 0:1], start=True, stop=True
                              ).then_inc(pe_step, 1)
                    pe.wait_ge(dve_step, 13)
                    for c in range(C):
                        mm = pe.matmul(bank[5][:, c * B:c * B + B], blocks[:, c * P:c * P + P], pick[:],
                                       start=True, stop=True)
                    mm.then_inc(pe_step, 1)
                    pe.wait_ge(dve_step, 14)
                    for c in range(C):
                        mm = pe.matmul(bank[6][0:B, :], mix_t[:, c * B:c * B + B], wo_t[:, c, :],
                                       start=(c == 0), stop=(c == C - 1))
                    mm.then_inc(pe_step, 1)
                    pe.wait_ge(dve_step, 15)
                    for b in range(B):
                        mm = pe.matmul(bank[b][:], batch_row[:, b * P:b * P + P], proj[:], start=True, stop=True)
                    mm.then_inc(pe_step, 1)
                    for w in range(3):
                        pe.wait_ge(abs_done, w + 1)
                        pe.matmul(bank[7][:, w:w + 1], ones[:], mean_abs[:], start=True, stop=True).then_inc(abs_mm, 1)

                @block.gpsimd
                def _(pool):
                    pool.wait_ge(dve_step, 6)
                    pool.tensor_tensor(stat[:, 2:3], stat[:, 2:3], minus_half[0:NB, :], ALU.pow).then_inc(pool_step, 1)

                @block.scalar
                def _(act):
                    act.wait_ge(dve_step, 2)
                    act.activation(junk[:], keys[:], ACT.Square, accum_out=stat[:, 0:1]).then_inc(act_step, 1)
                    act.wait_ge(dve_step, 9)
                    act.activation(row[0:1, 1, :], row[0:1, 0, :], ACT.Exp).then_inc(act_step, 1)

                @block.vector
                def _(dve):
                    steps = [0]

                    def step(ins):
                        steps[0] += 1
                        ins.then_inc(dve_step, 1)
                        dve.wait_ge(dve_step, steps[0])

                    dve.wait_ge(ld_c2, 16 * 9)
                    dve.wait_ge(pe_step, 1)
                    step(dve.tensor_copy(blocks_t[:].rearrange("p c n -> p (c n)"), bank[0][:, 0:C * NB]))
                    dve.wait_ge(pe_step, 2)
                    step(dve.tensor_copy(keys[:], bank[1][0:NB, :]))
                    step(dve.tensor_copy(blocks[:], bank[2][0:NB, :]))
                    step(dve.tensor_tensor(query[:], query[:], key_w[:], ALU.mult))
                    step(dve.scalar_tensor_tensor(query[:], keys[:], 1.0, query[:], ALU.mult, ALU.mult,
                                                  accum_out=stat[:, 1:2]))
                    dve.wait_ge(act_step, 1)
                    step(dve.tensor_scalar(stat[:, 2:3], stat[:, 0:1], 1.0 / D, RMS_EPS, ALU.mult, ALU.add))
                    dve.wait_ge(pool_step, 1)
                    step(dve.tensor_tensor(stat[:, 3:4], stat[:, 1:2], stat[:, 2:3], ALU.mult))
                    dve.wait_ge(pe_step, 3)
                    by_batch = bank[3][0:1, 0:NB].rearrange("o (b n) -> o b n", b=B)
                    out0, out1, out2 = (row[0:1, i, :].rearrange("o (b n) -> o b n", b=B) for i in range(3))
                    step(dve.tensor_reduce(rowb[0:1, 0, :], by_batch, AX_X, ALU.max))
                    step(dve.tensor_tensor(out0, by_batch, rowb[0:1, 0, :].unsqueeze(2).to_broadcast([1, B, NBLK]),
                                           ALU.subtract))
                    dve.wait_ge(act_step, 2)
                    step(dve.tensor_reduce(rowb[0:1, 1, :], out1, AX_X, ALU.add))
                    step(dve.reciprocal(rowb[0:1, 2, :], rowb[0:1, 1, :]))
                    step(dve.tensor_tensor(out2, out1, rowb[0:1, 2, :].unsqueeze(2).to_broadcast([1, B, NBLK]), ALU.mult))
                    dve.wait_ge(pe_step, 4)
                    step(dve.tensor_scalar(pick[:], batch_mask[:], bank[4][0:NB, 0:1], None, ALU.mult))
                    dve.wait_ge(pe_step, 5)
                    step(dve.tensor_copy(mix_t[:], bank[5][:, 0:C * B]))
                    dve.wait_ge(pe_step, 6)
                    step(dve.tensor_copy(proj[:], bank[6][0:B, :]))
                    dve.wait_ge(pe_step, 7)
                    for b in range(B):
                        dve.tensor_copy(shift[:, b, :], bank[b][:])

                    count = [0]

                    def link(ins):
                        count[0] += 1
                        ins.then_inc(tern_step, 1)
                        dve.wait_ge(tern_step, count[0])

                    for w in range(3):
                        dve.wait_ge(ld_raw, 16 * (w + 1))
                        for i in range(4):
                            ins = dve.tensor_reduce(abs_sum[:, i:i + 1], raw[:, i * F:(i + 1) * F], AX_X, ALU.add,
                                                    apply_absolute_value=True)
                        link(ins)
                        dve.tensor_reduce(mean_abs[:], abs_sum[:], AX_X, ALU.add).then_inc(abs_done, 1)
                        dve.wait_ge(abs_mm, w + 1)
                        link(dve.tensor_scalar(w_scale[:, w:w + 1], bank[7][:, w:w + 1], 1.0 / (D * F), TERN_EPS,
                                               ALU.mult, ALU.add))
                        link(dve.tensor_scalar(limits[:, w:w + 1], w_scale[:, w:w + 1], 0.5, None, ALU.mult))
                        link(dve.tensor_scalar(limits[:, 3 + w:4 + w], w_scale[:, w:w + 1], -0.5, None, ALU.mult))
                        for i in range(4):
                            part = slice(i * F, (i + 1) * F)
                            link(dve.tensor_scalar(below[:], raw[:, part], limits[:, 3 + w:4 + w], None, ALU.is_lt))
                            link(dve.scalar_tensor_tensor(tern[w][:, part], raw[:, part], limits[:, w:w + 1], below[:],
                                                          ALU.is_gt, ALU.subtract))
                        dve.memset(mean_abs[:], 0.0).then_inc(raw_free, 1)

        with ExitStack() as st:
            up_w = tern[0][:].rearrange("p (c e) -> p c e", c=C)
            gate_w = tern[1][:].rearrange("p (c e) -> p c e", c=C)
            down_w = tern[2][:].rearrange("p (t d) -> p t d", t=FT)
            xn = sb(st, "xn", [P, NT, D])
            bn = sb(st, "bn", [P, 6])
            bn_pad = sb(st, "bn_pad", [P, 1])
            mv = sb(st, "mv", [P, NT, 2])
            rstd = sb(st, "rstd", [P, NT])
            LN_STEPS = 4 * NT + 1
            xg = sb(st, "xg", [P, 2, T])
            x_hi = sb(st, "x_hi", [P, C, T], F32R)
            x_lo = sb(st, "x_lo", [P, C, T], F32R)
            act_up = sb(st, "act_up", [P, 2, T])
            hid = sb(st, "hid", [P, 2, T])
            h_hi = sb(st, "h_hi", [P, 2, T], F32R)
            h_lo = sb(st, "h_lo", [P, 2, T], F32R)
            y_out = sb(st, "y_out", [P, NT, D])
            ln_step = sem("ln_step")
            rstd_done = sem("rstd_done")
            xn_t = sem("xn_t")
            xg_done = sem("xg_done")
            x_split = sem("x_split")
            up_mm = sem("up_mm")
            down_mm = sem("down_mm")
            silu_done = sem("silu_done")
            hid_done = sem("hid_done")
            hhi_done = sem("hhi_done")
            hlo_done = sem("hlo_done")
            y_scaled = sem("y_scaled")
            y_stored = sem("y_stored")
            out_rows = a["out"].rearrange("b (q p) d -> b p q d", p=P)
            with nc.Block() as block:
                @block.sync
                def _(sp):
                    sp.dma_start(y_out[:, 0, 0:1], a["zero_col"]).then_inc(y_stored, 16)
                    with sp.Fori(0, B) as g:
                        sp.wait_ge(y_scaled, g * NT + NT + 1)
                        sp.dma_start(out_rows[g], y_out[:]).then_inc(y_stored, 16)
                    sp.wait_ge(y_stored, 16 * B + 16)

                @block.tensor
                def _(pe):
                    def expand(g, e):
                        up, gate = bank[4 + 2 * (e % 2)], bank[5 + 2 * (e % 2)]
                        for w, out in ((up_w, up), (gate_w, gate)):
                            for c in range(C):
                                for half, part in enumerate((x_hi, x_lo)):
                                    mm = pe.matmul(out[:], w[:, c, e * P:e * P + P], part[:, c, :],
                                                   start=(c == 0 and half == 0), stop=(c == C - 1 and half == 1))
                        mm.then_inc(up_mm, 1)

                    def contract(g, e):
                        pe.wait_ge(hhi_done, g * FT + e + 1)
                        pe.wait_ge(hlo_done, g * FT + e + 1)
                        for half, part in enumerate((h_hi, h_lo)):
                            for q in range(NT):
                                mm = pe.matmul(bank[q][:], part[:, e % 2, q * P:q * P + P], down_w[:, e, :],
                                               start=(e == 0 and half == 0), stop=(e == FT - 1 and half == 1))
                        mm.then_inc(down_mm, 1)

                    with pe.Fori(0, B) as g:
                        pe.wait_ge(ln_step, g * LN_STEPS + LN_STEPS)
                        pe.wait_ge(hid_done, g * FT + 1)
                        for c in range(C):
                            for q in range(NT):
                                tr = pe.transpose(bank[4 + c][:, q * P:q * P + P], xn[:, q, c * P:c * P + P], ident[:])
                            tr.then_inc(xn_t, 1)
                        pe.wait_ge(x_split, g * 2 * C + 2 * C)
                        for e in range(FT):
                            if e >= 2:
                                pe.wait_ge(hid_done, g * FT + e)
                            expand(g, e)
                            if e == 1:
                                pe.wait_ge(y_scaled, g * NT + 1)
                            if e > 0:
                                contract(g, e - 1)
                        contract(g, FT - 1)

                @block.scalar
                def _(act):
                    with act.Fori(0, B) as g:
                        for c in range(C):
                            act.wait_ge(xn_t, g * C + c + 1)
                            if c >= 2:
                                act.wait_ge(x_split, g * 2 * C + 2 * (c - 1))
                            act.activation(xg[:, c % 2, :], bank[4 + c][:], ACT.Identity, bias=beta_t[:, c:c + 1],
                                           scale=gamma_t[:, c:c + 1]).then_inc(xg_done, 1)
                        for e in range(FT):
                            act.wait_ge(up_mm, g * FT + e + 1)
                            if e >= 2:
                                act.wait_ge(hid_done, g * FT + e)
                            act.activation(act_up[:, e % 2, :], bank[4 + 2 * (e % 2)][:], ACT.Silu,
                                           scale=w_scale[:, 0:1]).then_inc(silu_done, 1)
                            act.wait_ge(hid_done, g * FT + e + 2)
                            if e >= 2:
                                act.wait_ge(down_mm, g * FT + e - 1)
                            act.activation(h_hi[:, e % 2, :], hid[:, e % 2, :], ACT.Copy).then_inc(hhi_done, 1)

                @block.vector
                def _(dve):
                    dve.memset(rstd[:], 0.0).then_inc(hid_done, 1)
                    dve.memset(mv[:], 0.0).then_inc(y_scaled, 1)
                    dve.wait_ge(hid_done, 1)
                    dve.wait_ge(y_scaled, 1)
                    with dve.Fori(0, B) as g:
                        for q in range(NT):
                            def chain(i, ins):
                                ins.then_inc(ln_step, 1)
                                dve.wait_ge(ln_step, g * LN_STEPS + q * 3 + i)
                            chain(1, dve.tensor_tensor(xn[:, q, :], x1[:, g, q, :], shift[:, g, :], ALU.add))
                            chain(2, dve.bn_stats(bn[:], xn[:, q, :]))
                            dve.memset(bn_pad[:], 0.0)
                            chain(3, dve.bn_aggr(mv[:, q, :], bn[:]))
                        dve.tensor_scalar(rstd[:], mv[:, :, 1], RMS_EPS, None, ALU.add).then_inc(ln_step, 1)
                        dve.wait_ge(rstd_done, g + 1)
                        for q in range(NT):
                            dve.tensor_scalar(xn[:, q, :], xn[:, q, :], mv[:, q, 0:1], rstd[:, q:q + 1], ALU.subtract,
                                              ALU.mult).then_inc(ln_step, 1)
                        for c in range(C):
                            dve.wait_ge(xg_done, g * C + c + 1)
                            dve.tensor_copy(x_hi[:, c, :], xg[:, c % 2, :]).then_inc(x_split, 1)
                            dve.wait_ge(x_split, g * 2 * C + 2 * c + 1)
                            dve.tensor_tensor(x_lo[:, c, :], xg[:, c % 2, :], x_hi[:, c, :].bitcast(F32), ALU.subtract
                                              ).then_inc(x_split, 1)
                        for e in range(FT):
                            dve.wait_ge(silu_done, g * FT + e + 1)
                            if e >= 2:
                                dve.wait_ge(hhi_done, g * FT + e - 1)
                            dve.scalar_tensor_tensor(hid[:, e % 2, :], bank[5 + 2 * (e % 2)][:], w_scale[:, 1:2],
                                                     act_up[:, e % 2, :], ALU.mult, ALU.mult).then_inc(hid_done, 1)
                            dve.wait_ge(hhi_done, g * FT + e + 1)
                            dve.tensor_tensor(h_lo[:, e % 2, :], hid[:, e % 2, :], h_hi[:, e % 2, :].bitcast(F32),
                                              ALU.subtract).then_inc(hlo_done, 1)
                        dve.wait_ge(down_mm, g * FT + FT)
                        dve.wait_ge(y_stored, g * 16 + 16)
                        for q in range(NT):
                            dve.scalar_tensor_tensor(y_out[:, q, :], bank[q][:], w_scale[:, 2:3], x1[:, g, q, :],
                                                     ALU.mult, ALU.add).then_inc(y_scaled, 1)

                @block.gpsimd
                def _(pool):
                    with pool.Fori(0, B) as g:
                        pool.wait_ge(ln_step, g * LN_STEPS + 3 * NT + 1)
                        pool.tensor_tensor(rstd[:], rstd[:], minus_half[:, 0:1].to_broadcast([P, NT]), ALU.pow
                                           ).then_inc(rstd_done, 1)


def _tables():
    eye = np.eye(P, dtype=np.float32)
    half = np.arange(P) % DR
    inv_freq = 1.0 / 10000.0 ** (np.arange(0, DR, 2, dtype=np.float32) / DR)
    freqs = np.outer(np.arange(T, dtype=np.float32), inv_freq)
    cos, sin = np.cos(freqs).T, np.sin(freqs).T
    q, k = np.meshgrid(np.arange(P), np.arange(P), indexing="ij")
    return {
        "ident": eye,
        "dup": (half[:, None] == half[None, :]).astype(np.float32),
        "rope": np.concatenate([cos, cos, -sin, sin]).astype(np.float32),
        "causal": np.where(k > q, np.float32(-1e30), np.float32(0)),
        "block_sel": np.kron(np.eye(2), np.ones((BLK, 1))).astype(np.float32),
        "batch_mask": np.kron(np.eye(B), np.ones((NBLK, 1))).astype(np.float32),
        "batch_row": np.kron(np.eye(B), np.ones((1, P))).astype(np.float32),
        "zero_col": np.zeros((P, 1), np.float32),
    }


def kernel(x, cond_2048, L0_cond_W_ih, L0_cond_W_hh, L0_cond_b_ih, L0_cond_b_hh, L0_attn_w_q_a, L0_attn_q_a_ln,
           L0_attn_w_q_b, L0_attn_w_kv_a, L0_attn_kv_a_ln, L0_attn_w_kv_b, L0_attn_w_out, L0_cond2_rms_weight,
           L0_cond2_Wk, L0_cond2_Wo, L0_cond2_ln_gamma, L0_cond2_ln_beta, L0_ffn_W_up, L0_ffn_W_gate, L0_ffn_W_down):
    import ml_dtypes
    from concourse import bacc
    from concourse.bass_utils import run_bass_kernel_spmd

    def np32(v):
        return np.ascontiguousarray(np.asarray(v))

    def tiles(w):
        return w.reshape(-1, P, w.shape[-1]).transpose(1, 0, 2)

    def state_tiles(w):
        return w.reshape(4, C, 32, w.shape[-1]).transpose(0, 2, 1, 3).reshape(P, C, w.shape[-1])

    def gate_cols(w):
        return w.reshape(-1, G3, 4, P).transpose(0, 2, 1, 3).reshape(-1, 4 * G3 * P)

    x, cond = np32(x), np32(cond_2048)
    w_hh, b_hh = np32(L0_cond_W_hh), np32(L0_cond_b_hh)
    t = _tables()
    arrays = dict(t)
    arrays["causal"] = t["causal"].astype(ml_dtypes.bfloat16)
    arrays["ident_bf"] = t["ident"].astype(ml_dtypes.bfloat16)
    arrays["x_t"] = x.reshape(B, NT, P, C, P).transpose(0, 1, 4, 3, 2).reshape(B * NT, P, C, P)
    arrays["x_rows"] = x.reshape(B, NT, P, D).transpose(0, 2, 1, 3)
    arrays["w_ih"] = tiles(gate_cols(np32(L0_cond_W_ih)))
    arrays["b_ih"] = gate_cols(np32(L0_cond_b_ih)[None])
    arrays["b_hh"] = gate_cols(b_hh[None])
    w_rnz = w_hh.reshape(D, G3, 4, P)[:, [0, 2, 1]].transpose(0, 2, 1, 3).reshape(D, -1)
    arrays["w_hh"] = state_tiles(w_rnz).reshape(P, C, 4, G3 * P)
    state = np.zeros((4, 32, P), np.float32)
    state[:, :B] = cond.reshape(B, 4, P).transpose(1, 0, 2)
    arrays["h0"] = state.reshape(P, P)
    bias = np.zeros((4, 32, P), np.float32)
    bias[:, :B] = b_hh[2 * D:].reshape(4, 1, P)
    arrays["b_hn"] = bias.reshape(P, P)
    w_qb = np32(L0_attn_w_q_b).reshape(QL, NH, DN + DR)
    w_kvb = np32(L0_attn_w_kv_b).reshape(KL, NH, DN + DV)
    w_o = np32(L0_attn_w_out).reshape(NH, DV, D)
    arrays["fold"] = np.concatenate([w_qb[:, :, :DN].transpose(1, 2, 0), w_kvb[:, :, :DN].transpose(1, 2, 0),
                                     w_kvb[:, :, DN:].transpose(1, 2, 0), w_o], axis=2)

    def rotary(w):
        return np.concatenate([w[..., 0::2], w[..., 1::2], w[..., 1::2], w[..., 0::2]], axis=-1)

    arrays["w_rope"] = rotary(w_qb[:, :, DN:]).reshape(QC, P, NH, P).transpose(2, 1, 0, 3).reshape(NH, P, QC * P)
    w_kva = np32(L0_attn_w_kv_a)
    arrays["w_qa"] = state_tiles(np32(L0_attn_w_q_a))
    arrays["w_kva"] = state_tiles(np.concatenate([w_kva[:, :KL], rotary(w_kva[:, KL:])], axis=1))
    arrays["ln_q"] = np32(L0_attn_q_a_ln).reshape(QC, P).T
    arrays["ln_kv"] = np32(L0_attn_kv_a_ln).reshape(P, 1)
    arrays["wk_t"] = tiles(np32(L0_cond2_Wk).T)
    arrays["wo_t"] = tiles(np32(L0_cond2_Wo).T)
    arrays["key_w"] = np32(L0_cond2_rms_weight)[None]
    arrays["query"] = cond[1:2]
    arrays["gamma_t"] = np32(L0_cond2_ln_gamma).reshape(C, P).T
    arrays["beta_t"] = np32(L0_cond2_ln_beta).reshape(C, P).T
    arrays["ffn"] = np.stack([tiles(np32(w).T).reshape(P, -1) for w in (L0_ffn_W_up, L0_ffn_W_gate, L0_ffn_W_down)])

    nc = bacc.Bacc("TRN2", target_bir_lowering=False, num_devices=1)
    arrays = {k: np.ascontiguousarray(v) for k, v in arrays.items()}
    aps = {k: nc.dram_tensor(f"in_{k}", v.shape, mybir.dt.from_np(v.dtype), kind="ExternalInput").ap()
           for k, v in arrays.items()}
    aps["out"] = nc.dram_tensor("out_0", [B, T, D], F32, kind="ExternalOutput").ap()
    build(nc, aps)
    result = run_bass_kernel_spmd(nc, [{f"in_{k}": v for k, v in arrays.items()}], core_ids=[0])
    return result.results[0]["out_0"]
```

```python
from contextlib import ExitStack

import concourse.bass as bass
import numpy as np
from concourse import mybir

F32 = mybir.dt.float32
F32R = mybir.dt.float32r
BF16 = mybir.dt.bfloat16
ACT = mybir.ActivationFunctionType
ALU = mybir.AluOpType
AX_X = mybir.AxisListType.X

P = 128
B, T, D = 4, 512, 512
C = D // P
G3 = 3
NH = 16
QL, KL = 384, 128
DN, DR, DV = 128, 64, 128
QC = QL // P
NT = T // P
F = 2048
FT = F // P
CH = 16
U = 8
BODIES = T // U
NG = 3
FIRST = B
GI_BODIES = NG * (B * NT - FIRST)
FOLD_BODIES = NH
TW = 4 * F // (B * NH)
NBLK, BLK = 8, T // 8
QSCALE = float(1.0 / np.sqrt(DN + DR))
RMS_EPS = 1e-6
TERN_EPS = 1e-8
KEY0 = [0, 128, 384, 768]
PT0 = [0, 512, 896, 1152]


def build(nc, a):
    x_t, x_rows = a["x_t"], a["x_rows"]
    gi_scratch = nc.dram_tensor("gi_scratch", [NT, B, P, NG * 512], F32, kind="Internal").ap()
    gi_tiles = gi_scratch.rearrange("q b p n -> (q b) p n")
    wqk_scratch = nc.dram_tensor("wqk_scratch", [NH, P, QC * P], F32, kind="Internal").ap()
    tern_scratch = nc.dram_tensor("tern_scratch", [3, P, 4 * F], F32, kind="Internal").ap()

    with ExitStack() as ctx:
        def sem(name):
            return ctx.enter_context(nc.semaphore(name))

        def sb(stack, name, shape, dt=F32):
            return stack.enter_context(nc.sbuf_tensor(name, shape, dt))

        bank = [ctx.enter_context(nc.psum_tensor(f"bank{i}", [P, 512], F32)) for i in range(8)]

        ident = sb(ctx, "ident", [P, P])
        ones = sb(ctx, "ones", [P, P])
        minus_half = sb(ctx, "minus_half", [P, 1])
        abs_part = sb(ctx, "abs_part", [P, BODIES, 3])
        w_scale = sb(ctx, "w_scale", [P, 3])
        hist = sb(ctx, "hist", [P, B, C, T])
        x1 = hist
        att_weights = ExitStack()
        wvo = sb(att_weights, "wvo", [P, NH, D])

        gru = ExitStack()
        w_ih = sb(gru, "w_ih", [P, C, NG * 512])
        gbias = sb(gru, "gbias", [P, NG * 512])
        w_hh = sb(gru, "w_hh", [P, C, 4, G3 * P])
        with ExitStack() as st:
            gbias2 = sb(st, "gbias2", [P, NG * 512])
            xt_first = sb(st, "xt_first", [P, FIRST, C, P])
            gi_first = sb(st, "gi_first", [P, 2, NG * 512])
            ld_const = sem("ld_const")
            ld_wih = sem("ld_wih")
            ld_bias = sem("ld_bias")
            ld_first = sem("ld_first")
            ld_gru = sem("ld_gru")
            bias_ready = sem("bias_ready")
            first_mm = sem("first_mm")
            first_added = sem("first_added")
            first_stored = [sem("first_stored0"), sem("first_stored1")]
            with nc.Block() as block:
                @block.sync
                def _(sp):
                    for c in range(C):
                        sp.dma_start(w_ih[:, c], a["w_ih"][:, c]).then_inc(ld_wih, 16)
                        if c == 0:
                            sp.dma_start(xt_first[:], x_t[0:FIRST].rearrange("i p c n -> p i c n")
                                         ).then_inc(ld_first, 16)
                    sp.dma_start(ident[:], a["ident"]).then_inc(ld_const, 16)
                    sp.dma_start(gbias[:], a["b_ih"].to_broadcast([P, NG * 512])).then_inc(ld_bias, 16)
                    sp.dma_start(gbias2[:], a["b_hh"].to_broadcast([P, NG * 512])).then_inc(ld_bias, 16)
                    sp.dma_start(w_hh[:], a["w_hh"]).then_inc(ld_gru, 16)
                    sp.wait_ge(ld_const, 16)
                    for i in range(FIRST):
                        sp.wait_ge(first_added, i + 1)
                        sp.dma_start(gi_tiles[i], gi_first[:, i % 2]).then_inc(first_stored[i % 2], 16)
                    for u in range(2):
                        sp.wait_ge(first_stored[u], 16 * (FIRST // 2))

                @block.gpsimd
                def _(pool):
                    pool.memset(ones[:], 1.0)
                    pool.memset(minus_half[:], -0.5)

                @block.tensor
                def _(pe):
                    pe.wait_ge(ld_wih, 16 * C)
                    pe.wait_ge(ld_first, 16)
                    for i in range(FIRST):
                        if i >= 2:
                            pe.wait_ge(first_added, i - 1)
                        for c in range(C):
                            for n in range(NG):
                                mm = pe.matmul(bank[3 * (i % 2) + n][:], xt_first[:, i, c], w_ih[:, c, n * 512:n * 512 + 512],
                                               start=(c == 0), stop=(c == C - 1))
                        mm.then_inc(first_mm, 1)

                @block.vector
                def _(dve):
                    dve.wait_ge(ld_bias, 32)
                    gb = gbias[:].rearrange("p (j g n) -> p j g n", j=4, g=G3)
                    gb2 = gbias2[:].rearrange("p (j g n) -> p j g n", j=4, g=G3)
                    for g in range(2):
                        dve.tensor_tensor(gb[:, :, g], gb[:, :, g], gb2[:, :, g], ALU.add).then_inc(bias_ready, 1)
                    dve.wait_ge(bias_ready, 2)
                    for i in range(FIRST):
                        dve.wait_ge(first_mm, i + 1)
                        if i >= 2:
                            dve.wait_ge(first_stored[i % 2], 16 * (i // 2))
                        for n in range(NG):
                            add = dve.tensor_tensor(gi_first[:, i % 2, n * 512:n * 512 + 512], bank[3 * (i % 2) + n][:],
                                                    gbias[:, n * 512:n * 512 + 512], ALU.add)
                        add.then_inc(first_added, 1)

        with gru as st:
            gates_in = sb(st, "gates_in", [P, 2, CH, G3 * P])
            xt_in = sb(st, "xt_in", [P, C, P])
            gi_out = sb(st, "gi_out", [P, 512])
            fold_in = sb(st, "fold_in", [P, QL + KL + DV + D])
            wqk_out = sb(st, "wqk_out", [P, QC * P])
            raw = sb(st, "raw", [P, 3, TW])
            b_hn = sb(st, "b_hn", [P, P])
            n_gate = sb(st, "n_gate", [P, 2, P])
            h = sb(st, "h", [P, P])
            h_t = sb(st, "h_t", [P, P])
            r = sb(st, "r", [P, P])
            z = sb(st, "z", [P, P])
            n = sb(st, "n", [P, P])
            rh = sb(st, "rh", [P, P])
            n_in = sb(st, "n_in", [P, P])
            zh = sb(st, "zh", [P, P])
            zn = sb(st, "zn", [P, P])
            bank_rn, bank_z, bank_gi, bank_qk, bank_vo = bank[0], bank[1], bank[2], bank[3], bank[4]
            HALVES = (slice(0, P // 2), slice(P // 2, P))
            gates_zero = sem("gates_zero")
            ld_gates = sem("ld_gates")
            rn_mm, z_mm = sem("rn_mm"), sem("z_mm")
            r_sig, z_sig = sem("r_sig"), sem("z_sig")
            n_tanh = sem("n_tanh")
            n_staged = sem("n_staged")
            rh_done, nin_done = sem("rh_done"), sem("nin_done")
            zh_done = sem("zh_done")
            zn_done = [sem("zn_done0"), sem("zn_done1")]
            h_done = [sem("h_done0"), sem("h_done1")]
            ht_done = [sem("ht_done0"), sem("ht_done1")]
            hist_done = sem("hist_done")
            ld_xt = sem("ld_xt")
            gi_mm = sem("gi_mm")
            gi_added = sem("gi_added")
            gi_stored = sem("gi_stored")
            ld_fold = sem("ld_fold")
            qk_mm = sem("qk_mm")
            vo_mm = sem("vo_mm")
            qk_out = sem("qk_out")
            vo_out = sem("vo_out")
            qk_stored = sem("qk_stored")
            ld_raw = sem("ld_raw")
            abs_done = sem("abs_done")
            NC = T // CH
            FOLD0 = GI_BODIES
            LAST0 = FOLD0 + FOLD_BODIES
            with nc.Block() as block:
                @block.sync
                def _(sp):
                    sp.dma_start(b_hn[:], a["b_hn"]).then_inc(ld_gru, 16)
                    sp.dma_start(h[:], a["h0"]).then_inc(ld_gru, 16)
                    sp.dma_start(gi_out[:, 0:1], a["zero_col"]).then_inc(gi_stored, 16)
                    sp.dma_start(wqk_out[:, 0:1], a["zero_col"]).then_inc(qk_stored, 16)

                    def load_chunk(k):
                        for j in range(4):
                            sp.dma_start(gates_in[32 * j:32 * j + B, k % 2],
                                         gi_scratch[k // (P // CH), :, bass.ds((k % (P // CH)) * CH, CH),
                                                    j * G3 * P:(j + 1) * G3 * P]).then_inc(ld_gates, 16)

                    def load_raw(i):
                        sp.dma_start(raw[:], a["ffn"][:, :, bass.ds(i * TW, TW)].rearrange("w p n -> p w n")
                                     ).then_inc(ld_raw, 16)

                    def common(i):
                        sp.wait_ge(abs_done, i + 1)
                        load_raw(i + 1)

                    def next_chunk(k):
                        sp.wait_ge(ld_gates, k * 64 + 128)
                        sp.wait_ge(nin_done, k * CH + CH + 1)
                        load_chunk(k + 2)

                    def gi_body(i):
                        common(i)
                        sp.wait_ge(gi_added, i + 2)
                        sp.dma_start(gi_tiles[FIRST + i // NG, :, bass.ds((i % NG) * 512, 512)], gi_out[:]
                                     ).then_inc(gi_stored, 16)
                        sp.wait_ge(gi_stored, i * 16 + 32)

                    sp.wait_ge(gates_zero, 1)
                    load_chunk(0)
                    sp.wait_ge(ld_gates, 64)
                    load_chunk(1)
                    load_raw(0)
                    sp.dma_start(xt_in[:], x_t[FIRST]).then_inc(ld_xt, 16)
                    sp.dma_start(fold_in[:], a["fold"][0]).then_inc(ld_fold, 16)
                    with sp.Fori(0, GI_BODIES // (2 * NG)) as m:
                        for v in range(2 * NG):
                            gi_body(m * 2 * NG + v)
                            if v == NG - 1:
                                sp.dma_start(xt_in[:], x_t[FIRST + 1 + m * 2]).then_inc(ld_xt, 16)
                            if v == 2 * NG - 1:
                                sp.dma_start(xt_in[:], x_t[(m * 2 + FIRST + 2) % (B * NT)]).then_inc(ld_xt, 16)
                            if v % 2 == 1:
                                next_chunk(m * NG + v // 2)

                    def fold_body(head):
                        i = head + FOLD0
                        common(i)
                        sp.wait_ge(qk_out, head + 2)
                        sp.dma_start(wqk_scratch[head], wqk_out[:]).then_inc(qk_stored, 16)
                        sp.wait_ge(vo_mm, head + 1)
                        sp.dma_start(fold_in[:], a["fold"][(head + 1) % NH]).then_inc(ld_fold, 16)

                    with sp.Fori(0, FOLD_BODIES // 2) as m:
                        for v in range(2):
                            fold_body(m * 2 + v)
                        next_chunk(m + FOLD0 // 2)
                    with sp.Fori(0, (BODIES - LAST0) // 2 - 2) as m:
                        for v in range(2):
                            common(m * 2 + v + LAST0)
                        next_chunk(m + LAST0 // 2)
                    for i in range(BODIES - 4, BODIES - 1):
                        common(i)
                    sp.wait_ge(ld_xt, 16 * (GI_BODIES // NG + 1))
                    sp.wait_ge(ld_fold, 16 * (NH + 1))
                    sp.wait_ge(ld_raw, 16 * BODIES)
                    sp.wait_ge(qk_stored, 16 * (NH + 1))
                    sp.wait_ge(ld_gates, 64 * NC)

                @block.gpsimd
                def _(pool):
                    ring = gates_in[:].rearrange("p k t n -> p (k t) n")
                    pool.memset(gates_in[:], 0.0).then_inc(gates_zero, 1)
                    pool.wait_ge(ld_gates, 64)
                    for v in range(2):
                        pool.tensor_copy(n_gate[:, v, :], ring[:, v, 2 * P:]).then_inc(n_staged, 1)
                    with pool.Fori(0, T // 2 - 1) as i:
                        for v in range(2):
                            pool.wait_ge(ld_gates, ((i * 2 + v + 2) // CH) * 64 + 64)
                            pool.wait_ge(nin_done, i * 2 + v + 2)
                            pool.tensor_copy(n_gate[:, v, :], ring[:, (i * 2 + v + 2) % (2 * CH), 2 * P:]
                                             ).then_inc(n_staged, 1)

                @block.tensor
                def _(pe):
                    def step(i, v):
                        now = i * U + v + 1
                        if v == 0:
                            pe.wait_ge(ld_gates, (i // (CH // U)) * 64 + 64)
                        gates = gates_in[:].rearrange("p k (s u) n -> p (k s) u n", u=U)[:, i % (2 * CH // U), v]
                        pe.wait_ge(rh_done, now)
                        pe.matmul(bank_rn[:, 0:P], ident[:], gates[:, 0:P], start=True, stop=False,
                                  skip_group_check=True)
                        pe.matmul(bank_rn[:, P:2 * P], ident[:], b_hn[:], start=False, stop=False,
                                  skip_group_check=True)
                        pe.wait_ge(z_sig, now)
                        pe.matmul(bank_z[:, 0:P], ident[:], gates[:, P:2 * P], start=True, stop=False,
                                  skip_group_check=True)
                        for c in range(C):
                            if c % 2 == 0:
                                pe.wait_ge(ht_done[c // 2], now)
                            for j in range(4):
                                mm = pe.matmul(bank_rn[32 * j:32 * j + B, 0:2 * P], h_t[:, 32 * c:32 * c + B],
                                               w_hh[:, c, j, 0:2 * P], start=False, stop=(c == C - 1),
                                               skip_group_check=True)
                        mm.then_inc(rn_mm, 1)
                        for c in range(C):
                            for j in range(4):
                                mm = pe.matmul(bank_z[32 * j:32 * j + B, 0:P], h_t[:, 32 * c:32 * c + B],
                                               w_hh[:, c, j, 2 * P:], start=False, stop=(c == C - 1),
                                               skip_group_check=True)
                        mm.then_inc(z_mm, 1)

                    pe.wait_ge(ld_gru, 48)
                    with pe.Fori(0, GI_BODIES) as i:
                        for v in range(U):
                            step(i, v)
                            if v == 2:
                                pe.wait_ge(ld_xt, (i // NG) * 16 + 16)
                                pe.wait_ge(gi_added, i + 1)
                            if 2 <= v < 2 + C:
                                c = v - 2
                                mm = pe.matmul(bank_gi[:], xt_in[:, c], w_ih[:, c, bass.ds((i % NG) * 512, 512)],
                                               start=(c == 0), stop=(c == C - 1))
                                if c == C - 1:
                                    mm.then_inc(gi_mm, 1)
                    with pe.Fori(0, FOLD_BODIES) as head:
                        for v in range(U):
                            step(head + FOLD0, v)
                            if v == 2:
                                pe.wait_ge(ld_fold, head * 16 + 16)
                                pe.wait_ge(qk_out, head + 1)
                                for m in range(QC):
                                    mm = pe.matmul(bank_qk[:, m * P:m * P + P], fold_in[:, m * P:m * P + P],
                                                   fold_in[:, QL:QL + KL], start=True, stop=True)
                                mm.then_inc(qk_mm, 1)
                            if v == 3:
                                pe.wait_ge(vo_out, head + 1)
                                pe.matmul(bank_vo[:], fold_in[:, QL + KL:QL + KL + DV], fold_in[:, QL + KL + DV:],
                                          start=True, stop=True).then_inc(vo_mm, 1)
                    with pe.Fori(LAST0, BODIES) as i:
                        for v in range(U):
                            step(i, v)

                @block.scalar
                def _(act):
                    act.wait_ge(ld_gru, 48)
                    act.activation(r[:], b_hn[:], ACT.Sigmoid).then_inc(r_sig, 1)
                    act.activation(z[:], b_hn[:], ACT.Sigmoid).then_inc(z_sig, 1)
                    act.activation(n[:], b_hn[:], ACT.Tanh).then_inc(hist_done, 1)
                    act.wait_ge(r_sig, 1)
                    act.wait_ge(z_sig, 1)
                    act.wait_ge(hist_done, 1)
                    with act.Fori(0, BODIES) as i:
                        for v in range(U):
                            t = i * U + v
                            act.wait_ge(rn_mm, t + 1)
                            act.activation(r[:], bank_rn[:, 0:P], ACT.Sigmoid).then_inc(r_sig, 1)
                            act.wait_ge(z_mm, t + 1)
                            act.activation(z[:], bank_z[:, 0:P], ACT.Sigmoid).then_inc(z_sig, 1)
                            act.wait_ge(nin_done, t + 2)
                            act.activation(n[:], n_in[:], ACT.Tanh).then_inc(n_tanh, 1)
                            act.wait_ge(ht_done[1], t + 2)
                            act.activation(hist[:, :, :, t].rearrange("p b c -> p c b"),
                                           h_t[:].rearrange("p (c q) -> p c q", c=C)[:, :, 0:B],
                                           ACT.Copy).then_inc(hist_done, 1)

                @block.vector
                def _(dve):
                    def step(i, v):
                        t = i * U + v
                        dve.wait_ge(r_sig, t + 2)
                        dve.tensor_tensor(rh[:], r[:], bank_rn[:, P:2 * P], ALU.mult).then_inc(rh_done, 1)
                        dve.wait_ge(n_staged, t + 1)
                        dve.wait_ge(rh_done, t + 2)
                        dve.tensor_tensor(n_in[:], rh[:], n_gate[:, v % 2, :], ALU.add).then_inc(nin_done, 1)
                        dve.wait_ge(z_sig, t + 2)
                        dve.tensor_tensor(zh[:], z[:], h[:], ALU.mult).then_inc(zh_done, 1)
                        dve.wait_ge(n_tanh, t + 1)
                        for q, half in enumerate(HALVES):
                            dve.scalar_tensor_tensor(zn[:, half], z[:, half], 1.0, n[:, half], ALU.subtract,
                                                     ALU.mult).then_inc(zn_done[q], 1)
                            if q == 0:
                                dve.wait_ge(zh_done, t + 1)
                            dve.wait_ge(zn_done[q], t + 1)
                            dve.tensor_tensor(h[:, half], zh[:, half], zn[:, half], ALU.subtract
                                              ).then_inc(h_done[q], 1)
                            if q == 0:
                                dve.wait_ge(hist_done, t + 1)
                            dve.wait_ge(h_done[q], t + 1)
                            dve.transpose(h_t[:, half], h[:, half]).then_inc(ht_done[q], 1)
                        if v == 0:
                            dve.wait_ge(ld_raw, i * 16 + 16)
                            dve.tensor_reduce(abs_part[:, i, :], raw[:], AX_X, ALU.add, apply_absolute_value=True
                                              ).then_inc(abs_done, 1)

                    dve.wait_ge(ld_gru, 48)
                    dve.memset(n_in[:], 0.0).then_inc(nin_done, 1)
                    dve.memset(rh[:], 0.0).then_inc(rh_done, 1)
                    dve.memset(zh[:], 0.0).then_inc(gi_added, 1)
                    dve.memset(zn[:], 0.0).then_inc(qk_out, 1)
                    dve.memset(wvo[:, 0, 0:1], 0.0).then_inc(vo_out, 1)
                    for q, half in enumerate(HALVES):
                        dve.transpose(h_t[:, half], h[:, half]).then_inc(ht_done[q], 1)
                    for stand_in in (nin_done, rh_done, gi_added, qk_out, vo_out):
                        dve.wait_ge(stand_in, 1)
                    with dve.Fori(0, GI_BODIES) as i:
                        for v in range(U):
                            step(i, v)
                            if v == 6:
                                dve.wait_ge(gi_mm, i + 1)
                                dve.wait_ge(gi_stored, i * 16 + 16)
                                dve.tensor_tensor(gi_out[:], bank_gi[:], gbias[:, bass.ds((i % NG) * 512, 512)], ALU.add
                                                  ).then_inc(gi_added, 1)
                    with dve.Fori(0, FOLD_BODIES) as head:
                        for v in range(U):
                            step(head + FOLD0, v)
                            if v == 4:
                                dve.wait_ge(qk_mm, head + 1)
                                dve.wait_ge(qk_stored, head * 16 + 16)
                                dve.tensor_copy(wqk_out[:], bank_qk[:, 0:QL]).then_inc(qk_out, 1)
                            if v == 5:
                                dve.wait_ge(vo_mm, head + 1)
                                dve.tensor_copy(wvo[:, head], bank_vo[:]).then_inc(vo_out, 1)
                    with dve.Fori(LAST0, BODIES) as i:
                        for v in range(U):
                            step(i, v)

        with ExitStack() as st:
            w_qa = sb(st, "w_qa", [P, C, QL])
            w_kva = sb(st, "w_kva", [P, C, 2 * P])
            rope = sb(st, "rope", [P, T])
            dup = sb(st, "dup", [P, P])
            ident_bf = sb(st, "ident_bf", [P, P], BF16)
            causal = sb(st, "causal", [P, P], BF16)
            ln_q = sb(st, "ln_q", [P, QC])
            ln_kv = sb(st, "ln_kv", [P, 1])
            head_w = sb(st, "head_w", [P, 2 * QL])
            q_raw = sb(st, "q_raw", [P, QC, T])
            q_lat = sb(st, "q_lat", [P, QC, T])
            kv_raw = sb(st, "kv_raw", [P, T])
            kv_t = sb(st, "kv_t", [P, T])
            kv_rows = sb(st, "kv_rows", [P, NT, KL])
            k_rot = sb(st, "k_rot", [P, T])
            sq = sb(st, "sq", [P, QC + 1, T])
            rms = sb(st, "rms", [P, 2, NT])
            rms_diag = sb(st, "rms_diag", [P, 2, T])
            q_t = sb(st, "q_t", [P, T])
            q_rot = sb(st, "q_rot", [P, T])
            prob = sb(st, "prob", [P, 10 * P])
            prob_t = sb(st, "prob_t", [P, 10 * P])
            negmax = sb(st, "negmax", [P, NT])
            psum_row = sb(st, "psum_row", [P, NT])
            pinv = sb(st, "pinv", [P, NT])
            o_t = sb(st, "o_t", [P, NH, T])
            raw_piece = sb(st, "raw_piece", [P, 3, TW])
            below = sb(st, "below", [P, 3, TW])
            tern_piece = sb(st, "tern_piece", [P, 3, TW], F32R)
            abs_sum = sb(st, "abs_sum", [P, 3])
            limits = sb(st, "limits", [P, 2, 3])
            ld_att = sem("ld_att")
            ld_head = sem("ld_head")
            ld_x1 = sem("ld_x1")
            lat_mm = sem("lat_mm")
            raw_done = sem("raw_done")
            rotk = sem("rotk")
            sq_done = sem("sq_done")
            ss_mm = sem("ss_mm")
            diag_done = sem("diag_done")
            spread_mm = sem("spread_mm")
            rms_a = sem("rms_a")
            lnq_scaled = sem("lnq_scaled")
            rms_b = sem("rms_b")
            lat_done = sem("lat_done")
            kdup_mm = sem("kdup_mm")
            krot_done = sem("krot_done")
            kvr_mm = sem("kvr_mm")
            kvr_done = sem("kvr_done")
            proj_mm = sem("proj_mm")
            qt_done = sem("qt_done")
            qrot_done = sem("qrot_done")
            s_mm = sem("s_mm")
            max_done = sem("max_done")
            exp_done = sem("exp_done")
            inv_done = sem("inv_done")
            norm_done = sem("norm_done")
            tr_mm = sem("tr_mm")
            ptA = sem("ptA")
            ptB = sem("ptB")
            pv_mm = sem("pv_mm")
            o_done = sem("o_done")
            y_mm = sem("y_mm")
            abs_total = sem("abs_total")
            abs_mm = sem("abs_mm")
            limit_step = sem("limit_step")
            ld_piece = sem("ld_piece")
            below_done = sem("below_done")
            tern_done = sem("tern_done")
            tern_stored = sem("tern_stored")
            y_done = sem("y_done")
            with nc.Block() as block:
                @block.sync
                def _(sp):
                    for dst, src in ((w_qa, "w_qa"), (w_kva, "w_kva"), (rope, "rope"), (dup, "dup"),
                                     (ident_bf, "ident_bf"), (causal, "causal"), (ln_q, "ln_q"), (ln_kv, "ln_kv")):
                        sp.dma_start(dst[:], a[src]).then_inc(ld_att, 16)

                    def load_head(g, head):
                        sp.dma_start(head_w[:, 0:QL], wqk_scratch[head]).then_inc(ld_head, 16)
                        sp.dma_start(head_w[:, QL:], a["w_rope"][head]).then_inc(ld_head, 16)

                    def load_piece(i):
                        sp.dma_start(raw_piece[:], a["ffn"][:, :, bass.ds(i * TW, TW)].rearrange("w p n -> p w n")
                                     ).then_inc(ld_piece, 16)

                    load_head(0, 0)
                    load_piece(0)
                    sp.dma_start(below[:, 0, 0:1], a["zero_col"]).then_inc(tern_stored, 16)
                    with sp.Fori(0, B) as b:
                        sp.wait_ge(lat_mm, b * 5 + 5)
                        sp.dma_start(x1[:, b], x_rows[b]).then_inc(ld_x1, 16)
                        with sp.Fori(0, NH) as hd:
                            sp.wait_ge(proj_mm, (b * NH + hd) * 2 + 2)
                            load_head(b * NH + hd + 1, (hd + 1) % NH)
                            g = b * NH + hd
                            sp.wait_ge(tern_done, g + 1)
                            sp.dma_start(tern_scratch[:, :, bass.ds(g * TW, TW)].rearrange("w p n -> p w n"), tern_piece[:].bitcast(F32)
                                         ).then_inc(tern_stored, 16)
                            load_piece((g + 1) % (B * NH))
                    sp.wait_ge(ld_head, 32 * (B * NH + 1))
                    sp.wait_ge(ld_piece, 16 * (B * NH + 1))
                    sp.wait_ge(tern_stored, 16 * (B * NH + 1))

                @block.tensor
                def _(pe):
                    def project(g):
                        pe.wait_ge(ld_head, g * 32 + 32)
                        for m in range(QC):
                            mm = pe.matmul(bank[4][:], head_w[:, m * P:m * P + P], q_lat[:, m, :],
                                           start=(m == 0), stop=(m == QC - 1))
                        mm.then_inc(proj_mm, 1)

                    def project_rot(g):
                        for m in range(QC):
                            mm = pe.matmul(bank[5][:], head_w[:, QL + m * P:QL + m * P + P], q_lat[:, m, :],
                                           start=(m == 0), stop=(m == QC - 1))
                        mm.then_inc(proj_mm, 1)

                    def scores(g):
                        pe.wait_ge(qt_done, g + 1)
                        pe.wait_ge(qrot_done, g + 1)
                        for q in range(NT):
                            nk = (q + 1) * P
                            pe.matmul(bank[q][:, 0:nk], q_t[:, q * P:q * P + P], kv_t[:, 0:nk],
                                      start=True, stop=False, skip_group_check=True)
                            pe.matmul(bank[q][:, q * P:nk], ident_bf[:], causal[:], start=False, stop=False,
                                      skip_group_check=True)
                            pe.matmul(bank[q][:, 0:nk], q_rot[:, q * P:q * P + P], k_rot[:, 0:nk],
                                      start=False, stop=True, skip_group_check=True).then_inc(s_mm, 1)

                    def turn(g):
                        for q in range(NT):
                            pe.wait_ge(norm_done, g * NT + q + 1)
                            for k in range(q + 1):
                                tr = pe.transpose(bank[k][:, (q - k) * P:(q - k + 1) * P],
                                                  prob[:, KEY0[q] + k * P:KEY0[q] + k * P + P], ident[:])
                        tr.then_inc(tr_mm, 1)

                    def values(g):
                        for k in range(NT):
                            if k % 2 == 0:
                                pe.wait_ge(ptA, g * 2 + k // 2 + 1)
                            else:
                                pe.wait_ge(ptB, g * 2 + k // 2 + 1)
                            mm = pe.matmul(bank[6][:, k * P:], kv_rows[:, k, :], prob_t[:, PT0[k]:PT0[k] + (NT - k) * P],
                                           start=(k == 0), stop=(k == NT - 1), skip_group_check=True)
                        mm.then_inc(pv_mm, 1)

                    pe.wait_ge(abs_total, 1)
                    pe.matmul(bank[7][:, 0:3], ones[:], abs_sum[:], start=True, stop=True).then_inc(abs_mm, 1)
                    pe.wait_ge(ld_att, 16 * 8)
                    pe.wait_ge(limit_step, 1)
                    with pe.Fori(0, B) as b:
                        for m in range(QC):
                            for c in range(C):
                                mm = pe.matmul(bank[m][:], w_qa[:, c, m * P:m * P + P], hist[:, b, c, :],
                                               start=(c == 0), stop=(c == C - 1))
                            mm.then_inc(lat_mm, 1)
                        for m in range(2):
                            for c in range(C):
                                mm = pe.matmul(bank[3 + m][:], w_kva[:, c, m * P:m * P + P], hist[:, b, c, :],
                                               start=(c == 0), stop=(c == C - 1))
                            mm.then_inc(lat_mm, 1)
                        pe.wait_ge(sq_done, b * 4 + 4)
                        for i, ms in enumerate((range(QC), range(QC, QC + 1))):
                            for q in range(NT):
                                for m in ms:
                                    mm = pe.matmul(bank[5 + i][:, q:q + 1], sq[:, m, q * P:q * P + P], ones[:, 0:1],
                                                   start=(m == ms[0]), stop=(m == ms[-1]))
                            mm.then_inc(ss_mm, 1)
                        pe.wait_ge(rotk, b + 1)
                        pe.matmul(bank[4][:], dup[:], k_rot[:], start=True, stop=True).then_inc(kdup_mm, 1)
                        for i in range(2):
                            pe.wait_ge(diag_done, b * 2 + i + 1)
                            pe.matmul(bank[6 + i][:], ones[:], rms_diag[:, i, :], start=True, stop=True
                                      ).then_inc(spread_mm, 1)
                        pe.wait_ge(lat_done, b * 4 + 4)
                        for k in range(NT):
                            tr = pe.transpose(bank[3][:, k * P:k * P + P], kv_t[:, k * P:k * P + P], ident[:])
                        tr.then_inc(kvr_mm, 1)
                        pe.wait_ge(krot_done, b + 1)
                        project(b * NH)
                        project_rot(b * NH)
                        with pe.Fori(0, NH - 1) as hd:
                            g = b * NH + hd
                            pe.wait_ge(krot_done, b + 1)
                            pe.wait_ge(kvr_done, b + 1)
                            scores(g)
                            project(g + 1)
                            turn(g)
                            project_rot(g + 1)
                            values(g)
                        g = b * NH + NH - 1
                        scores(g)
                        turn(g)
                        values(g)
                        pe.wait_ge(o_done, b * NH + NH)
                        for q in range(NT):
                            for hd in range(NH):
                                mm = pe.matmul(bank[q][:], o_t[:, hd, q * P:q * P + P], wvo[:, hd, :],
                                               start=(hd == 0), stop=(hd == NH - 1))
                            mm.then_inc(y_mm, 1)
                        pe.wait_ge(y_done, b * NT + NT)

                @block.gpsimd
                def _(pool):
                    with pool.Fori(0, B) as b:
                        pool.wait_ge(rms_a, b * 2 + 2)
                        flat = rms[:].rearrange("p i q -> p (i q)")
                        pool.tensor_tensor(flat, flat, minus_half[:, 0:1].to_broadcast([P, 2 * NT]), ALU.pow
                                           ).then_inc(rms_b, 1)

                @block.scalar
                def _(act):
                    def head(g):
                        for q in range(NT):
                            nk = (q + 1) * P
                            act.wait_ge(max_done, g * NT + q + 1)
                            act.activation(prob[:, KEY0[q]:KEY0[q] + nk], bank[q][:, 0:nk], ACT.Exp,
                                           bias=negmax[:, q:q + 1], scale=1.0,
                                           accum_out=psum_row[:, q:q + 1]).then_inc(exp_done, 1)

                    def copy_q(g):
                        act.wait_ge(proj_mm, g * 2 + 1)
                        act.activation(q_t[:], bank[4][:], ACT.Copy).then_inc(qt_done, 1)

                    def turned(g):
                        act.wait_ge(tr_mm, g + 1)
                        for k in (0, 2):
                            act.activation(prob_t[:, PT0[k]:PT0[k] + (NT - k) * P], bank[k][:, 0:(NT - k) * P],
                                           ACT.Copy).then_inc(ptA, 1)

                    def keep_o(g, hd):
                        act.wait_ge(pv_mm, g + 1)
                        act.activation(o_t[:, hd, :], bank[6][:], ACT.Copy).then_inc(o_done, 1)

                    with act.Fori(0, B) as b:
                        for m in range(QC):
                            act.wait_ge(raw_done, b * 4 + m + 1)
                            act.activation(sq[:, m, :], q_raw[:, m, :], ACT.Square).then_inc(sq_done, 1)
                        act.wait_ge(raw_done, b * 4 + 4)
                        act.activation(sq[:, QC, :], kv_raw[:], ACT.Square).then_inc(sq_done, 1)
                        act.wait_ge(kdup_mm, b + 1)
                        act.activation(k_rot[:], bank[4][:], ACT.Copy).then_inc(krot_done, 1)
                        act.wait_ge(kvr_mm, b + 1)
                        act.activation(kv_rows[:].rearrange("p k n -> p (k n)"), bank[3][:], ACT.Copy
                                       ).then_inc(kvr_done, 1)
                        copy_q(b * NH)
                        with act.Fori(0, NH - 1) as hd:
                            g = b * NH + hd
                            head(g)
                            copy_q(g + 1)
                            turned(g)
                            keep_o(g, hd)
                        g = b * NH + NH - 1
                        head(g)
                        turned(g)
                        keep_o(g, NH - 1)

                @block.vector
                def _(dve):
                    def head(g):
                        def normalise(q):
                            nk = (q + 1) * P
                            dve.wait_ge(exp_done, g * NT + q + 1)
                            dve.reciprocal(pinv[:, q:q + 1], psum_row[:, q:q + 1]).then_inc(inv_done, 1)
                            dve.wait_ge(inv_done, g * NT + q + 1)
                            dve.tensor_scalar(prob[:, KEY0[q]:KEY0[q] + nk], prob[:, KEY0[q]:KEY0[q] + nk],
                                              pinv[:, q:q + 1], None, ALU.mult).then_inc(norm_done, 1)

                        for q in range(NT):
                            nk = (q + 1) * P
                            dve.wait_ge(s_mm, g * NT + q + 1)
                            dve.tensor_reduce(negmax[:, q:q + 1], bank[q][:, 0:nk], AX_X, ALU.max,
                                              negate=True).then_inc(max_done, 1)
                            if q > 0:
                                normalise(q - 1)
                        normalise(NT - 1)

                    def turned(g):
                        dve.wait_ge(tr_mm, g + 1)
                        for k in (1, 3):
                            dve.tensor_copy(prob_t[:, PT0[k]:PT0[k] + (NT - k) * P], bank[k][:, 0:(NT - k) * P]
                                            ).then_inc(ptB, 1)

                    def rotate_q(g):
                        dve.wait_ge(proj_mm, g * 2 + 2)
                        dve.tensor_tensor(q_rot[:], bank[5][:], rope[:], ALU.mult).then_inc(qrot_done, 1)

                    def ternary(g):
                        dve.wait_ge(ld_piece, g * 16 + 16)
                        for w in range(3):
                            ins = dve.tensor_scalar(below[:, w, :], raw_piece[:, w, :], limits[:, 1, w:w + 1], None,
                                                    ALU.is_lt)
                        ins.then_inc(below_done, 1)
                        dve.wait_ge(below_done, g + 1)
                        dve.wait_ge(tern_stored, g * 16 + 16)
                        for w in range(3):
                            ins = dve.scalar_tensor_tensor(tern_piece[:, w, :], raw_piece[:, w, :], limits[:, 0, w:w + 1],
                                                           below[:, w, :], ALU.is_gt, ALU.subtract)
                        ins.then_inc(tern_done, 1)

                    dve.tensor_reduce(abs_sum[:], abs_part[:].rearrange("p i w -> p w i"), AX_X, ALU.add
                                      ).then_inc(abs_total, 1)
                    dve.wait_ge(abs_mm, 1)
                    dve.tensor_scalar(w_scale[:], bank[7][:, 0:3], 1.0 / (D * F), TERN_EPS, ALU.mult, ALU.add
                                      ).then_inc(limit_step, 1)
                    dve.wait_ge(limit_step, 1)
                    dve.wait_ge(tern_stored, 16)
                    for i, factor in enumerate((0.5, -0.5)):
                        dve.tensor_scalar(limits[:, i, :], w_scale[:], factor, None, ALU.mult).then_inc(limit_step, 1)
                    dve.wait_ge(limit_step, 3)
                    dve.wait_ge(ld_att, 16 * 8)
                    dve.tensor_scalar(ln_q[:], ln_q[:], QSCALE, None, ALU.mult).then_inc(lnq_scaled, 1)
                    dve.wait_ge(lnq_scaled, 1)
                    with dve.Fori(0, B) as b:
                        for m in range(QC):
                            dve.wait_ge(lat_mm, b * 5 + m + 1)
                            dve.tensor_copy(q_raw[:, m, :], bank[m][:]).then_inc(raw_done, 1)
                        dve.wait_ge(lat_mm, b * 5 + 4)
                        dve.tensor_copy(kv_raw[:], bank[3][:]).then_inc(raw_done, 1)
                        dve.wait_ge(lat_mm, b * 5 + 5)
                        dve.tensor_tensor(k_rot[:], bank[4][:], rope[:], ALU.mult).then_inc(rotk, 1)
                        for i, width in enumerate((QL, KL)):
                            dve.wait_ge(ss_mm, b * 2 + i + 1)
                            dve.tensor_scalar(rms[:, i], bank[5 + i][:, 0:NT], 1.0 / width, RMS_EPS, ALU.mult, ALU.add
                                              ).then_inc(rms_a, 1)
                        dve.wait_ge(rms_b, b + 1)
                        for i in range(2):
                            for q in range(NT):
                                diag = dve.tensor_scalar(rms_diag[:, i, q * P:q * P + P], ident[:], rms[:, i, q:q + 1],
                                                         None, ALU.mult)
                            diag.then_inc(diag_done, 1)
                        dve.wait_ge(spread_mm, b * 2 + 2)
                        dve.scalar_tensor_tensor(kv_t[:], kv_raw[:], ln_kv[:, 0:1], bank[7][:], ALU.mult, ALU.mult
                                                 ).then_inc(lat_done, 1)
                        for m in range(QC):
                            dve.scalar_tensor_tensor(q_lat[:, m, :], q_raw[:, m, :], ln_q[:, m:m + 1], bank[6][:],
                                                     ALU.mult, ALU.mult).then_inc(lat_done, 1)
                        rotate_q(b * NH)
                        with dve.Fori(0, NH - 1) as hd:
                            g = b * NH + hd
                            head(g)
                            turned(g)
                            rotate_q(g + 1)
                            ternary(g)
                        head(b * NH + NH - 1)
                        turned(b * NH + NH - 1)
                        ternary(b * NH + NH - 1)
                        dve.wait_ge(ld_x1, b * 16 + 16)
                        for q in range(NT):
                            dve.wait_ge(y_mm, b * NT + q + 1)
                            dve.tensor_tensor(x1[:, b, q, :], bank[q][:], x1[:, b, q, :], ALU.add).then_inc(y_done, 1)

        att_weights.close()

        tern = [sb(ctx, f"tern_{w}", [P, 4 * F], F32R) for w in ("up", "gate", "down")]
        shift = sb(ctx, "shift", [P, B, D])
        gamma_t = sb(ctx, "gamma_t", [P, C])
        beta_t = sb(ctx, "beta_t", [P, C])
        NB = B * NBLK
        with ExitStack() as st:
            wk_t = sb(st, "wk_t", [P, C, D])
            wo_t = sb(st, "wo_t", [P, C, D])
            block_sel = sb(st, "block_sel", [P, 2])
            batch_mask = sb(st, "batch_mask", [NB, B])
            batch_row = sb(st, "batch_row", [B, B * P])
            key_w = sb(st, "key_w", [NB, D])
            query = sb(st, "query", [NB, D])
            blocks_t = sb(st, "blocks_t", [P, C, NB])
            blocks = sb(st, "blocks", [NB, D])
            keys = sb(st, "keys", [NB, D])
            junk = sb(st, "junk", [NB, D])
            stat = sb(st, "stat", [NB, 8])
            row = sb(st, "row", [1, 3, NB])
            rowb = sb(st, "rowb", [1, 3, B])
            pick = sb(st, "pick", [NB, B])
            mix_t = sb(st, "mix_t", [P, C * B])
            proj = sb(st, "proj", [B, D])
            ld_c2 = sem("ld_c2")
            ld_tern = [sem(f"ld_tern{i}") for i in range(4)]
            pe_step = sem("pe_step")
            dve_step = sem("dve_step")
            act_step = sem("act_step")
            pool_step = sem("pool_step")
            with nc.Block() as block:
                @block.sync
                def _(sp):
                    for dst, src in ((wk_t[:], a["wk_t"]), (wo_t[:], a["wo_t"]), (block_sel[:], a["block_sel"]),
                                     (batch_mask[:], a["batch_mask"]), (batch_row[:], a["batch_row"]),
                                     (key_w[:], a["key_w"].to_broadcast([NB, D])),
                                     (query[:], a["query"].to_broadcast([NB, D])),
                                     (gamma_t[:], a["gamma_t"]), (beta_t[:], a["beta_t"])):
                        sp.dma_start(dst, src).then_inc(ld_c2, 16)
                    for i in range(4):
                        for w in range(2):
                            sp.dma_start(tern[w][:].bitcast(F32).rearrange("p (c e) -> p c e", c=C)[:, :, i * 512:i * 512 + 512],
                                         tern_scratch[w].rearrange("p (c e) -> p c e", c=C)[:, :, i * 512:i * 512 + 512]
                                         ).then_inc(ld_tern[i], 16)
                        sp.dma_start(tern[2][:, i * F:(i + 1) * F].bitcast(F32), tern_scratch[2][:, i * F:(i + 1) * F]
                                     ).then_inc(ld_tern[i], 16)

                @block.tensor
                def _(pe):
                    pe.wait_ge(ld_c2, 16 * 9)
                    for b in range(B):
                        for q in range(NT):
                            for c in range(C):
                                at = c * NB + b * NBLK + 2 * q
                                mm = pe.matmul(bank[0][:, at:at + 2], x1[:, b, q, c * P:c * P + P], block_sel[:],
                                               start=True, stop=True)
                    mm.then_inc(pe_step, 1)
                    pe.wait_ge(dve_step, 1)
                    for c in range(C):
                        pe.matmul(bank[1][0:NB, :], blocks_t[:, c, :], wk_t[:, c, :], start=(c == 0), stop=(c == C - 1))
                    for c in range(C):
                        mm = pe.transpose(bank[2][0:NB, c * P:c * P + P], blocks_t[:, c, :], ident[:])
                    mm.then_inc(pe_step, 1)
                    pe.wait_ge(dve_step, 7)
                    pe.transpose(bank[3][0:1, 0:NB], stat[:, 3:4], ident[0:NB, 0:NB]).then_inc(pe_step, 1)
                    pe.wait_ge(dve_step, 12)
                    pe.matmul(bank[4][0:NB, 0:1], row[0:1, 2, :], ones[0:1, 0:1], start=True, stop=True
                              ).then_inc(pe_step, 1)
                    pe.wait_ge(dve_step, 13)
                    for c in range(C):
                        mm = pe.matmul(bank[5][:, c * B:c * B + B], blocks[:, c * P:c * P + P], pick[:],
                                       start=True, stop=True)
                    mm.then_inc(pe_step, 1)
                    pe.wait_ge(dve_step, 14)
                    for c in range(C):
                        mm = pe.matmul(bank[6][0:B, :], mix_t[:, c * B:c * B + B], wo_t[:, c, :],
                                       start=(c == 0), stop=(c == C - 1))
                    mm.then_inc(pe_step, 1)
                    pe.wait_ge(dve_step, 15)
                    for b in range(B):
                        mm = pe.matmul(bank[b][:], batch_row[:, b * P:b * P + P], proj[:], start=True, stop=True)
                    mm.then_inc(pe_step, 1)

                @block.gpsimd
                def _(pool):
                    pool.wait_ge(dve_step, 6)
                    pool.tensor_tensor(stat[:, 2:3], stat[:, 2:3], minus_half[0:NB, :], ALU.pow).then_inc(pool_step, 1)

                @block.scalar
                def _(act):
                    act.wait_ge(dve_step, 2)
                    act.activation(junk[:], keys[:], ACT.Square, accum_out=stat[:, 0:1]).then_inc(act_step, 1)
                    act.wait_ge(dve_step, 9)
                    act.activation(row[0:1, 1, :], row[0:1, 0, :], ACT.Exp).then_inc(act_step, 1)

                @block.vector
                def _(dve):
                    steps = [0]

                    def step(ins):
                        steps[0] += 1
                        ins.then_inc(dve_step, 1)
                        dve.wait_ge(dve_step, steps[0])

                    dve.wait_ge(ld_c2, 16 * 9)
                    dve.wait_ge(pe_step, 1)
                    step(dve.tensor_copy(blocks_t[:].rearrange("p c n -> p (c n)"), bank[0][:, 0:C * NB]))
                    dve.wait_ge(pe_step, 2)
                    step(dve.tensor_copy(keys[:], bank[1][0:NB, :]))
                    step(dve.tensor_copy(blocks[:], bank[2][0:NB, :]))
                    step(dve.tensor_tensor(query[:], query[:], key_w[:], ALU.mult))
                    step(dve.scalar_tensor_tensor(query[:], keys[:], 1.0, query[:], ALU.mult, ALU.mult,
                                                  accum_out=stat[:, 1:2]))
                    dve.wait_ge(act_step, 1)
                    step(dve.tensor_scalar(stat[:, 2:3], stat[:, 0:1], 1.0 / D, RMS_EPS, ALU.mult, ALU.add))
                    dve.wait_ge(pool_step, 1)
                    step(dve.tensor_tensor(stat[:, 3:4], stat[:, 1:2], stat[:, 2:3], ALU.mult))
                    dve.wait_ge(pe_step, 3)
                    by_batch = bank[3][0:1, 0:NB].rearrange("o (b n) -> o b n", b=B)
                    out0, out1, out2 = (row[0:1, i, :].rearrange("o (b n) -> o b n", b=B) for i in range(3))
                    step(dve.tensor_reduce(rowb[0:1, 0, :], by_batch, AX_X, ALU.max))
                    step(dve.tensor_tensor(out0, by_batch, rowb[0:1, 0, :].unsqueeze(2).to_broadcast([1, B, NBLK]),
                                           ALU.subtract))
                    dve.wait_ge(act_step, 2)
                    step(dve.tensor_reduce(rowb[0:1, 1, :], out1, AX_X, ALU.add))
                    step(dve.reciprocal(rowb[0:1, 2, :], rowb[0:1, 1, :]))
                    step(dve.tensor_tensor(out2, out1, rowb[0:1, 2, :].unsqueeze(2).to_broadcast([1, B, NBLK]), ALU.mult))
                    dve.wait_ge(pe_step, 4)
                    step(dve.tensor_scalar(pick[:], batch_mask[:], bank[4][0:NB, 0:1], None, ALU.mult))
                    dve.wait_ge(pe_step, 5)
                    step(dve.tensor_copy(mix_t[:], bank[5][:, 0:C * B]))
                    dve.wait_ge(pe_step, 6)
                    step(dve.tensor_copy(proj[:], bank[6][0:B, :]))
                    dve.wait_ge(pe_step, 7)
                    for b in range(B):
                        dve.tensor_copy(shift[:, b, :], bank[b][:])

        with ExitStack() as st:
            up_w = tern[0][:].rearrange("p (c e) -> p c e", c=C)
            gate_w = tern[1][:].rearrange("p (c e) -> p c e", c=C)
            down_w = tern[2][:].rearrange("p (t d) -> p t d", t=FT)
            xn = sb(st, "xn", [P, NT, D])
            bn = sb(st, "bn", [P, 6])
            bn_pad = sb(st, "bn_pad", [P, 1])
            mv = sb(st, "mv", [P, NT, 2])
            rstd = sb(st, "rstd", [P, NT])
            LN_STEPS = 4 * NT + 1
            xg = sb(st, "xg", [P, 2, T])
            x_hi = sb(st, "x_hi", [P, C, T], F32R)
            x_lo = sb(st, "x_lo", [P, C, T], F32R)
            act_up = sb(st, "act_up", [P, 2, T])
            hid = sb(st, "hid", [P, 2, T])
            h_hi = sb(st, "h_hi", [P, 2, T], F32R)
            h_lo = sb(st, "h_lo", [P, 2, T], F32R)
            y_out = sb(st, "y_out", [P, NT, D])
            ln_step = sem("ln_step")
            rstd_done = sem("rstd_done")
            xn_t = sem("xn_t")
            xg_done = sem("xg_done")
            x_split = sem("x_split")
            up_mm = sem("up_mm")
            down_mm = sem("down_mm")
            silu_done = sem("silu_done")
            hid_done = sem("hid_done")
            hhi_done = sem("hhi_done")
            hlo_done = sem("hlo_done")
            y_scaled = sem("y_scaled")
            y_stored = sem("y_stored")
            out_rows = a["out"].rearrange("b (q p) d -> b p q d", p=P)
            with nc.Block() as block:
                @block.sync
                def _(sp):
                    sp.dma_start(y_out[:, 0, 0:1], a["zero_col"]).then_inc(y_stored, 16)
                    with sp.Fori(0, B) as g:
                        sp.wait_ge(y_scaled, g * NT + NT + 1)
                        sp.dma_start(out_rows[g], y_out[:]).then_inc(y_stored, 16)
                    sp.wait_ge(y_stored, 16 * B + 16)

                @block.tensor
                def _(pe):
                    def expand(g, e):
                        up, gate = bank[4 + 2 * (e % 2)], bank[5 + 2 * (e % 2)]
                        if e % 4 == 0:
                            pe.wait_ge(ld_tern[e // 4], 48)
                        for w, out in ((up_w, up), (gate_w, gate)):
                            for c in range(C):
                                for half, part in enumerate((x_hi, x_lo)):
                                    mm = pe.matmul(out[:], w[:, c, e * P:e * P + P], part[:, c, :],
                                                   start=(c == 0 and half == 0), stop=(c == C - 1 and half == 1))
                        mm.then_inc(up_mm, 1)

                    def contract(g, e):
                        pe.wait_ge(hhi_done, g * FT + e + 1)
                        pe.wait_ge(hlo_done, g * FT + e + 1)
                        for half, part in enumerate((h_hi, h_lo)):
                            for q in range(NT):
                                mm = pe.matmul(bank[q][:], part[:, e % 2, q * P:q * P + P], down_w[:, e, :],
                                               start=(e == 0 and half == 0), stop=(e == FT - 1 and half == 1))
                        mm.then_inc(down_mm, 1)

                    with pe.Fori(0, B) as g:
                        pe.wait_ge(ln_step, g * LN_STEPS + LN_STEPS)
                        pe.wait_ge(hid_done, g * FT + 1)
                        for c in range(C):
                            for q in range(NT):
                                tr = pe.transpose(bank[4 + c][:, q * P:q * P + P], xn[:, q, c * P:c * P + P], ident[:])
                            tr.then_inc(xn_t, 1)
                        pe.wait_ge(x_split, g * 2 * C + 2 * C)
                        for e in range(FT):
                            if e >= 2:
                                pe.wait_ge(hid_done, g * FT + e)
                            expand(g, e)
                            if e == 1:
                                pe.wait_ge(y_scaled, g * NT + 1)
                            if e > 0:
                                contract(g, e - 1)
                        contract(g, FT - 1)

                @block.scalar
                def _(act):
                    with act.Fori(0, B) as g:
                        for c in range(C):
                            act.wait_ge(xn_t, g * C + c + 1)
                            if c >= 2:
                                act.wait_ge(x_split, g * 2 * C + 2 * (c - 1))
                            act.activation(xg[:, c % 2, :], bank[4 + c][:], ACT.Identity, bias=beta_t[:, c:c + 1],
                                           scale=gamma_t[:, c:c + 1]).then_inc(xg_done, 1)
                        for e in range(FT):
                            act.wait_ge(up_mm, g * FT + e + 1)
                            if e >= 2:
                                act.wait_ge(hid_done, g * FT + e)
                            act.activation(act_up[:, e % 2, :], bank[4 + 2 * (e % 2)][:], ACT.Silu,
                                           scale=w_scale[:, 0:1]).then_inc(silu_done, 1)
                            act.wait_ge(hid_done, g * FT + e + 2)
                            if e >= 2:
                                act.wait_ge(down_mm, g * FT + e - 1)
                            act.activation(h_hi[:, e % 2, :], hid[:, e % 2, :], ACT.Copy).then_inc(hhi_done, 1)

                @block.vector
                def _(dve):
                    dve.memset(rstd[:], 0.0).then_inc(hid_done, 1)
                    dve.memset(mv[:], 0.0).then_inc(y_scaled, 1)
                    dve.wait_ge(hid_done, 1)
                    dve.wait_ge(y_scaled, 1)
                    with dve.Fori(0, B) as g:
                        for q in range(NT):
                            def chain(i, ins):
                                ins.then_inc(ln_step, 1)
                                dve.wait_ge(ln_step, g * LN_STEPS + q * 3 + i)
                            chain(1, dve.tensor_tensor(xn[:, q, :], x1[:, g, q, :], shift[:, g, :], ALU.add))
                            chain(2, dve.bn_stats(bn[:], xn[:, q, :]))
                            dve.memset(bn_pad[:], 0.0)
                            chain(3, dve.bn_aggr(mv[:, q, :], bn[:]))
                        dve.tensor_scalar(rstd[:], mv[:, :, 1], RMS_EPS, None, ALU.add).then_inc(ln_step, 1)
                        dve.wait_ge(rstd_done, g + 1)
                        for q in range(NT):
                            dve.tensor_scalar(xn[:, q, :], xn[:, q, :], mv[:, q, 0:1], rstd[:, q:q + 1], ALU.subtract,
                                              ALU.mult).then_inc(ln_step, 1)
                        for c in range(C):
                            dve.wait_ge(xg_done, g * C + c + 1)
                            dve.tensor_copy(x_hi[:, c, :], xg[:, c % 2, :]).then_inc(x_split, 1)
                            dve.wait_ge(x_split, g * 2 * C + 2 * c + 1)
                            dve.tensor_tensor(x_lo[:, c, :], xg[:, c % 2, :], x_hi[:, c, :].bitcast(F32), ALU.subtract
                                              ).then_inc(x_split, 1)
                        for e in range(FT):
                            dve.wait_ge(silu_done, g * FT + e + 1)
                            if e >= 2:
                                dve.wait_ge(hhi_done, g * FT + e - 1)
                            dve.scalar_tensor_tensor(hid[:, e % 2, :], bank[5 + 2 * (e % 2)][:], w_scale[:, 1:2],
                                                     act_up[:, e % 2, :], ALU.mult, ALU.mult).then_inc(hid_done, 1)
                            dve.wait_ge(hhi_done, g * FT + e + 1)
                            dve.tensor_tensor(h_lo[:, e % 2, :], hid[:, e % 2, :], h_hi[:, e % 2, :].bitcast(F32),
                                              ALU.subtract).then_inc(hlo_done, 1)
                        dve.wait_ge(down_mm, g * FT + FT)
                        dve.wait_ge(y_stored, g * 16 + 16)
                        for q in range(NT):
                            dve.scalar_tensor_tensor(y_out[:, q, :], bank[q][:], w_scale[:, 2:3], x1[:, g, q, :],
                                                     ALU.mult, ALU.add).then_inc(y_scaled, 1)

                @block.gpsimd
                def _(pool):
                    with pool.Fori(0, B) as g:
                        pool.wait_ge(ln_step, g * LN_STEPS + 3 * NT + 1)
                        pool.tensor_tensor(rstd[:], rstd[:], minus_half[:, 0:1].to_broadcast([P, NT]), ALU.pow
                                           ).then_inc(rstd_done, 1)


def _tables():
    eye = np.eye(P, dtype=np.float32)
    half = np.arange(P) % DR
    inv_freq = 1.0 / 10000.0 ** (np.arange(0, DR, 2, dtype=np.float32) / DR)
    freqs = np.outer(np.arange(T, dtype=np.float32), inv_freq)
    cos, sin = np.cos(freqs).T, np.sin(freqs).T
    q, k = np.meshgrid(np.arange(P), np.arange(P), indexing="ij")
    return {
        "ident": eye,
        "dup": (half[:, None] == half[None, :]).astype(np.float32),
        "rope": np.concatenate([cos, cos, -sin, sin]).astype(np.float32),
        "causal": np.where(k > q, np.float32(-1e30), np.float32(0)),
        "block_sel": np.kron(np.eye(2), np.ones((BLK, 1))).astype(np.float32),
        "batch_mask": np.kron(np.eye(B), np.ones((NBLK, 1))).astype(np.float32),
        "batch_row": np.kron(np.eye(B), np.ones((1, P))).astype(np.float32),
        "zero_col": np.zeros((P, 1), np.float32),
    }


def kernel(x, cond_2048, L0_cond_W_ih, L0_cond_W_hh, L0_cond_b_ih, L0_cond_b_hh, L0_attn_w_q_a, L0_attn_q_a_ln,
           L0_attn_w_q_b, L0_attn_w_kv_a, L0_attn_kv_a_ln, L0_attn_w_kv_b, L0_attn_w_out, L0_cond2_rms_weight,
           L0_cond2_Wk, L0_cond2_Wo, L0_cond2_ln_gamma, L0_cond2_ln_beta, L0_ffn_W_up, L0_ffn_W_gate, L0_ffn_W_down):
    import ml_dtypes
    from concourse import bacc
    from concourse.bass_utils import run_bass_kernel_spmd

    def np32(v):
        return np.ascontiguousarray(np.asarray(v))

    def tiles(w):
        return w.reshape(-1, P, w.shape[-1]).transpose(1, 0, 2)

    def state_tiles(w):
        return w.reshape(4, C, 32, w.shape[-1]).transpose(0, 2, 1, 3).reshape(P, C, w.shape[-1])

    def gate_cols(w):
        return w.reshape(-1, G3, 4, P).transpose(0, 2, 1, 3).reshape(-1, 4 * G3 * P)

    x, cond = np32(x), np32(cond_2048)
    w_hh, b_hh = np32(L0_cond_W_hh), np32(L0_cond_b_hh)
    t = _tables()
    arrays = dict(t)
    arrays["causal"] = t["causal"].astype(ml_dtypes.bfloat16)
    arrays["ident_bf"] = t["ident"].astype(ml_dtypes.bfloat16)
    arrays["x_t"] = x.reshape(B, NT, P, C, P).transpose(1, 0, 4, 3, 2).reshape(B * NT, P, C, P)
    arrays["x_rows"] = x.reshape(B, NT, P, D).transpose(0, 2, 1, 3)
    arrays["w_ih"] = tiles(gate_cols(np32(L0_cond_W_ih)))
    arrays["b_ih"] = gate_cols(np32(L0_cond_b_ih)[None])
    arrays["b_hh"] = gate_cols(b_hh[None])
    w_rnz = w_hh.reshape(D, G3, 4, P)[:, [0, 2, 1]].transpose(0, 2, 1, 3).reshape(D, -1)
    arrays["w_hh"] = state_tiles(w_rnz).reshape(P, C, 4, G3 * P)
    state = np.zeros((4, 32, P), np.float32)
    state[:, :B] = cond.reshape(B, 4, P).transpose(1, 0, 2)
    arrays["h0"] = state.reshape(P, P)
    bias = np.zeros((4, 32, P), np.float32)
    bias[:, :B] = b_hh[2 * D:].reshape(4, 1, P)
    arrays["b_hn"] = bias.reshape(P, P)
    w_qb = np32(L0_attn_w_q_b).reshape(QL, NH, DN + DR)
    w_kvb = np32(L0_attn_w_kv_b).reshape(KL, NH, DN + DV)
    w_o = np32(L0_attn_w_out).reshape(NH, DV, D)
    arrays["fold"] = np.concatenate([w_qb[:, :, :DN].transpose(1, 2, 0), w_kvb[:, :, :DN].transpose(1, 2, 0),
                                     w_kvb[:, :, DN:].transpose(1, 2, 0), w_o], axis=2)

    def rotary(w):
        return np.concatenate([w[..., 0::2], w[..., 1::2], w[..., 1::2], w[..., 0::2]], axis=-1)

    arrays["w_rope"] = rotary(w_qb[:, :, DN:]).reshape(QC, P, NH, P).transpose(2, 1, 0, 3).reshape(NH, P, QC * P)
    w_kva = np32(L0_attn_w_kv_a)
    arrays["w_qa"] = state_tiles(np32(L0_attn_w_q_a))
    arrays["w_kva"] = state_tiles(np.concatenate([w_kva[:, :KL], rotary(w_kva[:, KL:])], axis=1))
    arrays["ln_q"] = np32(L0_attn_q_a_ln).reshape(QC, P).T
    arrays["ln_kv"] = np32(L0_attn_kv_a_ln).reshape(P, 1)
    arrays["wk_t"] = tiles(np32(L0_cond2_Wk).T)
    arrays["wo_t"] = tiles(np32(L0_cond2_Wo).T)
    arrays["key_w"] = np32(L0_cond2_rms_weight)[None]
    arrays["query"] = cond[1:2]
    arrays["gamma_t"] = np32(L0_cond2_ln_gamma).reshape(C, P).T
    arrays["beta_t"] = np32(L0_cond2_ln_beta).reshape(C, P).T
    arrays["ffn"] = np.stack([tiles(np32(w).T).reshape(P, -1) for w in (L0_ffn_W_up, L0_ffn_W_gate, L0_ffn_W_down)])

    nc = bacc.Bacc("TRN2", target_bir_lowering=False, num_devices=1)
    arrays = {k: np.ascontiguousarray(v) for k, v in arrays.items()}
    aps = {k: nc.dram_tensor(f"in_{k}", v.shape, mybir.dt.from_np(v.dtype), kind="ExternalInput").ap()
           for k, v in arrays.items()}
    aps["out"] = nc.dram_tensor("out_0", [B, T, D], F32, kind="ExternalOutput").ap()
    build(nc, aps)
    result = run_bass_kernel_spmd(nc, [{f"in_{k}": v for k, v in arrays.items()}], core_ids=[0])
    return result.results[0]["out_0"]
```

```python
from contextlib import ExitStack

import concourse.bass as bass
import numpy as np
from concourse import mybir

F32 = mybir.dt.float32
F32R = mybir.dt.float32r
BF16 = mybir.dt.bfloat16
ACT = mybir.ActivationFunctionType
ALU = mybir.AluOpType
AX_X = mybir.AxisListType.X

P = 128
B, T, D = 4, 512, 512
C = D // P
G3 = 3
NH = 16
QL, KL = 384, 128
DN, DR, DV = 128, 64, 128
QC = QL // P
NT = T // P
F = 2048
FT = F // P
CH = 16
U = 8
BODIES = T // U
NG = 3
TS = P // B
TILES = T // TS
FIRST = 2
GI_BODIES = NG * (TILES - FIRST)
FOLD_BODIES = NH
TW = 4 * F // (B * NH)
NBLK, BLK = 8, T // 8
QSCALE = float(1.0 / np.sqrt(DN + DR))
RMS_EPS = 1e-6
TERN_EPS = 1e-8
KEY0 = [0, 128, 384, 768]
ORDER = [1, 0, 2, 3]
PT0 = [0, 512, 1024, 896]


def build(nc, a):
    x_t, x_rows = a["x_t"], a["x_rows"]
    gi_scratch = nc.dram_tensor("gi_scratch", [TILES, B, TS, NG * 512], F32, kind="Internal").ap()
    gi_tiles = gi_scratch.rearrange("i b s n -> i (b s) n")
    wqk_scratch = nc.dram_tensor("wqk_scratch", [NH, P, 2 * QC * P], F32, kind="Internal").ap()
    tern_scratch = nc.dram_tensor("tern_scratch", [3, P, 4 * F], F32, kind="Internal").ap()

    with ExitStack() as ctx:
        def sem(name):
            return ctx.enter_context(nc.semaphore(name))

        def sb(stack, name, shape, dt=F32):
            return stack.enter_context(nc.sbuf_tensor(name, shape, dt))

        bank = [ctx.enter_context(nc.psum_tensor(f"bank{i}", [P, 512], F32)) for i in range(8)]

        ident = sb(ctx, "ident", [P, P])
        ones = sb(ctx, "ones", [P, P])
        minus_half = sb(ctx, "minus_half", [P, 1])
        abs_part = sb(ctx, "abs_part", [P, BODIES, 3])
        w_scale = sb(ctx, "w_scale", [P, 3])
        hist = sb(ctx, "hist", [P, B, C, T])
        x1 = hist
        att_weights = ExitStack()
        wvo = sb(att_weights, "wvo", [P, NH, D])

        gru = ExitStack()
        w_ih = sb(gru, "w_ih", [P, C, NG * 512])
        gbias = sb(gru, "gbias", [P, NG * 512])
        w_hh = sb(gru, "w_hh", [P, C, 4, G3 * P])
        gates_in = sb(gru, "gates_in", [P, 2, CH, G3 * P])
        with ExitStack() as st:
            gbias2 = sb(st, "gbias2", [P, NG * 512])
            xt_first = sb(st, "xt_first", [P, FIRST, C, P])
            gi_first = sb(st, "gi_first", [P, 2, NG * 512])
            ld_const = sem("ld_const")
            ld_wih = [sem(f"ld_wih{c}") for c in range(C)]
            ld_bias = sem("ld_bias")
            ld_first = sem("ld_first")
            ld_gru = sem("ld_gru")
            bias_ready = sem("bias_ready")
            first_mm = sem("first_mm")
            first_added = sem("first_added")
            first_stored = [sem("first_stored0"), sem("first_stored1")]
            with nc.Block() as block:
                @block.sync
                def _(sp):
                    for c in range(C):
                        sp.dma_start(w_ih[:, c], a["w_ih"][:, c]).then_inc(ld_wih[c], 16)
                        if c == 0:
                            sp.dma_start(xt_first[:], x_t[0:FIRST].rearrange("i p c n -> p i c n")
                                         ).then_inc(ld_first, 16)
                    sp.dma_start(ident[:], a["ident"]).then_inc(ld_const, 16)
                    sp.dma_start(gbias[:], a["b_ih"].to_broadcast([P, NG * 512])).then_inc(ld_bias, 16)
                    sp.dma_start(gbias2[:], a["b_hh"].to_broadcast([P, NG * 512])).then_inc(ld_bias, 16)
                    sp.dma_start(w_hh[:], a["w_hh"]).then_inc(ld_gru, 16)
                    sp.wait_ge(ld_const, 16)
                    for i in range(FIRST):
                        sp.wait_ge(first_added, i + 1)
                        sp.dma_start(gi_tiles[i], gi_first[:, i % 2]).then_inc(first_stored[i % 2], 16)
                    for u in range(2):
                        sp.wait_ge(first_stored[u], 16 * (FIRST // 2))

                @block.gpsimd
                def _(pool):
                    pool.memset(ones[:], 1.0)
                    pool.memset(minus_half[:], -0.5)
                    pool.memset(gates_in[:], 0.0)

                @block.tensor
                def _(pe):
                    pe.wait_ge(ld_first, 16)
                    for i in range(FIRST):
                        if i >= 2:
                            pe.wait_ge(first_added, i - 1)
                        for c in range(C):
                            if i == 0:
                                pe.wait_ge(ld_wih[c], 16)
                            for n in range(NG):
                                mm = pe.matmul(bank[3 * (i % 2) + n][:], xt_first[:, i, c], w_ih[:, c, n * 512:n * 512 + 512],
                                               start=(c == 0), stop=(c == C - 1))
                        mm.then_inc(first_mm, 1)

                @block.vector
                def _(dve):
                    dve.wait_ge(ld_bias, 32)
                    gb = gbias[:].rearrange("p (j g n) -> p j g n", j=4, g=G3)
                    gb2 = gbias2[:].rearrange("p (j g n) -> p j g n", j=4, g=G3)
                    for g in range(2):
                        dve.tensor_tensor(gb[:, :, g], gb[:, :, g], gb2[:, :, g], ALU.add).then_inc(bias_ready, 1)
                    dve.wait_ge(bias_ready, 2)
                    for i in range(FIRST):
                        dve.wait_ge(first_mm, i + 1)
                        if i >= 2:
                            dve.wait_ge(first_stored[i % 2], 16 * (i // 2))
                        for n in range(NG):
                            add = dve.tensor_tensor(gi_first[:, i % 2, n * 512:n * 512 + 512], bank[3 * (i % 2) + n][:],
                                                    gbias[:, n * 512:n * 512 + 512], ALU.add)
                        add.then_inc(first_added, 1)

        with gru as st:
            xt_in = sb(st, "xt_in", [P, C, P])
            gi_out = sb(st, "gi_out", [P, 512])
            fold_in = sb(st, "fold_in", [P, QL + KL + DV + D])
            wqk_out = sb(st, "wqk_out", [P, 2, QC * P], F32R)
            raw = sb(st, "raw", [P, 3, TW])
            b_hn = sb(st, "b_hn", [P, P])
            n_gate = sb(st, "n_gate", [P, 2, P])
            h = sb(st, "h", [P, P])
            h_t = sb(st, "h_t", [P, P])
            r = sb(st, "r", [P, P])
            z = sb(st, "z", [P, P])
            n = sb(st, "n", [P, P])
            rh = sb(st, "rh", [P, P])
            n_in = sb(st, "n_in", [P, P])
            zh = sb(st, "zh", [P, P])
            zn = sb(st, "zn", [P, P])
            bank_rn, bank_z, bank_gi, bank_qk, bank_vo = bank[0], bank[1], bank[2], bank[3], bank[4]
            HALVES = (slice(0, P // 2), slice(P // 2, P))
            ld_gates = sem("ld_gates")
            rn_mm, z_mm = sem("rn_mm"), sem("z_mm")
            r_sig, z_sig = sem("r_sig"), sem("z_sig")
            n_tanh = sem("n_tanh")
            n_staged = sem("n_staged")
            rh_done, nin_done = sem("rh_done"), sem("nin_done")
            zh_done = sem("zh_done")
            zn_done = [sem("zn_done0"), sem("zn_done1")]
            h_done = [sem("h_done0"), sem("h_done1")]
            ht_done = [sem("ht_done0"), sem("ht_done1")]
            hist_done = sem("hist_done")
            ld_xt = sem("ld_xt")
            gi_mm = sem("gi_mm")
            gi_added = sem("gi_added")
            gi_stored = sem("gi_stored")
            ld_fold = sem("ld_fold")
            qk_mm = sem("qk_mm")
            vo_mm = sem("vo_mm")
            qk_high = sem("qk_high")
            qk_out = sem("qk_out")
            vo_out = sem("vo_out")
            qk_stored = sem("qk_stored")
            ld_raw = sem("ld_raw")
            abs_done = sem("abs_done")
            NC = T // CH
            FOLD0 = GI_BODIES
            LAST0 = FOLD0 + FOLD_BODIES
            with nc.Block() as block:
                @block.sync
                def _(sp):
                    sp.dma_start(b_hn[:], a["b_hn"]).then_inc(ld_gru, 16)
                    sp.dma_start(h[:], a["h0"]).then_inc(ld_gru, 16)
                    sp.dma_start(gi_out[:, 0:1], a["zero_col"]).then_inc(gi_stored, 16)
                    sp.dma_start(wqk_out[:, 0, 0:1].bitcast(F32), a["zero_col"]).then_inc(qk_stored, 16)

                    def load_chunk(k):
                        for j in range(4):
                            sp.dma_start(gates_in[32 * j:32 * j + B, k % 2],
                                         gi_scratch[k // (TS // CH), :, bass.ds((k % (TS // CH)) * CH, CH),
                                                    j * G3 * P:(j + 1) * G3 * P]).then_inc(ld_gates, 16)

                    def load_raw(i):
                        sp.dma_start(raw[:], a["ffn"][:, :, bass.ds(i * TW, TW)].rearrange("w p n -> p w n")
                                     ).then_inc(ld_raw, 16)

                    def common(i):
                        sp.wait_ge(abs_done, i + 1)
                        load_raw(i + 1)

                    def next_chunk(k):
                        sp.wait_ge(ld_gates, k * 64 + 128)
                        sp.wait_ge(nin_done, k * CH + CH + 1)
                        load_chunk(k + 2)

                    def gi_body(i):
                        common(i)
                        sp.wait_ge(gi_added, i + 2)
                        sp.dma_start(gi_tiles[FIRST + i // NG, :, bass.ds((i % NG) * 512, 512)], gi_out[:]
                                     ).then_inc(gi_stored, 16)
                        sp.wait_ge(gi_stored, i * 16 + 32)

                    load_chunk(0)
                    sp.wait_ge(ld_gates, 64)
                    load_chunk(1)
                    load_raw(0)
                    sp.dma_start(xt_in[:], x_t[FIRST]).then_inc(ld_xt, 16)
                    sp.dma_start(fold_in[:], a["fold"][0]).then_inc(ld_fold, 16)
                    with sp.Fori(0, GI_BODIES // (2 * NG)) as m:
                        for v in range(2 * NG):
                            gi_body(m * 2 * NG + v)
                            if v == NG - 1:
                                sp.dma_start(xt_in[:], x_t[FIRST + 1 + m * 2]).then_inc(ld_xt, 16)
                            if v == 2 * NG - 1:
                                sp.dma_start(xt_in[:], x_t[(m * 2 + FIRST + 2) % TILES]).then_inc(ld_xt, 16)
                            if v % 2 == 1:
                                next_chunk(m * NG + v // 2)

                    def fold_body(head):
                        i = head + FOLD0
                        common(i)
                        sp.wait_ge(qk_out, head + 2)
                        sp.dma_start(wqk_scratch[head], wqk_out[:].bitcast(F32).rearrange("p i n -> p (i n)")).then_inc(qk_stored, 16)
                        sp.wait_ge(vo_mm, head + 1)
                        sp.dma_start(fold_in[:], a["fold"][(head + 1) % NH]).then_inc(ld_fold, 16)

                    with sp.Fori(0, FOLD_BODIES // 2) as m:
                        for v in range(2):
                            fold_body(m * 2 + v)
                        next_chunk(m + FOLD0 // 2)
                    with sp.Fori(0, (BODIES - LAST0) // 2 - 2) as m:
                        for v in range(2):
                            common(m * 2 + v + LAST0)
                        next_chunk(m + LAST0 // 2)
                    for i in range(BODIES - 4, BODIES - 1):
                        common(i)
                    sp.wait_ge(ld_xt, 16 * (GI_BODIES // NG + 1))
                    sp.wait_ge(ld_fold, 16 * (NH + 1))
                    sp.wait_ge(ld_raw, 16 * BODIES)
                    sp.wait_ge(qk_stored, 16 * (NH + 1))
                    sp.wait_ge(ld_gates, 64 * NC)

                @block.gpsimd
                def _(pool):
                    ring = gates_in[:].rearrange("p k t n -> p (k t) n")
                    pool.wait_ge(ld_gates, 64)
                    for v in range(2):
                        pool.tensor_copy(n_gate[:, v, :], ring[:, v, 2 * P:]).then_inc(n_staged, 1)
                    with pool.Fori(0, T // 2 - 1) as i:
                        for v in range(2):
                            pool.wait_ge(ld_gates, ((i * 2 + v + 2) // CH) * 64 + 64)
                            pool.wait_ge(nin_done, i * 2 + v + 2)
                            pool.tensor_copy(n_gate[:, v, :], ring[:, (i * 2 + v + 2) % (2 * CH), 2 * P:]
                                             ).then_inc(n_staged, 1)

                @block.tensor
                def _(pe):
                    def step(i, v):
                        now = i * U + v + 1
                        if v == 0:
                            pe.wait_ge(ld_gates, (i // (CH // U)) * 64 + 64)
                        gates = gates_in[:].rearrange("p k (s u) n -> p (k s) u n", u=U)[:, i % (2 * CH // U), v]
                        pe.wait_ge(rh_done, now)
                        pe.matmul(bank_rn[:, 0:P], ident[:], gates[:, 0:P], start=True, stop=False,
                                  skip_group_check=True)
                        pe.matmul(bank_rn[:, P:2 * P], ident[:], b_hn[:], start=False, stop=False,
                                  skip_group_check=True)
                        pe.wait_ge(z_sig, now)
                        pe.matmul(bank_z[:, 0:P], ident[:], gates[:, P:2 * P], start=True, stop=False,
                                  skip_group_check=True)
                        for c in range(C):
                            if c % 2 == 0:
                                pe.wait_ge(ht_done[c // 2], now)
                            for j in range(4):
                                mm = pe.matmul(bank_rn[32 * j:32 * j + B, 0:2 * P], h_t[:, 32 * c:32 * c + B],
                                               w_hh[:, c, j, 0:2 * P], start=False, stop=(c == C - 1),
                                               skip_group_check=True)
                        mm.then_inc(rn_mm, 1)
                        for c in range(C):
                            for j in range(4):
                                mm = pe.matmul(bank_z[32 * j:32 * j + B, 0:P], h_t[:, 32 * c:32 * c + B],
                                               w_hh[:, c, j, 2 * P:], start=False, stop=(c == C - 1),
                                               skip_group_check=True)
                        mm.then_inc(z_mm, 1)

                    pe.wait_ge(ld_gru, 48)
                    with pe.Fori(0, GI_BODIES) as i:
                        for v in range(U):
                            step(i, v)
                            if v == 2:
                                pe.wait_ge(ld_xt, (i // NG) * 16 + 16)
                                pe.wait_ge(gi_added, i + 1)
                            if 2 <= v < 2 + C:
                                c = v - 2
                                mm = pe.matmul(bank_gi[:], xt_in[:, c], w_ih[:, c, bass.ds((i % NG) * 512, 512)],
                                               start=(c == 0), stop=(c == C - 1))
                                if c == C - 1:
                                    mm.then_inc(gi_mm, 1)
                    with pe.Fori(0, FOLD_BODIES) as head:
                        for v in range(U):
                            step(head + FOLD0, v)
                            if v == 2:
                                pe.wait_ge(ld_fold, head * 16 + 16)
                                pe.wait_ge(qk_out, head + 1)
                                for m in range(QC):
                                    mm = pe.matmul(bank_qk[:, m * P:m * P + P], fold_in[:, m * P:m * P + P],
                                                   fold_in[:, QL:QL + KL], start=True, stop=True)
                                mm.then_inc(qk_mm, 1)
                            if v == 3:
                                pe.wait_ge(vo_out, head + 1)
                                pe.matmul(bank_vo[:], fold_in[:, QL + KL:QL + KL + DV], fold_in[:, QL + KL + DV:],
                                          start=True, stop=True).then_inc(vo_mm, 1)
                    with pe.Fori(LAST0, BODIES) as i:
                        for v in range(U):
                            step(i, v)

                @block.scalar
                def _(act):
                    act.wait_ge(ld_gru, 48)
                    act.activation(r[:], b_hn[:], ACT.Sigmoid).then_inc(r_sig, 1)
                    act.activation(z[:], b_hn[:], ACT.Sigmoid).then_inc(z_sig, 1)
                    act.activation(n[:], b_hn[:], ACT.Tanh).then_inc(hist_done, 1)
                    act.wait_ge(r_sig, 1)
                    act.wait_ge(z_sig, 1)
                    act.wait_ge(hist_done, 1)
                    with act.Fori(0, BODIES) as i:
                        for v in range(U):
                            t = i * U + v
                            act.wait_ge(rn_mm, t + 1)
                            act.activation(r[:], bank_rn[:, 0:P], ACT.Sigmoid).then_inc(r_sig, 1)
                            act.wait_ge(z_mm, t + 1)
                            act.activation(z[:], bank_z[:, 0:P], ACT.Sigmoid).then_inc(z_sig, 1)
                            act.wait_ge(nin_done, t + 2)
                            act.activation(n[:], n_in[:], ACT.Tanh).then_inc(n_tanh, 1)
                            act.wait_ge(ht_done[1], t + 2)
                            act.activation(hist[:, :, :, t].rearrange("p b c -> p c b"),
                                           h_t[:].rearrange("p (c q) -> p c q", c=C)[:, :, 0:B],
                                           ACT.Copy).then_inc(hist_done, 1)

                @block.vector
                def _(dve):
                    def step(i, v):
                        t = i * U + v
                        dve.wait_ge(r_sig, t + 2)
                        dve.tensor_tensor(rh[:], r[:], bank_rn[:, P:2 * P], ALU.mult).then_inc(rh_done, 1)
                        dve.wait_ge(n_staged, t + 1)
                        dve.wait_ge(rh_done, t + 2)
                        dve.tensor_tensor(n_in[:], rh[:], n_gate[:, v % 2, :], ALU.add).then_inc(nin_done, 1)
                        dve.wait_ge(z_sig, t + 2)
                        dve.tensor_tensor(zh[:], z[:], h[:], ALU.mult).then_inc(zh_done, 1)
                        dve.wait_ge(n_tanh, t + 1)
                        for q, half in enumerate(HALVES):
                            dve.scalar_tensor_tensor(zn[:, half], z[:, half], 1.0, n[:, half], ALU.subtract,
                                                     ALU.mult).then_inc(zn_done[q], 1)
                            if q == 0:
                                dve.wait_ge(zh_done, t + 1)
                            dve.wait_ge(zn_done[q], t + 1)
                            dve.tensor_tensor(h[:, half], zh[:, half], zn[:, half], ALU.subtract
                                              ).then_inc(h_done[q], 1)
                            if q == 0:
                                dve.wait_ge(hist_done, t + 1)
                            dve.wait_ge(h_done[q], t + 1)
                            dve.transpose(h_t[:, half], h[:, half]).then_inc(ht_done[q], 1)
                        if v == 0:
                            dve.wait_ge(ld_raw, i * 16 + 16)
                            dve.tensor_reduce(abs_part[:, i, :], raw[:], AX_X, ALU.add, apply_absolute_value=True
                                              ).then_inc(abs_done, 1)

                    dve.wait_ge(ld_gru, 48)
                    dve.memset(n_in[:], 0.0).then_inc(nin_done, 1)
                    dve.memset(rh[:], 0.0).then_inc(rh_done, 1)
                    dve.memset(zh[:], 0.0).then_inc(gi_added, 1)
                    dve.memset(zn[:], 0.0).then_inc(qk_out, 1)
                    dve.memset(wvo[:, 0, 0:1], 0.0).then_inc(vo_out, 1)
                    for q, half in enumerate(HALVES):
                        dve.transpose(h_t[:, half], h[:, half]).then_inc(ht_done[q], 1)
                    for stand_in in (nin_done, rh_done, gi_added, qk_out, vo_out):
                        dve.wait_ge(stand_in, 1)
                    with dve.Fori(0, GI_BODIES) as i:
                        for v in range(U):
                            step(i, v)
                            if v == 6:
                                dve.wait_ge(gi_mm, i + 1)
                                dve.wait_ge(gi_stored, i * 16 + 16)
                                dve.tensor_tensor(gi_out[:], bank_gi[:], gbias[:, bass.ds((i % NG) * 512, 512)], ALU.add
                                                  ).then_inc(gi_added, 1)
                    with dve.Fori(0, FOLD_BODIES) as head:
                        for v in range(U):
                            step(head + FOLD0, v)
                            if v == 4:
                                dve.wait_ge(qk_mm, head + 1)
                                dve.wait_ge(qk_stored, head * 16 + 16)
                                dve.tensor_copy(wqk_out[:, 0], bank_qk[:, 0:QL]).then_inc(qk_high, 1)
                                dve.wait_ge(qk_high, head + 1)
                                dve.tensor_tensor(wqk_out[:, 1], bank_qk[:, 0:QL], wqk_out[:, 0].bitcast(F32),
                                                  ALU.subtract).then_inc(qk_out, 1)
                            if v == 5:
                                dve.wait_ge(vo_mm, head + 1)
                                dve.tensor_copy(wvo[:, head], bank_vo[:]).then_inc(vo_out, 1)
                    with dve.Fori(LAST0, BODIES) as i:
                        for v in range(U):
                            step(i, v)

        with ExitStack() as st:
            w_qa = sb(st, "w_qa", [P, C, QL])
            w_kva = sb(st, "w_kva", [P, C, 2 * P])
            rope = sb(st, "rope", [P, T])
            dup = sb(st, "dup", [P, P])
            ident_bf = sb(st, "ident_bf", [P, P], BF16)
            causal = sb(st, "causal", [P, P], BF16)
            ln_q = sb(st, "ln_q", [P, QC])
            ln_kv = sb(st, "ln_kv", [P, 1])
            head_w = sb(st, "head_w", [P, 2, QL], F32R)
            rot_raw = sb(st, "rot_raw", [P, QL])
            rot_w = sb(st, "rot_w", [P, 2, QL], F32R)
            rope_q = sb(st, "rope_q", [P, 2, T])
            q_raw = sb(st, "q_raw", [P, QC, T])
            q_lat = sb(st, "q_lat", [P, QC, T])
            q_high = sb(st, "q_high", [P, QC, T], F32R)
            q_low = sb(st, "q_low", [P, QC, T], F32R)
            kv_raw = sb(st, "kv_raw", [P, T])
            kv_t = sb(st, "kv_t", [P, T])
            kv_rows = sb(st, "kv_rows", [P, NT, KL])
            k_rot = sb(st, "k_rot", [P, T])
            sq = sb(st, "sq", [P, QC + 1, T])
            rms = sb(st, "rms", [P, 2, NT])
            rms_diag = sb(st, "rms_diag", [P, 2, T])
            q_t = sb(st, "q_t", [P, T])
            q_rot = sb(st, "q_rot", [P, 2, T])
            prob = sb(st, "prob", [P, 10 * P])
            prob_t = sb(st, "prob_t", [P, 10 * P])
            negmax = sb(st, "negmax", [P, NT])
            psum_row = sb(st, "psum_row", [P, NT])
            pinv = sb(st, "pinv", [P, NT])
            o_t = sb(st, "o_t", [P, NH, T])
            raw_piece = sb(st, "raw_piece", [P, 3, TW])
            below = sb(st, "below", [P, 3, TW])
            tern_piece = sb(st, "tern_piece", [P, 3, TW], F32R)
            abs_sum = sb(st, "abs_sum", [P, 3])
            limits = sb(st, "limits", [P, 2, 3])
            ld_att = sem("ld_att")
            ld_head = sem("ld_head")
            ld_rot = sem("ld_rot")
            rot_high = sem("rot_high")
            rot_low = sem("rot_low")
            ld_x1 = sem("ld_x1")
            lat_mm = sem("lat_mm")
            raw_done = sem("raw_done")
            rotk = sem("rotk")
            sq_done = sem("sq_done")
            ss_mm = sem("ss_mm")
            diag_done = sem("diag_done")
            spread_mm = sem("spread_mm")
            rms_a = sem("rms_a")
            lnq_scaled = sem("lnq_scaled")
            rms_b = sem("rms_b")
            lat_done = sem("lat_done")
            lat_high = sem("lat_high")
            lat_low = sem("lat_low")
            kdup_mm = sem("kdup_mm")
            krot_done = sem("krot_done")
            kvr_mm = sem("kvr_mm")
            kvr_done = sem("kvr_done")
            proj_mm = sem("proj_mm")
            rot_mm = sem("rot_mm")
            qt_done = sem("qt_done")
            qrot_done = sem("qrot_done")
            s_mm = sem("s_mm")
            max_done = sem("max_done")
            exp_done = sem("exp_done")
            inv_done = sem("inv_done")
            norm_done = sem("norm_done")
            tr_mm = sem("tr_mm")
            ptA = sem("ptA")
            ptB = sem("ptB")
            pv_mm = sem("pv_mm")
            o_done = sem("o_done")
            y_mm = sem("y_mm")
            abs_total = sem("abs_total")
            abs_mm = sem("abs_mm")
            limit_step = sem("limit_step")
            ld_piece = sem("ld_piece")
            below_done = sem("below_done")
            tern_done = sem("tern_done")
            tern_stored = sem("tern_stored")
            y_done = sem("y_done")

            def score_out(q):
                return (bank[1][:, 3 * P:], bank[2][:, 0:2 * P], bank[1][:, 0:3 * P], bank[0][:])[q]

            def turn_out(k):
                return (bank[3][:], bank[5][:, 0:3 * P], bank[7][:, 0:2 * P], bank[5][:, 3 * P:])[k]

            y_bank = (0, 1, 2, 0)
            query_bank, rot_bank = (bank[6], bank[4]), bank[4]
            with nc.Block() as block:
                @block.sync
                def _(sp):
                    for dst, src in ((w_qa, "w_qa"), (w_kva, "w_kva"), (rope, "rope"), (rope_q, "rope_q"), (dup, "dup"),
                                     (ident_bf, "ident_bf"), (causal, "causal"), (ln_q, "ln_q"), (ln_kv, "ln_kv")):
                        sp.dma_start(dst[:], a[src]).then_inc(ld_att, 16)

                    def load_head(head):
                        sp.dma_start(head_w[:].bitcast(F32).rearrange("p i n -> p (i n)"), wqk_scratch[head]).then_inc(ld_head, 16)

                    def load_rot(pair):
                        sp.dma_start(rot_raw[:], a["w_rope"][pair]).then_inc(ld_rot, 16)

                    load_head(0)
                    load_rot(0)
                    with sp.Fori(0, B) as b:
                        sp.wait_ge(lat_mm, b * 5 + 5)
                        sp.dma_start(x1[:, b], x_rows[b]).then_inc(ld_x1, 16)
                        with sp.Fori(0, NH // 2) as pair:
                            sp.wait_ge(rot_low, b * (NH // 2) + pair + 1)
                            load_rot((pair + 1) % (NH // 2))
                            for v in range(2):
                                g = b * NH + pair * 2 + v
                                sp.wait_ge(proj_mm, g + 1)
                                load_head((pair * 2 + v + 1) % NH)
                    sp.wait_ge(ld_head, 16 * (B * NH + 1))
                    sp.wait_ge(ld_rot, 16 * (B * NH // 2 + 1))

                @block.tensor
                def _(pe):
                    def project(g, v):
                        pe.wait_ge(ld_head, g * 16 + 16)
                        for i, (part, lat) in enumerate(((0, q_high), (0, q_low), (1, q_high))):
                            for m in range(QC):
                                mm = pe.matmul(query_bank[v][:], head_w[:, part, m * P:m * P + P], lat[:, m, :],
                                               start=(i == 0 and m == 0), stop=(i == 2 and m == QC - 1))
                        mm.then_inc(proj_mm, 1)

                    def project_rot(pair):
                        pe.wait_ge(rot_low, pair + 1)
                        for i, (part, lat) in enumerate(((0, q_high), (0, q_low), (1, q_high))):
                            for m in range(QC):
                                mm = pe.matmul(rot_bank[:], rot_w[:, part, m * P:m * P + P], lat[:, m, :],
                                               start=(i == 0 and m == 0), stop=(i == 2 and m == QC - 1))
                        mm.then_inc(rot_mm, 1)

                    def scores(g, v):
                        pe.wait_ge(qt_done, g + 1)
                        pe.wait_ge(qrot_done, g + 2 - v)
                        for q in ORDER:
                            nk = (q + 1) * P
                            out = score_out(q)
                            pe.matmul(out, q_t[:, q * P:q * P + P], kv_t[:, 0:nk],
                                      start=True, stop=False, skip_group_check=True)
                            pe.matmul(out[:, q * P:nk], ident_bf[:], causal[:], start=False, stop=False,
                                      skip_group_check=True)
                            mm = pe.matmul(out, q_rot[:, v, q * P:q * P + P], k_rot[:, 0:nk],
                                           start=False, stop=True, skip_group_check=True)
                            if q != 0:
                                mm.then_inc(s_mm, 2 if q == 2 else 1)

                    def turn(g):
                        for i, q in enumerate(ORDER):
                            pe.wait_ge(norm_done, g * NT + i + 1)
                            for k in range(q + 1):
                                tr = pe.transpose(turn_out(k)[:, (q - k) * P:(q - k + 1) * P],
                                                  prob[:, KEY0[q] + k * P:KEY0[q] + k * P + P], ident[:])
                        tr.then_inc(tr_mm, 1)

                    def values(g):
                        pe.wait_ge(ptA, g * 2 + 1)
                        for i, k in enumerate((0, 1, 3, 2)):
                            if i == 1:
                                pe.wait_ge(ptB, g + 1)
                            if i == 3:
                                pe.wait_ge(ptA, g * 2 + 2)
                            mm = pe.matmul(bank[6][:, k * P:], kv_rows[:, k, :], prob_t[:, PT0[k]:PT0[k] + (NT - k) * P],
                                           start=(i == 0), stop=(i == NT - 1), skip_group_check=True)
                        mm.then_inc(pv_mm, 1)

                    pe.wait_ge(abs_total, 1)
                    pe.matmul(bank[7][:, 0:3], ones[:], abs_sum[:], start=True, stop=True).then_inc(abs_mm, 1)
                    pe.wait_ge(ld_att, 16 * 9)
                    pe.wait_ge(limit_step, 1)

                    def latents(b):
                        for m in range(QC):
                            for c in range(C):
                                mm = pe.matmul(bank[m][:], w_qa[:, c, m * P:m * P + P], hist[:, b, c, :],
                                               start=(c == 0), stop=(c == C - 1))
                            mm.then_inc(lat_mm, 1)
                        for m in range(2):
                            for c in range(C):
                                mm = pe.matmul(bank[3 + m][:], w_kva[:, c, m * P:m * P + P], hist[:, b, c, :],
                                               start=(c == 0), stop=(c == C - 1))
                            mm.then_inc(lat_mm, 1)
                        pe.wait_ge(sq_done, b * 4 + 4)
                        for i, ms in enumerate((range(QC), range(QC, QC + 1))):
                            for q in range(NT):
                                for m in ms:
                                    mm = pe.matmul(bank[5 + i][:, q:q + 1], sq[:, m, q * P:q * P + P], ones[:, 0:1],
                                                   start=(m == ms[0]), stop=(m == ms[-1]))
                            mm.then_inc(ss_mm, 1)
                        pe.wait_ge(rotk, b + 1)
                        pe.matmul(bank[4][:], dup[:], k_rot[:], start=True, stop=True).then_inc(kdup_mm, 1)

                    def spread(b):
                        for i in range(2):
                            pe.wait_ge(diag_done, b * 2 + i + 1)
                            pe.matmul(bank[6 + i][:], ones[:], rms_diag[:, i, :], start=True, stop=True
                                      ).then_inc(spread_mm, 1)

                    def value_rows(b):
                        pe.wait_ge(lat_done, b * 4 + 4)
                        for k in range(NT):
                            tr = pe.transpose(bank[3][:, k * P:k * P + P], kv_t[:, k * P:k * P + P], ident[:])
                        tr.then_inc(kvr_mm, 1)

                    def first_queries(b):
                        pe.wait_ge(krot_done, b + 1)
                        pe.wait_ge(lat_low, b * QC + QC)
                        project(b * NH, 0)
                        project_rot(b * (NH // 2))

                    def heads(b):
                        pe.wait_ge(kvr_done, b + 1)
                        scores(b * NH, 0)
                        with pe.Fori(0, NH // 2 - 1) as pair:
                            for v in range(2):
                                g = b * NH + pair * 2 + v
                                if v == 1:
                                    project_rot(b * (NH // 2) + pair + 1)
                                    pe.wait_ge(o_done, g)
                                project(g + 1, (v + 1) % 2)
                                turn(g)
                                scores(g + 1, (v + 1) % 2)
                                values(g)
                        g = b * NH + NH - 2
                        project(g + 1, 1)
                        turn(g)
                        scores(g + 1, 1)
                        values(g)
                        turn(g + 1)
                        values(g + 1)

                    def out_rows(b, q):
                        if q == 0:
                            pe.wait_ge(o_done, b * NH + NH)
                        if q == NT - 1:
                            pe.wait_ge(y_done, b * NT + 1)
                        for hd in range(NH):
                            mm = pe.matmul(bank[y_bank[q]][:], o_t[:, hd, q * P:q * P + P], wvo[:, hd, :],
                                           start=(hd == 0), stop=(hd == NH - 1))
                        mm.then_inc(y_mm, 1)

                    latents(0)
                    spread(0)
                    value_rows(0)
                    first_queries(0)
                    with pe.Fori(0, B - 1) as b:
                        heads(b)
                        latents(b + 1)
                        out_rows(b, 0)
                        spread(b + 1)
                        out_rows(b, 1)
                        value_rows(b + 1)
                        out_rows(b, 2)
                        first_queries(b + 1)
                        out_rows(b, 3)
                        pe.wait_ge(y_done, b * NT + NT)
                    heads(B - 1)
                    for q in range(NT):
                        out_rows(B - 1, q)

                @block.gpsimd
                def _(pool):
                    def load_piece(i):
                        pool.dma_start(raw_piece[:], a["ffn"][:, :, bass.ds(i * TW, TW)].rearrange("w p n -> p w n")
                                       ).then_inc(ld_piece, 16)

                    load_piece(0)
                    pool.dma_start(below[:, 0, 0:1], a["zero_col"]).then_inc(tern_stored, 16)
                    with pool.Fori(0, B) as b:
                        pool.wait_ge(rms_a, b * 2 + 2)
                        flat = rms[:].rearrange("p i q -> p (i q)")
                        pool.tensor_tensor(flat, flat, minus_half[:, 0:1].to_broadcast([P, 2 * NT]), ALU.pow
                                           ).then_inc(rms_b, 1)
                        with pool.Fori(0, NH) as hd:
                            g = b * NH + hd
                            pool.wait_ge(tern_done, g + 1)
                            pool.dma_start(tern_scratch[:, :, bass.ds(g * TW, TW)].rearrange("w p n -> p w n"),
                                           tern_piece[:].bitcast(F32)).then_inc(tern_stored, 16)
                            load_piece((g + 1) % (B * NH))
                    pool.wait_ge(ld_piece, 16 * (B * NH + 1))
                    pool.wait_ge(tern_stored, 16 * (B * NH + 1))

                @block.scalar
                def _(act):
                    def head(g):
                        for i, q in enumerate(ORDER):
                            nk = (q + 1) * P
                            act.wait_ge(max_done, g * NT + (3 if q == 0 else i + 1))
                            act.activation(prob[:, KEY0[q]:KEY0[q] + nk], score_out(q), ACT.Exp,
                                           bias=negmax[:, q:q + 1], scale=1.0,
                                           accum_out=psum_row[:, q:q + 1]).then_inc(exp_done, 1)

                    def split_rot(pair):
                        act.wait_ge(ld_rot, pair * 16 + 16)
                        act.activation(rot_w[:, 0], rot_raw[:], ACT.Copy).then_inc(rot_high, 1)

                    def copy_q(g, v):
                        act.wait_ge(proj_mm, g + 1)
                        act.activation(q_t[:], query_bank[v][:], ACT.Copy).then_inc(qt_done, 1)

                    def turned(g):
                        act.wait_ge(tr_mm, g + 1)
                        for k in (0, 2):
                            act.activation(prob_t[:, PT0[k]:PT0[k] + (NT - k) * P], turn_out(k), ACT.Copy
                                           ).then_inc(ptA, 1)

                    def keep_o(g, hd):
                        act.wait_ge(pv_mm, g + 1)
                        act.activation(o_t[:, hd, :], bank[6][:], ACT.Copy).then_inc(o_done, 1)

                    split_rot(0)
                    with act.Fori(0, B) as b:
                        for m in range(QC):
                            act.wait_ge(raw_done, b * 4 + m + 1)
                            act.activation(sq[:, m, :], q_raw[:, m, :], ACT.Square).then_inc(sq_done, 1)
                        act.wait_ge(raw_done, b * 4 + 4)
                        act.activation(sq[:, QC, :], kv_raw[:], ACT.Square).then_inc(sq_done, 1)
                        act.wait_ge(kdup_mm, b + 1)
                        act.activation(k_rot[:], bank[4][:], ACT.Copy).then_inc(krot_done, 1)
                        act.wait_ge(kvr_mm, b + 1)
                        act.activation(kv_rows[:].rearrange("p k n -> p (k n)"), bank[3][:], ACT.Copy
                                       ).then_inc(kvr_done, 1)
                        copy_q(b * NH, 0)
                        act.wait_ge(rot_mm, b * (NH // 2) + 1)
                        split_rot(b * (NH // 2) + 1)
                        head(b * NH)
                        with act.Fori(0, NH // 2 - 1) as pair:
                            for v in range(2):
                                g = b * NH + pair * 2 + v
                                copy_q(g + 1, (v + 1) % 2)
                                turned(g)
                                if v == 1:
                                    split_rot(b * (NH // 2) + pair + 2)
                                head(g + 1)
                                keep_o(g, pair * 2 + v)
                        g = b * NH + NH - 2
                        copy_q(g + 1, 1)
                        turned(g)
                        head(g + 1)
                        keep_o(g, NH - 2)
                        turned(g + 1)
                        keep_o(g + 1, NH - 1)

                @block.vector
                def _(dve):
                    def head(g):
                        def normalise(i):
                            q = ORDER[i]
                            nk = (q + 1) * P
                            dve.wait_ge(exp_done, g * NT + i + 1)
                            dve.reciprocal(pinv[:, q:q + 1], psum_row[:, q:q + 1]).then_inc(inv_done, 1)
                            dve.wait_ge(inv_done, g * NT + i + 1)
                            dve.tensor_scalar(prob[:, KEY0[q]:KEY0[q] + nk], prob[:, KEY0[q]:KEY0[q] + nk],
                                              pinv[:, q:q + 1], None, ALU.mult).then_inc(norm_done, 1)

                        for i, q in enumerate(ORDER):
                            dve.wait_ge(s_mm, g * NT + i + 1)
                            dve.tensor_reduce(negmax[:, q:q + 1], score_out(q), AX_X, ALU.max,
                                              negate=True).then_inc(max_done, 1)
                            if i > 1:
                                normalise(i - 2)
                        normalise(NT - 2)
                        normalise(NT - 1)

                    def turned(g):
                        dve.wait_ge(tr_mm, g + 1)
                        dve.tensor_copy(prob_t[:, PT0[1]:PT0[1] + NT * P], bank[5][:]).then_inc(ptB, 1)

                    def split_rot(pair):
                        dve.wait_ge(rot_high, pair + 1)
                        dve.tensor_tensor(rot_w[:, 1], rot_raw[:], rot_w[:, 0].bitcast(F32), ALU.subtract
                                          ).then_inc(rot_low, 1)

                    def rotate_q(pair):
                        dve.wait_ge(rot_mm, pair + 1)
                        for v in range(2):
                            rows = slice(v * DR, v * DR + DR)
                            for i in range(2):
                                mul = dve.tensor_tensor(q_rot[i * DR:i * DR + DR, v, :], rot_bank[rows, :],
                                                        rope_q[rows, i, :], ALU.mult)
                            mul.then_inc(qrot_done, 1)

                    def ternary(g):
                        dve.wait_ge(ld_piece, g * 16 + 16)
                        for w in range(3):
                            ins = dve.tensor_scalar(below[:, w, :], raw_piece[:, w, :], limits[:, 1, w:w + 1], None,
                                                    ALU.is_lt)
                        ins.then_inc(below_done, 1)
                        dve.wait_ge(below_done, g + 1)
                        dve.wait_ge(tern_stored, g * 16 + 16)
                        for w in range(3):
                            ins = dve.scalar_tensor_tensor(tern_piece[:, w, :], raw_piece[:, w, :], limits[:, 0, w:w + 1],
                                                           below[:, w, :], ALU.is_gt, ALU.subtract)
                        ins.then_inc(tern_done, 1)

                    dve.tensor_reduce(abs_sum[:], abs_part[:].rearrange("p i w -> p w i"), AX_X, ALU.add
                                      ).then_inc(abs_total, 1)
                    dve.wait_ge(abs_mm, 1)
                    dve.tensor_scalar(w_scale[:], bank[7][:, 0:3], 1.0 / (D * F), TERN_EPS, ALU.mult, ALU.add
                                      ).then_inc(limit_step, 1)
                    dve.wait_ge(limit_step, 1)
                    dve.wait_ge(tern_stored, 16)
                    for i, factor in enumerate((0.5, -0.5)):
                        dve.tensor_scalar(limits[:, i, :], w_scale[:], factor, None, ALU.mult).then_inc(limit_step, 1)
                    dve.wait_ge(limit_step, 3)
                    dve.wait_ge(ld_att, 16 * 9)
                    dve.tensor_scalar(ln_q[:], ln_q[:], QSCALE, None, ALU.mult).then_inc(lnq_scaled, 1)
                    dve.wait_ge(lnq_scaled, 1)

                    def factors(b):
                        for m in range(QC):
                            dve.wait_ge(lat_mm, b * 5 + m + 1)
                            dve.tensor_copy(q_raw[:, m, :], bank[m][:]).then_inc(raw_done, 1)
                        dve.wait_ge(lat_mm, b * 5 + 4)
                        dve.tensor_copy(kv_raw[:], bank[3][:]).then_inc(raw_done, 1)
                        dve.wait_ge(lat_mm, b * 5 + 5)
                        dve.tensor_tensor(k_rot[:], bank[4][:], rope[:], ALU.mult).then_inc(rotk, 1)
                        for i, width in enumerate((QL, KL)):
                            dve.wait_ge(ss_mm, b * 2 + i + 1)
                            dve.tensor_scalar(rms[:, i], bank[5 + i][:, 0:NT], 1.0 / width, RMS_EPS, ALU.mult, ALU.add
                                              ).then_inc(rms_a, 1)
                        dve.wait_ge(rms_b, b + 1)
                        for i in range(2):
                            for q in range(NT):
                                diag = dve.tensor_scalar(rms_diag[:, i, q * P:q * P + P], ident[:], rms[:, i, q:q + 1],
                                                         None, ALU.mult)
                            diag.then_inc(diag_done, 1)

                    def scale_latents(b):
                        dve.wait_ge(spread_mm, b * 2 + 2)
                        dve.scalar_tensor_tensor(kv_t[:], kv_raw[:], ln_kv[:, 0:1], bank[7][:], ALU.mult, ALU.mult
                                                 ).then_inc(lat_done, 1)
                        for m in range(QC):
                            dve.scalar_tensor_tensor(q_lat[:, m, :], q_raw[:, m, :], ln_q[:, m:m + 1], bank[6][:],
                                                     ALU.mult, ALU.mult).then_inc(lat_done, 1)
                        for m in range(QC):
                            dve.wait_ge(lat_done, b * 4 + m + 2)
                            dve.tensor_copy(q_high[:, m, :], q_lat[:, m, :]).then_inc(lat_high, 1)
                        for m in range(QC):
                            dve.wait_ge(lat_high, b * QC + m + 1)
                            dve.tensor_tensor(q_low[:, m, :], q_lat[:, m, :], q_high[:, m, :].bitcast(F32),
                                              ALU.subtract).then_inc(lat_low, 1)

                    def heads(b):
                        split_rot(b * (NH // 2) + 1)
                        head(b * NH)
                        with dve.Fori(0, NH // 2 - 1) as pair:
                            for v in range(2):
                                g = b * NH + pair * 2 + v
                                if v == 1:
                                    rotate_q(b * (NH // 2) + pair + 1)
                                turned(g)
                                head(g + 1)
                                if v == 1:
                                    split_rot(b * (NH // 2) + pair + 2)
                                ternary(g)
                        g = b * NH + NH - 2
                        turned(g)
                        head(g + 1)
                        ternary(g)
                        turned(g + 1)
                        ternary(g + 1)

                    def add_rows(b, q):
                        if q == 0:
                            dve.wait_ge(ld_x1, b * 16 + 16)
                        dve.wait_ge(y_mm, b * NT + q + 1)
                        dve.tensor_tensor(x1[:, b, q, :], bank[y_bank[q]][:], x1[:, b, q, :], ALU.add
                                          ).then_inc(y_done, 1)

                    factors(0)
                    scale_latents(0)
                    split_rot(0)
                    rotate_q(0)
                    with dve.Fori(0, B - 1) as b:
                        heads(b)
                        factors(b + 1)
                        add_rows(b, 0)
                        scale_latents(b + 1)
                        add_rows(b, 1)
                        add_rows(b, 2)
                        rotate_q((b + 1) * (NH // 2))
                        add_rows(b, 3)
                    heads(B - 1)
                    for q in range(NT):
                        add_rows(B - 1, q)

        att_weights.close()

        tern = [sb(ctx, f"tern_{w}", [P, 4 * F], F32R) for w in ("up", "gate", "down")]
        shift = sb(ctx, "shift", [P, B, D])
        gamma_t = sb(ctx, "gamma_t", [P, C])
        beta_t = sb(ctx, "beta_t", [P, C])
        NB = B * NBLK
        with ExitStack() as st:
            wk_t = sb(st, "wk_t", [P, C, D])
            wo_t = sb(st, "wo_t", [P, C, D])
            block_sel = sb(st, "block_sel", [P, B * NT, NB])
            batch_mask = sb(st, "batch_mask", [NB, B])
            batch_row = sb(st, "batch_row", [B, B * P])
            key_w = sb(st, "key_w", [NB, D])
            query = sb(st, "query", [NB, D])
            blocks_t = sb(st, "blocks_t", [P, C, NB])
            blocks = sb(st, "blocks", [NB, D])
            keys = sb(st, "keys", [NB, D])
            junk = sb(st, "junk", [NB, D])
            stat = sb(st, "stat", [NB, 8])
            row = sb(st, "row", [1, 3, NB])
            rowb = sb(st, "rowb", [1, 3, B])
            pick = sb(st, "pick", [NB, B])
            mix_t = sb(st, "mix_t", [P, C * B])
            proj = sb(st, "proj", [B, D])
            ld_c2 = sem("ld_c2")
            ld_sel = sem("ld_sel")
            ld_tern = [sem(f"ld_tern{i}") for i in range(4)]
            pe_step = sem("pe_step")
            dve_step = sem("dve_step")
            act_step = sem("act_step")
            pool_step = sem("pool_step")
            with nc.Block() as block:
                @block.sync
                def _(sp):
                    sp.dma_start(block_sel[:], a["block_sel"]).then_inc(ld_sel, 16)
                    for dst, src in ((wk_t[:], a["wk_t"]), (wo_t[:], a["wo_t"]),
                                     (batch_mask[:], a["batch_mask"]), (batch_row[:], a["batch_row"]),
                                     (key_w[:], a["key_w"].to_broadcast([NB, D])),
                                     (query[:], a["query"].to_broadcast([NB, D])),
                                     (gamma_t[:], a["gamma_t"]), (beta_t[:], a["beta_t"])):
                        sp.dma_start(dst, src).then_inc(ld_c2, 16)
                    for i in range(4):
                        for w in range(2):
                            sp.dma_start(tern[w][:].bitcast(F32).rearrange("p (c e) -> p c e", c=C)[:, :, i * 512:i * 512 + 512],
                                         tern_scratch[w].rearrange("p (c e) -> p c e", c=C)[:, :, i * 512:i * 512 + 512]
                                         ).then_inc(ld_tern[i], 16)
                        sp.dma_start(tern[2][:, i * F:(i + 1) * F].bitcast(F32), tern_scratch[2][:, i * F:(i + 1) * F]
                                     ).then_inc(ld_tern[i], 16)

                @block.tensor
                def _(pe):
                    pe.wait_ge(ld_sel, 16)
                    for i in range(B * NT):
                        mm = pe.matmul(bank[0][0:NB, :], block_sel[:, i, :], x1[:, i // NT, i % NT, :],
                                       start=(i == 0), stop=(i == B * NT - 1))
                    mm.then_inc(pe_step, 1)
                    pe.wait_ge(dve_step, 2)
                    for c in range(C):
                        mm = pe.transpose(bank[2][:, c * NB:c * NB + NB], blocks[:, c * P:c * P + P], ident[0:NB, 0:NB])
                    mm.then_inc(pe_step, 1)
                    pe.wait_ge(dve_step, 3)
                    pe.wait_ge(ld_c2, 16 * 8)
                    for c in range(C):
                        mm = pe.matmul(bank[1][0:NB, :], blocks_t[:, c, :], wk_t[:, c, :], start=(c == 0),
                                       stop=(c == C - 1))
                    mm.then_inc(pe_step, 1)
                    pe.wait_ge(dve_step, 7)
                    pe.transpose(bank[3][0:1, 0:NB], stat[:, 3:4], ident[0:NB, 0:NB]).then_inc(pe_step, 1)
                    pe.wait_ge(dve_step, 12)
                    pe.matmul(bank[4][0:NB, 0:1], row[0:1, 2, :], ones[0:1, 0:1], start=True, stop=True
                              ).then_inc(pe_step, 1)
                    pe.wait_ge(dve_step, 13)
                    for c in range(C):
                        mm = pe.matmul(bank[5][:, c * B:c * B + B], blocks[:, c * P:c * P + P], pick[:],
                                       start=True, stop=True)
                    mm.then_inc(pe_step, 1)
                    pe.wait_ge(dve_step, 14)
                    for c in range(C):
                        mm = pe.matmul(bank[6][0:B, :], mix_t[:, c * B:c * B + B], wo_t[:, c, :],
                                       start=(c == 0), stop=(c == C - 1))
                    mm.then_inc(pe_step, 1)
                    pe.wait_ge(dve_step, 15)
                    for b in range(B):
                        mm = pe.matmul(bank[b][:], batch_row[:, b * P:b * P + P], proj[:], start=True, stop=True)
                    mm.then_inc(pe_step, 1)

                @block.gpsimd
                def _(pool):
                    pool.wait_ge(dve_step, 6)
                    pool.tensor_tensor(stat[:, 2:3], stat[:, 2:3], minus_half[0:NB, :], ALU.pow).then_inc(pool_step, 1)

                @block.scalar
                def _(act):
                    act.wait_ge(dve_step, 4)
                    act.activation(junk[:], keys[:], ACT.Square, accum_out=stat[:, 0:1]).then_inc(act_step, 1)
                    act.wait_ge(dve_step, 9)
                    act.activation(row[0:1, 1, :], row[0:1, 0, :], ACT.Exp).then_inc(act_step, 1)

                @block.vector
                def _(dve):
                    steps = [0]

                    def step(ins):
                        steps[0] += 1
                        ins.then_inc(dve_step, 1)
                        dve.wait_ge(dve_step, steps[0])

                    dve.wait_ge(ld_c2, 16 * 8)
                    step(dve.tensor_tensor(query[:], query[:], key_w[:], ALU.mult))
                    dve.wait_ge(pe_step, 1)
                    step(dve.tensor_copy(blocks[:], bank[0][0:NB, :]))
                    dve.wait_ge(pe_step, 2)
                    step(dve.tensor_copy(blocks_t[:].rearrange("p c n -> p (c n)"), bank[2][:, 0:C * NB]))
                    dve.wait_ge(pe_step, 3)
                    step(dve.tensor_copy(keys[:], bank[1][0:NB, :]))
                    step(dve.scalar_tensor_tensor(query[:], keys[:], 1.0, query[:], ALU.mult, ALU.mult,
                                                  accum_out=stat[:, 1:2]))
                    dve.wait_ge(act_step, 1)
                    step(dve.tensor_scalar(stat[:, 2:3], stat[:, 0:1], 1.0 / D, RMS_EPS, ALU.mult, ALU.add))
                    dve.wait_ge(pool_step, 1)
                    step(dve.tensor_tensor(stat[:, 3:4], stat[:, 1:2], stat[:, 2:3], ALU.mult))
                    dve.wait_ge(pe_step, 4)
                    by_batch = bank[3][0:1, 0:NB].rearrange("o (b n) -> o b n", b=B)
                    out0, out1, out2 = (row[0:1, i, :].rearrange("o (b n) -> o b n", b=B) for i in range(3))
                    step(dve.tensor_reduce(rowb[0:1, 0, :], by_batch, AX_X, ALU.max))
                    step(dve.tensor_tensor(out0, by_batch, rowb[0:1, 0, :].unsqueeze(2).to_broadcast([1, B, NBLK]),
                                           ALU.subtract))
                    dve.wait_ge(act_step, 2)
                    step(dve.tensor_reduce(rowb[0:1, 1, :], out1, AX_X, ALU.add))
                    step(dve.reciprocal(rowb[0:1, 2, :], rowb[0:1, 1, :]))
                    step(dve.tensor_tensor(out2, out1, rowb[0:1, 2, :].unsqueeze(2).to_broadcast([1, B, NBLK]), ALU.mult))
                    dve.wait_ge(pe_step, 5)
                    step(dve.tensor_scalar(pick[:], batch_mask[:], bank[4][0:NB, 0:1], None, ALU.mult))
                    dve.wait_ge(pe_step, 6)
                    step(dve.tensor_copy(mix_t[:], bank[5][:, 0:C * B]))
                    dve.wait_ge(pe_step, 7)
                    step(dve.tensor_copy(proj[:], bank[6][0:B, :]))
                    dve.wait_ge(pe_step, 8)
                    for b in range(B):
                        dve.tensor_copy(shift[:, b, :], bank[b][:])

        with ExitStack() as st:
            up_w = tern[0][:].rearrange("p (c e) -> p c e", c=C)
            gate_w = tern[1][:].rearrange("p (c e) -> p c e", c=C)
            down_w = tern[2][:].rearrange("p (t d) -> p t d", t=FT)
            xn = sb(st, "xn", [P, NT, D])
            bn = sb(st, "bn", [P, NT, 6])
            bn_pad = sb(st, "bn_pad", [P, 1])
            mv = sb(st, "mv", [P, NT, 2])
            rstd = sb(st, "rstd", [P, NT])
            LN_STEPS = 4 * NT + 1
            LN_AT = [FT - 3 - 3 * (NT - q) for q in range(NT)]
            xg = sb(st, "xg", [P, 2, T])
            x_hi = sb(st, "x_hi", [P, C, T], F32R)
            x_lo = sb(st, "x_lo", [P, C, T], F32R)
            act_up = sb(st, "act_up", [P, 2, T])
            hid = sb(st, "hid", [P, 2, T])
            h_hi = sb(st, "h_hi", [P, 2, T], F32R)
            h_lo = sb(st, "h_lo", [P, 2, T], F32R)
            y_out = sb(st, "y_out", [P, NT, D])
            ln_step = sem("ln_step")
            rstd_done = sem("rstd_done")
            xn_t = sem("xn_t")
            xg_done = sem("xg_done")
            x_split = sem("x_split")
            up_mm = sem("up_mm")
            down_mm = sem("down_mm")
            silu_done = sem("silu_done")
            hid_done = sem("hid_done")
            hhi_done = sem("hhi_done")
            hlo_done = sem("hlo_done")
            y_scaled = sem("y_scaled")
            y_stored = sem("y_stored")
            out_rows = a["out"].rearrange("b (q p) d -> b p q d", p=P)
            with nc.Block() as block:
                @block.sync
                def _(sp):
                    sp.dma_start(y_out[:, 0, 0:1], a["zero_col"]).then_inc(y_stored, 16)
                    with sp.Fori(0, B) as g:
                        sp.wait_ge(y_scaled, g * NT + NT + 1)
                        sp.dma_start(out_rows[g], y_out[:]).then_inc(y_stored, 16)
                    sp.wait_ge(y_stored, 16 * B + 16)

                @block.tensor
                def _(pe):
                    def expand(g, e):
                        up, gate = bank[4 + 2 * (e % 2)], bank[5 + 2 * (e % 2)]
                        if e % 4 == 0:
                            pe.wait_ge(ld_tern[e // 4], 48)
                        for w, out in ((up_w, up), (gate_w, gate)):
                            for c in range(C):
                                if e == 0 and w is up_w:
                                    pe.wait_ge(x_split, g * 2 * C + 2 * c + 2)
                                for half, part in enumerate((x_hi, x_lo)):
                                    mm = pe.matmul(out[:], w[:, c, e * P:e * P + P], part[:, c, :],
                                                   start=(c == 0 and half == 0), stop=(c == C - 1 and half == 1))
                        mm.then_inc(up_mm, 1)

                    def contract(g, e):
                        pe.wait_ge(hhi_done, g * FT + e + 1)
                        pe.wait_ge(hlo_done, g * FT + e + 1)
                        for half, part in enumerate((h_hi, h_lo)):
                            for q in range(NT):
                                mm = pe.matmul(bank[q][:], part[:, e % 2, q * P:q * P + P], down_w[:, e, :],
                                               start=(e == 0 and half == 0), stop=(e == FT - 1 and half == 1))
                        mm.then_inc(down_mm, 1)

                    with pe.Fori(0, B) as g:
                        pe.wait_ge(ln_step, g * LN_STEPS + LN_STEPS)
                        pe.wait_ge(hid_done, g * FT + 1)
                        for c in range(C):
                            for q in range(NT):
                                tr = pe.transpose(bank[4 + c][:, q * P:q * P + P], xn[:, q, c * P:c * P + P], ident[:])
                            tr.then_inc(xn_t, 1)
                        for e in range(FT):
                            if e >= 2:
                                pe.wait_ge(hid_done, g * FT + e)
                            expand(g, e)
                            if e == 1:
                                pe.wait_ge(y_scaled, g * NT + 1)
                            if e > 0:
                                contract(g, e - 1)
                        contract(g, FT - 1)

                @block.scalar
                def _(act):
                    with act.Fori(0, B) as g:
                        for c in range(C):
                            act.wait_ge(xn_t, g * C + c + 1)
                            if c >= 2:
                                act.wait_ge(x_split, g * 2 * C + 2 * (c - 1))
                            act.activation(xg[:, c % 2, :], bank[4 + c][:], ACT.Identity, bias=beta_t[:, c:c + 1],
                                           scale=gamma_t[:, c:c + 1]).then_inc(xg_done, 1)
                        for e in range(FT):
                            act.wait_ge(up_mm, g * FT + e + 1)
                            if e >= 2:
                                act.wait_ge(hid_done, g * FT + e)
                            act.activation(act_up[:, e % 2, :], bank[4 + 2 * (e % 2)][:], ACT.Silu,
                                           scale=w_scale[:, 0:1]).then_inc(silu_done, 1)
                            act.wait_ge(hid_done, g * FT + e + 2)
                            if e >= 2:
                                act.wait_ge(down_mm, g * FT + e - 1)
                            act.activation(h_hi[:, e % 2, :], hid[:, e % 2, :], ACT.Copy).then_inc(hhi_done, 1)

                @block.vector
                def _(dve):
                    dve.memset(rstd[:], 0.0).then_inc(hid_done, 1)
                    dve.memset(mv[:], 0.0).then_inc(y_scaled, 1)
                    dve.wait_ge(hid_done, 1)
                    dve.wait_ge(y_scaled, 1)

                    def moments(g, b, q):
                        def chain(i, ins):
                            ins.then_inc(ln_step, 1)
                            dve.wait_ge(ln_step, g * LN_STEPS + q * 3 + i)
                        chain(1, dve.tensor_tensor(xn[:, q, :], x1[:, b, q, :], shift[:, b, :], ALU.add))
                        chain(2, dve.bn_stats(bn[:, q, :], xn[:, q, :]))
                        dve.memset(bn_pad[:], 0.0)
                        chain(3, dve.bn_aggr(mv[:, q, :], bn[:, q, :]))

                    def ask_rstd():
                        dve.tensor_scalar(rstd[:], mv[:, :, 1], RMS_EPS, None, ALU.add).then_inc(ln_step, 1)

                    def normalise(g):
                        dve.wait_ge(rstd_done, g + 1)
                        for q in range(NT):
                            dve.tensor_scalar(xn[:, q, :], xn[:, q, :], mv[:, q, 0:1], rstd[:, q:q + 1], ALU.subtract,
                                              ALU.mult).then_inc(ln_step, 1)

                    for q in range(NT):
                        dve.tensor_tensor(xn[:, q, :], x1[:, 0, q, :], shift[:, 0, :], ALU.add).then_inc(ln_step, 1)
                    for q in range(NT):
                        dve.wait_ge(ln_step, q + 1)
                        dve.bn_stats(bn[:, q, :], xn[:, q, :]).then_inc(ln_step, 1)
                    for q in range(NT):
                        dve.wait_ge(ln_step, NT + q + 1)
                        dve.bn_aggr(mv[:, q, :], bn[:, q, :]).then_inc(ln_step, 1)
                    dve.wait_ge(ln_step, 3 * NT)
                    ask_rstd()
                    normalise(0)
                    with dve.Fori(0, B) as g:
                        for c in range(C):
                            dve.wait_ge(xg_done, g * C + c + 1)
                            dve.tensor_copy(x_hi[:, c, :], xg[:, c % 2, :]).then_inc(x_split, 1)
                            dve.wait_ge(x_split, g * 2 * C + 2 * c + 1)
                            dve.tensor_tensor(x_lo[:, c, :], xg[:, c % 2, :], x_hi[:, c, :].bitcast(F32), ALU.subtract
                                              ).then_inc(x_split, 1)
                        for e in range(FT):
                            dve.wait_ge(silu_done, g * FT + e + 1)
                            if e >= 2:
                                dve.wait_ge(hhi_done, g * FT + e - 1)
                            dve.scalar_tensor_tensor(hid[:, e % 2, :], bank[5 + 2 * (e % 2)][:], w_scale[:, 1:2],
                                                     act_up[:, e % 2, :], ALU.mult, ALU.mult).then_inc(hid_done, 1)
                            dve.wait_ge(hhi_done, g * FT + e + 1)
                            dve.tensor_tensor(h_lo[:, e % 2, :], hid[:, e % 2, :], h_hi[:, e % 2, :].bitcast(F32),
                                              ALU.subtract).then_inc(hlo_done, 1)
                            if e in LN_AT:
                                moments(g + 1, (g + 1) % B, LN_AT.index(e))
                            if e == LN_AT[-1] + 1:
                                ask_rstd()
                            if e == LN_AT[-1] + 2:
                                normalise(g + 1)
                        dve.wait_ge(down_mm, g * FT + FT)
                        dve.wait_ge(y_stored, g * 16 + 16)
                        for q in range(NT):
                            dve.scalar_tensor_tensor(y_out[:, q, :], bank[q][:], w_scale[:, 2:3], x1[:, g, q, :],
                                                     ALU.mult, ALU.add).then_inc(y_scaled, 1)

                @block.gpsimd
                def _(pool):
                    with pool.Fori(0, B + 1) as g:
                        pool.wait_ge(ln_step, g * LN_STEPS + 3 * NT + 1)
                        pool.tensor_tensor(rstd[:], rstd[:], minus_half[:, 0:1].to_broadcast([P, NT]), ALU.pow
                                           ).then_inc(rstd_done, 1)


def _tables():
    eye = np.eye(P, dtype=np.float32)
    half = np.arange(P) % DR
    to = np.concatenate([np.arange(DR), (np.arange(DR) + DR // 2) % DR])
    inv_freq = 1.0 / 10000.0 ** (np.arange(0, DR, 2, dtype=np.float32) / DR)
    freqs = np.outer(np.arange(T, dtype=np.float32), inv_freq)
    cos, sin = np.cos(freqs).T, np.sin(freqs).T
    q, k = np.meshgrid(np.arange(P), np.arange(P), indexing="ij")
    return {
        "ident": eye,
        "dup": (half[:, None] == to[None, :]).astype(np.float32),
        "rope": np.concatenate([cos, cos, -sin, sin]).astype(np.float32),
        "rope_q": np.stack([np.concatenate([cos] * 4), np.concatenate([sin, -sin] * 2)], axis=1).astype(np.float32),
        "causal": np.where(k > q, np.float32(-1e30), np.float32(0)),
        "block_sel": np.kron(np.eye(B * NBLK), np.ones((BLK, 1))).reshape(B * NT, P, B * NBLK).transpose(1, 0, 2)
                       .astype(np.float32),
        "batch_mask": np.kron(np.eye(B), np.ones((NBLK, 1))).astype(np.float32),
        "batch_row": np.kron(np.eye(B), np.ones((1, P))).astype(np.float32),
        "zero_col": np.zeros((P, 1), np.float32),
    }


def kernel(x, cond_2048, L0_cond_W_ih, L0_cond_W_hh, L0_cond_b_ih, L0_cond_b_hh, L0_attn_w_q_a, L0_attn_q_a_ln,
           L0_attn_w_q_b, L0_attn_w_kv_a, L0_attn_kv_a_ln, L0_attn_w_kv_b, L0_attn_w_out, L0_cond2_rms_weight,
           L0_cond2_Wk, L0_cond2_Wo, L0_cond2_ln_gamma, L0_cond2_ln_beta, L0_ffn_W_up, L0_ffn_W_gate, L0_ffn_W_down):
    import ml_dtypes
    from concourse import bacc
    from concourse.bass_utils import run_bass_kernel_spmd

    def np32(v):
        return np.ascontiguousarray(np.asarray(v))

    def tiles(w):
        return w.reshape(-1, P, w.shape[-1]).transpose(1, 0, 2)

    def state_tiles(w):
        return w.reshape(4, C, 32, w.shape[-1]).transpose(0, 2, 1, 3).reshape(P, C, w.shape[-1])

    def gate_cols(w):
        return w.reshape(-1, G3, 4, P).transpose(0, 2, 1, 3).reshape(-1, 4 * G3 * P)

    x, cond = np32(x), np32(cond_2048)
    w_hh, b_hh = np32(L0_cond_W_hh), np32(L0_cond_b_hh)
    t = _tables()
    arrays = dict(t)
    arrays["causal"] = t["causal"].astype(ml_dtypes.bfloat16)
    arrays["ident_bf"] = t["ident"].astype(ml_dtypes.bfloat16)
    arrays["x_t"] = x.reshape(B, TILES, TS, C, P).transpose(1, 4, 3, 0, 2).reshape(TILES, P, C, P)
    arrays["x_rows"] = x.reshape(B, NT, P, D).transpose(0, 2, 1, 3)
    arrays["w_ih"] = tiles(gate_cols(np32(L0_cond_W_ih)))
    arrays["b_ih"] = gate_cols(np32(L0_cond_b_ih)[None])
    arrays["b_hh"] = gate_cols(b_hh[None])
    w_rnz = w_hh.reshape(D, G3, 4, P)[:, [0, 2, 1]].transpose(0, 2, 1, 3).reshape(D, -1)
    arrays["w_hh"] = state_tiles(w_rnz).reshape(P, C, 4, G3 * P)
    state = np.zeros((4, 32, P), np.float32)
    state[:, :B] = cond.reshape(B, 4, P).transpose(1, 0, 2)
    arrays["h0"] = state.reshape(P, P)
    bias = np.zeros((4, 32, P), np.float32)
    bias[:, :B] = b_hh[2 * D:].reshape(4, 1, P)
    arrays["b_hn"] = bias.reshape(P, P)
    w_qb = np32(L0_attn_w_q_b).reshape(QL, NH, DN + DR)
    w_kvb = np32(L0_attn_w_kv_b).reshape(KL, NH, DN + DV)
    w_o = np32(L0_attn_w_out).reshape(NH, DV, D)
    arrays["fold"] = np.concatenate([w_qb[:, :, :DN].transpose(1, 2, 0), w_kvb[:, :, :DN].transpose(1, 2, 0),
                                     w_kvb[:, :, DN:].transpose(1, 2, 0), w_o], axis=2)

    def rotary(w):
        return np.concatenate([w[..., 0::2], w[..., 1::2], w[..., 1::2], w[..., 0::2]], axis=-1)

    w_rot = np.concatenate([w_qb[:, :, DN::2], w_qb[:, :, DN + 1::2]], axis=-1)
    arrays["w_rope"] = w_rot.reshape(QC, P, NH // 2, P).transpose(2, 1, 0, 3).reshape(NH // 2, P, QC * P)
    w_kva = np32(L0_attn_w_kv_a)
    arrays["w_qa"] = state_tiles(np32(L0_attn_w_q_a))
    arrays["w_kva"] = state_tiles(np.concatenate([w_kva[:, :KL], rotary(w_kva[:, KL:])], axis=1))
    arrays["ln_q"] = np32(L0_attn_q_a_ln).reshape(QC, P).T
    arrays["ln_kv"] = np32(L0_attn_kv_a_ln).reshape(P, 1)
    arrays["wk_t"] = tiles(np32(L0_cond2_Wk).T)
    arrays["wo_t"] = tiles(np32(L0_cond2_Wo).T)
    arrays["key_w"] = np32(L0_cond2_rms_weight)[None]
    arrays["query"] = cond[1:2]
    arrays["gamma_t"] = np32(L0_cond2_ln_gamma).reshape(C, P).T
    arrays["beta_t"] = np32(L0_cond2_ln_beta).reshape(C, P).T
    arrays["ffn"] = np.stack([tiles(np32(w).T).reshape(P, -1) for w in (L0_ffn_W_up, L0_ffn_W_gate, L0_ffn_W_down)])

    nc = bacc.Bacc("TRN2", target_bir_lowering=False, num_devices=1)
    arrays = {k: np.ascontiguousarray(v) for k, v in arrays.items()}
    aps = {k: nc.dram_tensor(f"in_{k}", v.shape, mybir.dt.from_np(v.dtype), kind="ExternalInput").ap()
           for k, v in arrays.items()}
    aps["out"] = nc.dram_tensor("out_0", [B, T, D], F32, kind="ExternalOutput").ap()
    build(nc, aps)
    result = run_bass_kernel_spmd(nc, [{f"in_{k}": v for k, v in arrays.items()}], core_ids=[0])
    return result.results[0]["out_0"]
```
